# Optimizing a Trainium2 kernel written in Bass

```python
import numpy as np
import jax
import jax.numpy as jnp

def _softmax(x, axis=-1):
    return jax.nn.softmax(x, axis=axis)

def _gelu(x):
    return jax.nn.gelu(x, approximate=True)

def _silu(x):
    return jax.nn.silu(x)

def _sigmoid(x):
    return jax.nn.sigmoid(x)

def _layernorm(x, axis=-1, eps=1e-05):
    m = jnp.mean(x, axis=axis, keepdims=True)
    v = jnp.var(x, axis=axis, keepdims=True)
    return (x - m) / jnp.sqrt(v + eps)

def _scatter_add(tgt, idx, src, axis=0):
    return tgt.at[idx].add(src)

def _segment_sum(src, seg, n):
    return jax.ops.segment_sum(src, seg, n)
kernel_name = 'mk_prb_d2_jaxref_r8_f87a5e'

def setup_inputs(seed: int=0):
    np.random.seed(seed)
    _w = jnp.asarray

    def _L0_attn_setup():
        import jax, jax.numpy as jnp
        import numpy as np
        B, T, D, S = (4, 256, 128, 64)
        EPS = 1e-08
        key = jax.random.key(seed)
        ks = jax.random.split(key, 6)
        return {'token_embeddings': jax.random.normal(ks[0], (B, T, D), dtype=jnp.float32), 'splat_positions': jax.random.normal(ks[1], (S, D), dtype=jnp.float32), 'splat_log_scales': jax.random.uniform(ks[2], (S,), dtype=jnp.float32), 'splat_amplitudes': jax.random.uniform(ks[3], (S,), dtype=jnp.float32), 'Wv': jax.random.normal(ks[4], (D, D), dtype=jnp.float32) / np.sqrt(D).astype(np.float32), 'Wo': jax.random.normal(ks[5], (D, D), dtype=jnp.float32) / np.sqrt(D).astype(np.float32)}
    _L0_attn_in = _L0_attn_setup()

    def _L0_ffn_setup():
        import jax, jax.numpy as jnp
        import numpy as np
        B, N, D, H, E = (4, 128, 128, 16, 8)
        DK = D // H
        HID = 4 * D
        EPS = 1e-05

        def _layernorm(x, w, b):
            m = jnp.mean(x, axis=-1, keepdims=True)
            v = jnp.mean(jnp.square(x - m), axis=-1, keepdims=True)
            return (x - m) * jax.lax.rsqrt(v + EPS) * w + b

        def _msa(x, w_qkv, w_proj):
            b, n, d = x.shape
            qkv = (x @ w_qkv).reshape(b, n, 3, H, DK)
            q = qkv[:, :, 0].transpose(0, 2, 1, 3)
            k = qkv[:, :, 1].transpose(0, 2, 1, 3)
            v = qkv[:, :, 2].transpose(0, 2, 1, 3)
            attn = jnp.einsum('bhnd,bhmd->bhnm', q, k) * (1.0 / np.sqrt(DK))
            attn = jax.nn.softmax(attn, axis=-1)
            y = jnp.einsum('bhnm,bhmd->bhnd', attn, v)
            y = y.transpose(0, 2, 1, 3).reshape(b, n, d)
            return y @ w_proj

        def _moe_mlp(x, gate_w, gate_b, w1, w2):
            b, n, d = x.shape
            xf = x.reshape(b * n, d)
            logits = xf @ gate_w + gate_b
            one_hot = jax.nn.one_hot(jnp.argmax(logits, axis=-1), E, dtype=xf.dtype)
            h = jax.nn.gelu(jnp.einsum('td,edh->teh', xf, w1), approximate=True)
            y = jnp.einsum('teh,ehd->ted', h, w2)
            out = jnp.einsum('te,ted->td', one_hot, y)
            return out.reshape(b, n, d)
        key = jax.random.key(seed)
        ks = jax.random.split(key, 8)
        s = 0.02
        return {'x': jax.random.normal(ks[0], (B, N, D), jnp.float32), 'ln1_w': jnp.ones((D,), jnp.float32), 'ln1_b': jnp.zeros((D,), jnp.float32), 'w_qkv': jax.random.normal(ks[1], (D, 3 * D), jnp.float32) * s, 'w_proj': jax.random.normal(ks[2], (D, D), jnp.float32) * s, 'ln2_w': jnp.ones((D,), jnp.float32), 'ln2_b': jnp.zeros((D,), jnp.float32), 'gate_w': jax.random.normal(ks[3], (D, E), jnp.float32) * s, 'gate_b': jnp.zeros((E,), jnp.float32), 'w1': jax.random.normal(ks[4], (E, D, HID), jnp.float32) * s, 'w2': jax.random.normal(ks[5], (E, HID, D), jnp.float32) * s}
    _L0_ffn_in = _L0_ffn_setup()

    def _L1_attn_setup():
        import jax, jax.numpy as jnp
        import numpy as np
        B, S, IN_DIM = (2, 256, 128)
        OUT_DIM, H = (128, 16)
        D = OUT_DIM // H
        W1, W2 = (16, 16)
        LN_EPS = 1e-05

        def _causal_windows(t, w):
            b, s, h, d = t.shape
            padded = jnp.concatenate([jnp.zeros((b, w - 1, h, d), t.dtype), t], axis=1)
            return jnp.stack([padded[:, j:j + s] for j in range(w)], axis=2)

        def _forward(x, Wq, Wk, Wv, Wkp, Wo, gamma, beta):
            b, s, _ = x.shape
            proj = lambda W: (x @ W.T).reshape(b, s, H, D)
            Q, K, V, Kp = (proj(Wq), proj(Wk), proj(Wv), proj(Wkp))
            K_win = _causal_windows(K, W1)
            Kp_win = _causal_windows(Kp, W2)
            V_win = _causal_windows(V, W1)
            Vp_win = _causal_windows(V, W2)
            A = jnp.einsum('bshd,bsjhd,bskhd->bshjk', Q, K_win, Kp_win) / jnp.sqrt(jnp.float32(D))
            s_idx = jnp.arange(s)[:, None]
            m1 = jnp.arange(W1)[None, :] >= W1 - 1 - s_idx
            m2 = jnp.arange(W2)[None, :] >= W2 - 1 - s_idx
            mask = m1[:, :, None] & m2[:, None, :]
            A = jnp.where(mask[None, :, None], A, -jnp.inf)
            P = jax.nn.softmax(A.reshape(b, s, H, W1 * W2), axis=-1).reshape(b, s, H, W1, W2)
            Z = jnp.einsum('bshjk,bsjhd,bskhd->bshd', P, V_win, Vp_win)
            out = Z.reshape(b, s, OUT_DIM) @ Wo.T + x
            mu = jnp.mean(out, axis=-1, keepdims=True)
            var = jnp.mean(jnp.square(out - mu), axis=-1, keepdims=True)
            return (out - mu) / jnp.sqrt(var + LN_EPS) * gamma + beta
        key = jax.random.key(seed)
        ks = jax.random.split(key, 8)
        sc_in = 1.0 / np.sqrt(IN_DIM)
        sc_out = 1.0 / np.sqrt(OUT_DIM)
        return {'x': jax.random.normal(ks[0], (B, S, IN_DIM), dtype=jnp.float32), 'Wq': jax.random.normal(ks[1], (OUT_DIM, IN_DIM), dtype=jnp.float32) * sc_in, 'Wk': jax.random.normal(ks[2], (OUT_DIM, IN_DIM), dtype=jnp.float32) * sc_in, 'Wv': jax.random.normal(ks[3], (OUT_DIM, IN_DIM), dtype=jnp.float32) * sc_in, 'Wkp': jax.random.normal(ks[4], (OUT_DIM, IN_DIM), dtype=jnp.float32) * sc_in, 'Wo': jax.random.normal(ks[5], (OUT_DIM, OUT_DIM), dtype=jnp.float32) * sc_out, 'gamma': jnp.ones((OUT_DIM,), dtype=jnp.float32), 'beta': jnp.zeros((OUT_DIM,), dtype=jnp.float32)}
    _L1_attn_in = _L1_attn_setup()

    def _L1_ffn_setup():
        import jax, jax.numpy as jnp
        import numpy as np
        E, D, F, GATE_DIM = (8, 128, 512, 16)
        B, T = (2, 256)
        key = jax.random.key(seed)
        ks = jax.random.split(key, 7)
        s = 0.02
        return {'hidden_states': jax.random.normal(ks[0], (B, T, D), dtype=jnp.float32), 'w_red': jax.random.normal(ks[1], (D, GATE_DIM), dtype=jnp.float32) * s, 'wg': jax.random.normal(ks[2], (E, GATE_DIM), dtype=jnp.float32), 'w1': jax.random.normal(ks[3], (E, D, F), dtype=jnp.float32) * s, 'b1': jax.random.normal(ks[4], (E, F), dtype=jnp.float32) * s, 'w2': jax.random.normal(ks[5], (E, F, D), dtype=jnp.float32) * s, 'b2': jax.random.normal(ks[6], (E, D), dtype=jnp.float32) * s}
    _L1_ffn_in = _L1_ffn_setup()
    _d = {'L0_attn_token_embeddings': _L0_attn_in['token_embeddings'], 'L0_attn_splat_positions': _L0_attn_in['splat_positions'], 'L0_attn_splat_log_scales': _L0_attn_in['splat_log_scales'], 'L0_attn_splat_amplitudes': _L0_attn_in['splat_amplitudes'], 'L0_attn_Wv': _L0_attn_in['Wv'], 'L0_attn_Wo': _L0_attn_in['Wo'], 'L0_ffn_ln1_w': _L0_ffn_in['ln1_w'], 'L0_ffn_ln1_b': _L0_ffn_in['ln1_b'], 'L0_ffn_w_qkv': _L0_ffn_in['w_qkv'], 'L0_ffn_w_proj': _L0_ffn_in['w_proj'], 'L0_ffn_ln2_w': _L0_ffn_in['ln2_w'], 'L0_ffn_ln2_b': _L0_ffn_in['ln2_b'], 'L0_ffn_gate_w': _L0_ffn_in['gate_w'], 'L0_ffn_gate_b': _L0_ffn_in['gate_b'], 'L0_ffn_w1': _L0_ffn_in['w1'], 'L0_ffn_w2': _L0_ffn_in['w2'], 'L1_attn_Wq': _L1_attn_in['Wq'], 'L1_attn_Wk': _L1_attn_in['Wk'], 'L1_attn_Wv': _L1_attn_in['Wv'], 'L1_attn_Wkp': _L1_attn_in['Wkp'], 'L1_attn_Wo': _L1_attn_in['Wo'], 'L1_attn_gamma': _L1_attn_in['gamma'], 'L1_attn_beta': _L1_attn_in['beta'], 'L1_ffn_w_red': _L1_ffn_in['w_red'], 'L1_ffn_wg': _L1_ffn_in['wg'], 'L1_ffn_w1': _L1_ffn_in['w1'], 'L1_ffn_b1': _L1_ffn_in['b1'], 'L1_ffn_w2': _L1_ffn_in['w2'], 'L1_ffn_b2': _L1_ffn_in['b2']}
    _x0 = _d['L0_attn_token_embeddings']
    _d['L0_attn_token_embeddings'] = jax.random.normal(jax.random.fold_in(jax.random.key(seed), 1), (2, 1024, 128), dtype=_x0.dtype)
    del _x0
    return _d

def reference(L0_attn_token_embeddings, L0_attn_splat_positions, L0_attn_splat_log_scales, L0_attn_splat_amplitudes, L0_attn_Wv, L0_attn_Wo, L0_ffn_ln1_w, L0_ffn_ln1_b, L0_ffn_w_qkv, L0_ffn_w_proj, L0_ffn_ln2_w, L0_ffn_ln2_b, L0_ffn_gate_w, L0_ffn_gate_b, L0_ffn_w1, L0_ffn_w2, L1_attn_Wq, L1_attn_Wk, L1_attn_Wv, L1_attn_Wkp, L1_attn_Wo, L1_attn_gamma, L1_attn_beta, L1_ffn_w_red, L1_ffn_wg, L1_ffn_w1, L1_ffn_b1, L1_ffn_w2, L1_ffn_b2):

    def _L0_attn_ref(token_embeddings, splat_positions, splat_log_scales, splat_amplitudes, Wv, Wo):
        import jax, jax.numpy as jnp
        import numpy as np
        B, T, D, S = (4, 256, 128, 64)
        EPS = 1e-08
        x = token_embeddings
        p = splat_positions
        x2 = jnp.sum(x * x, axis=-1, keepdims=True)
        p2 = jnp.sum(p * p, axis=-1)
        xp = jnp.einsum('btd,sd->bts', x, p)
        d2 = jnp.maximum(x2 + p2[None, None, :] - 2.0 * xp, 0.0)
        scales = jnp.exp(splat_log_scales)
        gauss = splat_amplitudes * jnp.exp(-0.5 * d2 / (scales * scales))
        attn = jnp.einsum('bis,bjs->bij', gauss, gauss)
        attn = attn / (jnp.sum(attn, axis=-1, keepdims=True) + EPS)
        v = jnp.einsum('btd,de->bte', x, Wv)
        out = jnp.einsum('bij,bjd->bid', attn, v)
        return jnp.einsum('btd,de->bte', out, Wo)

    def _L0_ffn_ref(x, ln1_w, ln1_b, w_qkv, w_proj, ln2_w, ln2_b, gate_w, gate_b, w1, w2):
        import jax, jax.numpy as jnp
        import numpy as np
        B, N, D, H, E = (4, 128, 128, 16, 8)
        DK = D // H
        HID = 4 * D
        EPS = 1e-05

        def _layernorm(x, w, b):
            m = jnp.mean(x, axis=-1, keepdims=True)
            v = jnp.mean(jnp.square(x - m), axis=-1, keepdims=True)
            return (x - m) * jax.lax.rsqrt(v + EPS) * w + b

        def _msa(x, w_qkv, w_proj):
            b, n, d = x.shape
            qkv = (x @ w_qkv).reshape(b, n, 3, H, DK)
            q = qkv[:, :, 0].transpose(0, 2, 1, 3)
            k = qkv[:, :, 1].transpose(0, 2, 1, 3)
            v = qkv[:, :, 2].transpose(0, 2, 1, 3)
            attn = jnp.einsum('bhnd,bhmd->bhnm', q, k) * (1.0 / np.sqrt(DK))
            attn = jax.nn.softmax(attn, axis=-1)
            y = jnp.einsum('bhnm,bhmd->bhnd', attn, v)
            y = y.transpose(0, 2, 1, 3).reshape(b, n, d)
            return y @ w_proj

        def _moe_mlp(x, gate_w, gate_b, w1, w2):
            b, n, d = x.shape
            xf = x.reshape(b * n, d)
            logits = xf @ gate_w + gate_b
            one_hot = jax.nn.one_hot(jnp.argmax(logits, axis=-1), E, dtype=xf.dtype)
            h = jax.nn.gelu(jnp.einsum('td,edh->teh', xf, w1), approximate=True)
            y = jnp.einsum('teh,ehd->ted', h, w2)
            out = jnp.einsum('te,ted->td', one_hot, y)
            return out.reshape(b, n, d)
        x = x + _msa(_layernorm(x, ln1_w, ln1_b), w_qkv, w_proj)
        x = x + _moe_mlp(_layernorm(x, ln2_w, ln2_b), gate_w, gate_b, w1, w2)
        return x

    def _L1_attn_ref(x, Wq, Wk, Wv, Wkp, Wo, gamma, beta):
        import jax, jax.numpy as jnp
        import numpy as np
        B, S, IN_DIM = (2, 256, 128)
        OUT_DIM, H = (128, 16)
        D = OUT_DIM // H
        W1, W2 = (16, 16)
        LN_EPS = 1e-05

        def _causal_windows(t, w):
            b, s, h, d = t.shape
            padded = jnp.concatenate([jnp.zeros((b, w - 1, h, d), t.dtype), t], axis=1)
            return jnp.stack([padded[:, j:j + s] for j in range(w)], axis=2)

        def _forward(x, Wq, Wk, Wv, Wkp, Wo, gamma, beta):
            b, s, _ = x.shape
            proj = lambda W: (x @ W.T).reshape(b, s, H, D)
            Q, K, V, Kp = (proj(Wq), proj(Wk), proj(Wv), proj(Wkp))
            K_win = _causal_windows(K, W1)
            Kp_win = _causal_windows(Kp, W2)
            V_win = _causal_windows(V, W1)
            Vp_win = _causal_windows(V, W2)
            A = jnp.einsum('bshd,bsjhd,bskhd->bshjk', Q, K_win, Kp_win) / jnp.sqrt(jnp.float32(D))
            s_idx = jnp.arange(s)[:, None]
            m1 = jnp.arange(W1)[None, :] >= W1 - 1 - s_idx
            m2 = jnp.arange(W2)[None, :] >= W2 - 1 - s_idx
            mask = m1[:, :, None] & m2[:, None, :]
            A = jnp.where(mask[None, :, None], A, -jnp.inf)
            P = jax.nn.softmax(A.reshape(b, s, H, W1 * W2), axis=-1).reshape(b, s, H, W1, W2)
            Z = jnp.einsum('bshjk,bsjhd,bskhd->bshd', P, V_win, Vp_win)
            out = Z.reshape(b, s, OUT_DIM) @ Wo.T + x
            mu = jnp.mean(out, axis=-1, keepdims=True)
            var = jnp.mean(jnp.square(out - mu), axis=-1, keepdims=True)
            return (out - mu) / jnp.sqrt(var + LN_EPS) * gamma + beta
        return _forward(x, Wq, Wk, Wv, Wkp, Wo, gamma, beta)

    def _L1_ffn_ref(hidden_states, w_red, wg, w1, b1, w2, b2):
        import jax, jax.numpy as jnp
        import numpy as np
        E, D, F, GATE_DIM = (8, 128, 512, 16)
        B, T = (2, 256)
        b, t, c = hidden_states.shape
        x = hidden_states.reshape(-1, c)
        red = x @ w_red
        wg_n = wg / jnp.maximum(jnp.linalg.norm(wg, axis=1, keepdims=True), 0.0001)
        logits = red @ wg_n.T
        gates = jax.nn.softmax(logits, axis=1)
        idx = jnp.argmax(gates, axis=1)
        scores = jnp.take_along_axis(gates, idx[:, None], axis=1)
        h = jax.nn.gelu(jnp.einsum('td,edf->etf', x, w1) + b1[:, None, :], approximate=False)
        y = jnp.einsum('etf,efd->etd', h, w2) + b2[:, None, :]
        out = jnp.take_along_axis(y, idx[None, :, None], axis=0)[0]
        out = out * scores
        return out.reshape(b, t, c)
    x = L0_attn_token_embeddings
    xn = _layernorm(x, axis=-1)
    x = x + _L0_attn_ref(xn, L0_attn_splat_positions, L0_attn_splat_log_scales, L0_attn_splat_amplitudes, L0_attn_Wv, L0_attn_Wo) + _L0_ffn_ref(xn, L0_ffn_ln1_w, L0_ffn_ln1_b, L0_ffn_w_qkv, L0_ffn_w_proj, L0_ffn_ln2_w, L0_ffn_ln2_b, L0_ffn_gate_w, L0_ffn_gate_b, L0_ffn_w1, L0_ffn_w2)
    xn = _layernorm(x, axis=-1)
    x = x + _L1_attn_ref(xn, L1_attn_Wq, L1_attn_Wk, L1_attn_Wv, L1_attn_Wkp, L1_attn_Wo, L1_attn_gamma, L1_attn_beta) + _L1_ffn_ref(xn, L1_ffn_w_red, L1_ffn_wg, L1_ffn_w1, L1_ffn_b1, L1_ffn_w2, L1_ffn_b2)
    return x

_drawn_inputs = setup_inputs


def setup_inputs(seed=0):
    import zlib

    import numpy as np

    out = dict(_drawn_inputs(seed))
    spreads = {'L0_ffn_ln1_w': (1.0, 0.6),
     'L0_ffn_ln1_b': (0.0, 0.8),
     'L0_ffn_ln2_w': (1.0, 0.6),
     'L0_ffn_ln2_b': (0.0, 0.8),
     'L0_ffn_gate_b': (0.0, 0.342),
     'L1_attn_gamma': (1.0, 0.2),
     'L1_attn_beta': (0.0, 0.519)}
    factors = {'L0_ffn_w_qkv': 8.0,
     'L0_ffn_w_proj': 8.0,
     'L1_ffn_w_red': 8.0,
     'L1_ffn_wg': 8.0,
     'L1_ffn_w1': 8.0,
     'L1_ffn_b1': 8.0,
     'L1_ffn_w2': 8.0,
     'L1_ffn_b2': 33.954}
    for name, (base, spread) in spreads.items():
        noise = np.random.default_rng([zlib.crc32(name.encode()), seed]).standard_normal(out[name].shape)
        drawn = base * np.exp(spread * noise) if base else spread * noise
        out[name] = jnp.asarray(drawn.astype(out[name].dtype))
    for name, factor in factors.items():
        out[name] = (out[name] * factor).astype(out[name].dtype)
    return out
```

```python
from contextlib import ExitStack

import concourse.bass as bass
from concourse import mybir

F32 = mybir.dt.float32
BF16 = mybir.dt.bfloat16
ALU = mybir.AluOpType
ACT = mybir.ActivationFunctionType
X = mybir.AxisListType.X

P = 128
D = 128
B, T = 2, 1024
N = B * T
NT = N // P
CH = 512
NCH = N // CH
H, DK = 16, 8
S = 64
E = 8
HID = 512
FT = HID // P
LN_EPS = 1e-5
SPLAT_EPS = 1e-8
SCALE = float(DK) ** -0.5

HG = 4
NG = H // HG
GROUPS = B * NG
SPLITS = 3
KQ = SPLITS * SPLITS * DK
KX = KQ + SPLITS
RING = 3
MT = T // P
QH = T // CH
STEPS = QH * MT
UNITS = HG * MT

W = 16
TB = 16
WIN = W + TB
NB = T // TB
PADT = T + W
SC, MX, MXN, YB = 0, 4, 3, 7
AHEAD = 3
BIG = -1.0e30
PEEL, BODY, VRING = 2, 6, 6
WRING = 3
BLOCKS = B * NB


def chain(ins, steps):
    ins.then_inc(steps.sem, 1)
    steps.n += 1
    steps.eng.wait_ge(steps.sem, steps.base() + steps.n)


class Steps:

    def __init__(self, eng, sem):
        self.eng, self.sem, self.n, self.loop, self.per = eng, sem, 0, None, 0

    def base(self):
        return 0 if self.loop is None else self.loop * self.per

    def enter(self, i, per):
        self.loop, self.per, self.start = i, per, self.n

    def leave(self, times):
        assert self.n - self.start == self.per, (self.n - self.start, self.per)
        self.n += (times - 1) * self.per
        self.loop = None


def two_layers(nc, a, out):
    with ExitStack() as ctx:
        build(nc, ctx, a, out)


def build(nc, ctx, a, out):
    def sb(name, shape, dt=F32):
        return ctx.enter_context(nc.sbuf_tensor(name, shape, dt))

    def dram(name, shape, dt=F32):
        return nc.dram_tensor(name, shape, dt, kind="Internal").ap()

    sems = {}

    def sem(name):
        if name not in sems:
            sems[name] = ctx.enter_context(nc.semaphore(name))
        return sems[name]

    ps = ctx.enter_context(nc.psum_tensor("ps", [P, 8, CH], F32))

    x_tok = sb("x_tok", [P, NT, D])
    xn_tok = sb("xn_tok", [P, NT, D])
    moe_tok = sb("moe_tok", [P, NT, D])
    tmp_tok = sb("tmp_tok", [P, NT, D])
    xnT = sb("xnT", [P, N])
    hT = sb("hT", [P, N])

    ident = sb("ident", [P, P])
    ident_bf = sb("ident_bf", [P, P], BF16)
    ones = sb("ones", [P, 128])
    eps = sb("eps", [P, 1])
    rows = {}
    for name in ("L1_attn_gamma", "L1_attn_beta"):
        rows[name] = sb("row_" + name, [P, D])
    lncol = {}
    for name in ("L0_ffn_ln1_w", "L0_ffn_ln1_b", "L0_ffn_ln2_w", "L0_ffn_ln2_b"):
        lncol[name] = sb("col_" + name, [P, 1])
    gate_b = sb("gate_b_row", [P, E])
    col = sb("columns", [P, 8, NT])
    stats = sb("stats", [P, NT, 6])

    sqd = {"L0_attn_Wv": None, "L0_attn_Wo": None}
    for name in sqd:
        sqd[name] = sb("w_" + name, [D, D])
    wqkv = sb("wqkv", [D, 3 * D])
    gate_w = sb("gate_w_sb", [D, E])
    wproj = sb("wproj", [D, D])
    splatT = sb("splatT", [D, S])
    splat = sb("splat", [S, D])
    splat_ls = sb("splat_ls", [S, 1])
    splat_amp = sb("splat_amp", [S, 1])
    scol = sb("splat_columns", [S, 6])

    arena = sb("arena", [P, 27648])

    def carve(at, shape, dt=F32):
        n = 1
        for s in shape[1:]:
            n *= s
        words = n * (4 if dt == F32 else 2) // 4
        v = arena[0:shape[0], at:at + words]
        if dt != F32:
            v = v.bitcast(dt)
        if len(shape) > 2:
            names = "abcd"[:len(shape) - 1]
            v = v.rearrange("p (" + " ".join(names) + ") -> p " + " ".join(names),
                            **dict(zip(names[1:], shape[2:])))
        return v, at + words

    xsqT, at = carve(0, [P, N])
    gaussT, at = carve(at, [S, N])
    gauss, at = carve(at, [P, NT, S])
    xg, at = carve(at, [P, B, S])
    gvT, at = carve(at, [P, B, S])
    gvw, at = carve(at, [S, B, D + 1])
    Qs, at = carve(0, [P, RING, HG * T], BF16)
    Ks, at = carve(at, [P, RING, HG * T], BF16)
    probs, at = carve(at, [P, 2, HG, CH])
    Vg, at = carve(at, [P, RING, MT, HG, 32])
    split_hi, _ = carve(at, [P, SPLITS, N], BF16)
    split_r, _ = carve(at + SPLITS * N // 2, [P, 2, 2, CH])
    Yraw, at = carve(at, [P, NG, N])
    Vtok = tmp_tok
    mxh = sb("mx_halves", [P, UNITS, 2])
    nmx = sb("neg_max", [P, UNITS])
    mxr = sb("max_rest", [P, UNITS])
    mxs = sb("max_parts", [P, SPLITS, UNITS], BF16)
    mxrow = sb("max_rows", [SPLITS * UNITS, P], BF16)
    w1r, at = carve(0, [P, 2, HID])
    w2r, at = carve(at, [P, 2, FT, D])
    hid, at = carve(at, [P, 2, FT, CH])
    rden = sb("rden", [P, 2, H, 1])
    route = sb("route", [P, 6, NT, E])
    oh = sb("onehot", [P, NT, E])
    qT, at = carve(8192, [P, N])
    kT, at = carve(at, [P, B, PADT])
    kpT, at = carve(at, [P, B, PADT])
    vT, at = carve(at, [P, B, PADT])
    zT, at = carve(at, [P, N])
    denT, at = carve(at, [P, N])
    qk, at = carve(at, [P, WRING, TB, W])
    kdiag, at = carve(at, [P, WRING, H, WIN])
    vwin, at = carve(at, [P, VRING, D])
    vdiag, at = carve(at, [P, WRING, NG, HG, DK])
    rv, at = carve(at, [P, 2, TB, W])
    assert at <= 27648
    wprobs, _ = carve(0, [P, 2, NG, TB, W])
    cmax = sb("key_max", [P, 2, NG * TB])
    nM = sb("neg_block_max", [P, HG])
    mparts = sb("block_max_parts", [P, HG, WIN], BF16)
    head_rows = sb("head_rows", [P, H])
    quad_rows = sb("quad_rows", [P, HG, DK])
    mask_keys = sb("mask_keys", [P, HG, WIN], BF16)
    mask_toks = sb("mask_toks", [P, TB, W], BF16)
    tok_rows = sb("tok_rows", [TB, P // TB, TB], BF16)
    mask_seen = sb("mask_seen", [P, HG * WIN], BF16)
    mask_once = sb("mask_once", [P, HG * WIN])
    spread = sb("spread_max", [P, NG, TB, W], BF16)
    zero_rows = sb("zero_rows", [P, D])
    w1m = {}
    for name in ("Wq", "Wk", "Wkp", "Wv", "Wo"):
        w1m[name] = sb("w1_" + name, [D, D])
    w_red = sb("w_red_sb", [D, 16])
    wg = sb("wg_sb", [E, 16])
    wgn = sb("wgn", [E, 16])
    wgs = sb("wg_columns", [E, 4])
    wgT = sb("wgT", [16, E])
    redT = sb("redT", [16, N])
    b1r = sb("b1_ring", [P, 2, FT])
    b2s = sb("b2_sb", [E, D])
    ohT = sb("onehotT", [E, N])

    v_pad = dram("v_padded", (B, PADT, D))
    qs_d = dram("q_parts", (SPLITS, D, N), BF16)
    ks_d = dram("k_parts", (SPLITS, D, N), BF16)

    C = dict(locals())
    block = ctx.enter_context(nc.Block())

    @block.sync
    def _(sp):
        def load(dst, src, s):
            sp.dma_start(dst, src).then_inc(sem(s), 16)

        load(x_tok[:], a["L0_attn_token_embeddings"].rearrange("b (n p) d -> p (b n) d", p=P), "x_in")
        load(splat[:], a["L0_attn_splat_positions"], "splat_in")
        load(splatT[:], a["splat_positions_T"], "splat_in")
        load(splat_ls[:], a["L0_attn_splat_log_scales"].rearrange("(s o) -> s o", o=1), "splat_in")
        load(splat_amp[:], a["L0_attn_splat_amplitudes"].rearrange("(s o) -> s o", o=1), "splat_in")
        for name, t in sqd.items():
            load(t[:], a[name], "w_in")
        load(wqkv[:], a["L0_ffn_w_qkv"], "w_in")
        load(gate_w[:], a["L0_ffn_gate_w"], "w_in")
        for name, t in rows.items():
            load(t[:], a[name].partition_broadcast(P), "rows_in")
        for name, t in lncol.items():
            load(t[:], a[name].rearrange("(d o) -> d o", o=1), "lncol_in")
        load(gate_b[:], a["L0_ffn_gate_b"].partition_broadcast(P), "rows_in")
        load(wproj[:], a["L0_ffn_w_proj"], "wproj_in")

        for n, dst in enumerate((qs_d, ks_d)):
            sp.wait_ge(sem("parts_ready"), NCH * (n + 1))
            load(dst.rearrange("s d t -> d s t"), split_hi, "parts_stored")

        def load_group(G, slot):
            b, g = G // NG, G % NG
            for src_d, dst in ((qs_d, Qs), (ks_d, Ks)):
                q_side = src_d is qs_d
                for h in range(HG):
                    v = src_d[:, bass.ds((g * HG + h) * DK, DK), bass.ds(b * T, T)]
                    for i in range(SPLITS):
                        if q_side:
                            s = v[i].unsqueeze(0).broadcast_to([SPLITS, DK, T])
                        else:
                            s = v
                        load(dst[i * SPLITS * DK:(i + 1) * SPLITS * DK, slot, h * T:(h + 1) * T], s,
                             f"stack_in{slot}")

        def store_max(G, slot):
            sp.wait_ge(sem("max_rows_ready"), G + 1)
            load(Qs[KQ:KX, slot, :], mxrow[:], f"maxrow_in{slot}")

        sp.wait_ge(sem("parts_stored"), 32)
        sp.wait_ge(sem("ksrows_one"), 1)
        for G in range(RING):
            load_group(G, G)
        store_max(0, 0)

        def group(G, slot, prefetch=True):
            store_max(G + 1, (slot + 1) % RING)
            if prefetch:
                sp.wait_ge(sem("scores_done"), (G + 1) * STEPS * 2)
                load_group(G + RING, slot)

        for G in range(GROUPS - 1):
            group(G, G % RING, prefetch=G + RING < GROUPS)

        def experts(w1_d, w2_d, tag, after, b1_d=None):
            sp.wait_ge(sem(after), 1)

            def expert(e, par):
                load(w1r[:, par, :], w1_d[bass.ds(e, 1)].rearrange("o d f -> d (o f)"), f"{tag}_w{par}")
                load(w2r[:, par], w2_d[bass.ds(e, 1)].rearrange("o (f p) d -> p (o f) d", p=P), f"{tag}_w{par}")
                if b1_d is not None:
                    load(b1r[:, par], b1_d[:, bass.ds(e * FT, FT)], f"{tag}_w{par}")

            expert(0, 0)
            expert(1, 1)
            with sp.Fori(0, E // 2 - 1) as it:
                for par in range(2):
                    sp.wait_ge(sem(f"{tag}_y_done"), (it * 2 + par + 1) * NCH)
                    expert(it * 2 + par + 2, par)

        experts(a["L0_ffn_w1"], a["L0_ffn_w2"], "m0", "msa_done")

        for name, t in w1m.items():
            load(t[:], a[f"L1_{name}_T"], "w_l1")
        load(w_red[:], a["L1_ffn_w_red"], "w_l1")
        load(wg[:], a["L1_ffn_wg"], "w_l1")
        load(b2s[:], a["L1_ffn_b2"], "w_l1")
        sp.wait_ge(sem("masks_ready"), 1)
        sp.wait_ge(sem("v1_tok_ready"), NCH)
        for b in range(B):
            load(v_pad[b, 0:W, :], zero_rows[0:W, :], "v_stored")
            load(v_pad[b, W:PADT, :].rearrange("(n p) d -> p n d", p=P), tmp_tok[:, b * MT:(b + 1) * MT, :],
                 "v_stored")
        sp.wait_ge(sem("v_stored"), 64)

        def window(n, b, blk, slot):
            if not (isinstance(n, int) and n < VRING):
                sp.wait_ge(sem("vdiag_ready"), n - VRING + 1)
            src = v_pad[b, bass.ds(blk * TB, WIN), :]
            load(vwin[:, slot, :], src.unsqueeze(0).broadcast_to([HG, WIN, D]), f"window{slot}")

        for n in range(VRING):
            window(n, n % B, n // B, n)
        with sp.Fori(1, BLOCKS // VRING) as it:
            for u in range(VRING):
                window(it * VRING + u, u % B, it * (VRING // B) + u // B, u)
        for n in range(BLOCKS - BLOCKS % VRING, BLOCKS):
            window(n, n % B, n // B, n % VRING)

        experts(a["L1_ffn_w1"], a["L1_ffn_w2"], "m1", "attn1_done", a["L1_b1_cols"])
        sp.wait_ge(sem("final"), 1)
        load(out.rearrange("b (n p) d -> p (b n) d", p=P), x_tok[:], "stored")
        sp.wait_ge(sem("stored"), 16)

    @block.gpsimd
    def _(pool):
        st = Steps(pool, sem("pool_chain"))
        pool.memset(ident[:], 0.0)
        pool.memset(ident_bf[:], 0.0)
        pool.memset(eps[:], LN_EPS).then_inc(sem("eps_ready"), 1)
        pool.memset(ones[:], 1.0).then_inc(sem("ones_ready"), 1)
        pool.wait_ge(sem("ones_ready"), 1)
        for m in (ident, ident_bf):
            pool.affine_select(out=m[:], in_=m[:], compare_op=ALU.not_equal, fill=1.0, base=0,
                               pattern=[[-1, P]], channel_multiplier=1).then_inc(sem("ident_ready"), 1)
        pool.wait_ge(sem("xnT_ready"), NCH)
        for c in range(NCH):
            pool.tensor_tensor(xsqT[:, c * CH:(c + 1) * CH], xnT[:, c * CH:(c + 1) * CH],
                               xnT[:, c * CH:(c + 1) * CH], ALU.mult).then_inc(sem("xsq_ready"), 1)
        pool.wait_ge(sem("splat_done"), 1)
        pool.memset(Ks[64:P, :, :], 1.0).then_inc(sem("ksrows_one"), 1)
        pool.wait_ge(sem("ksrows_one"), 1)
        chain(pool.memset(Vg[:, :, :, :, DK:32], 1.0), st)

        def values(G, slot):
            if not (isinstance(G, int) and G < RING):
                pool.wait_ge(sem("pv_done"), (G - RING + 1) * STEPS)
            b, g = G // NG, G % NG
            src = Vtok[:, bass.ds(b * MT, MT), bass.ds(g * HG * DK, HG * DK)]
            pool.tensor_copy(Vg[:, slot, :, :, 0:DK], src.rearrange("p m (h d) -> p m h d", d=DK)) \
                .then_inc(sem("vg_ready"), 1)

        pool.wait_ge(sem("v_tok_ready"), 1)
        for G in range(GROUPS):
            values(G, G % RING)

        def keep(m, pattern, base, mult, op=ALU.is_ge, fill=0.0):
            chain(pool.affine_select(out=m, in_=m, compare_op=op, fill=fill, base=base, pattern=pattern,
                                     channel_multiplier=mult), st)

        chain(pool.memset(zero_rows[:], 0.0), st)
        chain(pool.memset(head_rows[:], 1.0), st)
        keep(head_rows[:], [[-DK, H]], 0, 1)
        keep(head_rows[:], [[DK, H]], DK - 1, -1)
        chain(pool.memset(quad_rows[:], 1.0), st)
        keep(quad_rows[:], [[-32, HG], [0, DK]], 0, 1)
        keep(quad_rows[:], [[32, HG], [0, DK]], 31, -1)
        chain(pool.memset(mask_keys[:], 0.0), st)
        keep(mask_keys[0:TB], [[0, HG], [1, WIN]], -1, -1, fill=BIG)
        keep(mask_keys[0:TB], [[0, HG], [-1, WIN]], W, 1, fill=BIG)
        chain(pool.memset(mask_keys[32:33], BIG), st)
        chain(pool.memset(mask_keys[64:65, :, 0:W], BIG), st)
        chain(pool.memset(mask_toks[:], 0.0), st)
        chain(pool.memset(mask_toks[32:33], 1.0), st)
        keep(mask_toks[32:33], [[-1, TB], [-1, W]], W - 2, 0)
        chain(pool.memset(mask_toks[64:65], 1.0), st)
        chain(pool.memset(tok_rows[:], 0.0), st)
        keep(tok_rows[:], [[0, P // TB], [-1, TB]], 0, 1, op=ALU.not_equal, fill=1.0)
        chain(pool.memset(mask_once[64:P], 0.0), st)
        chain(pool.memset(spread[:], 0.0), st)
        for part in range(2):
            keep(spread[:], [[-TB, NG], [-1, TB], [0, W]], -64 * part, 1, op=ALU.not_equal, fill=1.0)
        pool.wait_ge(sem("msa_done"), 1)
        for t in (kT, kpT, vT):
            chain(pool.memset(t[:, :, 0:W], 0.0), st)
        pool.memset(zero_rows[:], 0.0).then_inc(sem("masks_ready"), 1)

        def diagonals(n, b, blk, slot, turn):
            three = slot % WRING
            if not (isinstance(n, int) and n < WRING):
                pool.wait_ge(sem("win_scores"), n - 2)
            src = kpT[:, b, bass.ds(blk * TB, WIN)]
            pool.tensor_tensor(kdiag[:, three], src.unsqueeze(1).broadcast_to([P, H, WIN]),
                               head_rows[:].unsqueeze(2).broadcast_to([P, H, WIN]), ALU.mult) \
                .then_inc(sem("kdiag_ready"), 1)
            kw = kT[:, b, bass.ds(blk * TB + 1, TB + W - 1)]
            kw = bass.AP(kw.tensor, kw.offset, [list(kw.ap[0]), [1, TB], [1, W]])
            q = qT[:, bass.ds(blk * TB + b * T, TB)]
            pool.tensor_tensor(qk[:, three], q.unsqueeze(2).broadcast_to([P, TB, W]), kw, ALU.mult) \
                .then_inc(sem("qk_ready"), 1)
            if not (isinstance(n, int) and n < WRING):
                pool.wait_ge(sem("win_rv"), n - 2)
            pool.wait_ge(sem(f"window{slot}"), turn * 16)
            pool.tensor_tensor(vdiag[:, three],
                               vwin[:, slot].rearrange("p (g j d) -> p g j d", g=NG, j=HG),
                               quad_rows[:].unsqueeze(1).broadcast_to([P, NG, HG, DK]), ALU.mult) \
                .then_inc(sem("vdiag_ready"), 1)

        pool.wait_ge(sem("qkv1_ready"), 3 * NCH)
        for n in range(BODY):
            diagonals(n, n % B, n // B, n, 1)
        with pool.Fori(1, BLOCKS // BODY) as it:
            for u in range(BODY):
                diagonals(it * BODY + u, u % B, it * (BODY // B) + u // B, u, it + 1)
        for n in range(BLOCKS - BLOCKS % BODY, BLOCKS):
            diagonals(n, n % B, n // B, n % BODY, n // BODY + 1)

    @block.scalar
    def _(act):
        def evacuate(dst, after, ready, affine=None):
            kw = {} if affine is None else {"scale": lncol[affine + "_w"][:], "bias": lncol[affine + "_b"][:]}
            for c in range(NCH):
                act.wait_ge(sem(after), c + 1)
                act.activation(dst[:, c * CH:(c + 1) * CH], ps[:, c, :], ACT.Identity if affine else ACT.Copy,
                               **kw).then_inc(sem(ready), 1)

        def std(n):
            act.wait_ge(sem("ln_var"), n)
            act.activation(col[:, 4, :], col[:, 3, :], ACT.Sqrt, bias=eps[:], scale=1.0 / D) \
                .then_inc(sem("ln_std"), 1)

        act.wait_ge(sem("eps_ready"), 1)
        std(1)
        evacuate(xnT, "xnT_in_psum", "xnT_ready")
        act.wait_ge(sem("splat_in"), 64)
        act.activation(scol[:, 0:1], splat_ls[:], ACT.Exp).then_inc(sem("splat_scale"), 1)
        for c in range(NCH):
            act.wait_ge(sem("d2_ready"), c + 1)
            act.activation(gaussT[:, c * CH:(c + 1) * CH], gaussT[:, c * CH:(c + 1) * CH], ACT.Exp,
                           scale=scol[:, 3:4]).then_inc(sem("gauss_exp"), 1)
        for c in range(2):
            act.wait_ge(sem("gauss_in_psum"), c + 1)
            act.activation(gauss[:, 8 * c:8 * c + 8, :], ps[:, 4 + c, :].rearrange("p (n s) -> p n s", s=S),
                           ACT.Copy).then_inc(sem("gauss_ready"), 1)

        std(2)
        act.wait_ge(sem("lncol_in"), 4 * 16)
        evacuate(hT, "hT_in_psum", "hT_ready", "L0_ffn_ln1")
        for w in range(2):
            for c in range(NCH):
                n = w * NCH + c
                act.wait_ge(sem("qk_in_psum"), n + 1)
                if n == 0:
                    act.wait_ge(sem("splat_done"), 1)
                if w == 1 and c == 0:
                    act.wait_ge(sem("parts_stored"), 16)
                hi = split_hi[:, 0, c * CH:(c + 1) * CH]
                act.activation(hi, ps[:, n % 4, :], ACT.Copy).then_inc(sem("part_hi"), 1)
                act.wait_ge(sem("part_r1"), n + 1)
                act.activation(split_hi[:, 1, c * CH:(c + 1) * CH], split_r[:, n % 2, 0, :], ACT.Copy) \
                    .then_inc(sem("part_mid"), 1)
        def take_y(half):
            G = half // QH
            act.wait_ge(sem("pv_done"), (half + 1) * MT)
            b, g, col0 = G // NG, G % NG, (G // NG) * T + (half % QH) * CH
            act.activation(Yraw[:, g, col0:col0 + CH], ps[:, YB, :], ACT.Copy).then_inc(sem("y_taken"), 1)

        taken = ("scores_taken", "scores_taken", "y_taken", "v_tok_ready")
        for c in range(NCH):
            act.wait_ge(sem("v_in_psum"), c + 1)
            act.activation(Vtok[:, 4 * c:4 * c + 4, :], ps[:, 4 + c, :].rearrange("p (n d) -> p n d", d=D),
                           ACT.Copy).then_inc(sem(taken[c]), 1)

        for G in range(GROUPS):
            b, g = G // NG, G % NG
            for k in range(STEPS):
                n = G * STEPS + k
                for pair in range(2):
                    act.wait_ge(sem("scores_done"), n * 2 + pair + 1)
                    if n >= 2 and pair == 0:
                        act.wait_ge(sem("pv_done"), n - 1)
                    act.activation(probs[:, k % 2, 2 * pair:2 * pair + 2, :],
                                   ps[:, 2 * pair:2 * pair + 2, :], ACT.Exp, scale=SCALE) \
                        .then_inc(sem("scores_taken"), 1)
                if n and k % MT == 0:
                    take_y(n // MT - 1)
        take_y(GROUPS * QH - 1)

        for c in range(NCH):
            act.wait_ge(sem("yT_in_psum"), c + 1)
            act.activation(hT[:, c * CH:(c + 1) * CH], ps[:, 4 + c, :], ACT.Copy).then_inc(sem("yT_ready"), 1)

        std(3)
        evacuate(hT, "h2T_in_psum", "h2T_ready", "L0_ffn_ln2")

        def gelus(tag, func, bias=None):
            def expert(e, par):
                for c in range(NCH):
                    n = e * NCH + c
                    for f in range(FT):
                        act.wait_ge(sem(f"{tag}_h_in_psum"), n * FT + f + 1)
                        if f == 0 and not (isinstance(e, int) and e == 0 and c < 2):
                            act.wait_ge(sem(f"{tag}_y_done"), n - 1)
                        kw = {} if bias is None else {"bias": bias[:, par, f:f + 1]}
                        act.activation(hid[:, c % 2, f, :], ps[:, f, :], func, **kw) \
                            .then_inc(sem(f"{tag}_h_ready"), 1)
            expert(0, 0)
            expert(1, 1)
            with act.Fori(1, E // 2) as it:
                for par in range(2):
                    expert(it * 2 + par, par)

        gelus("m0", ACT.Gelu_apprx_tanh)

        std(4)
        act.wait_ge(sem("wg_norm2"), 1)
        act.activation(wgs[:, 1:2], wgs[:, 0:1], ACT.Sqrt).then_inc(sem("wg_norm"), 1)
        evacuate(xnT, "xn1T_in_psum", "xn1T_ready")
        for w, dst in enumerate((qT, kT, kpT, vT)):
            for c in range(NCH):
                act.wait_ge(sem("qkv1_in_psum"), w * NCH + c + 1)
                if w == 0:
                    v = dst[:, c * CH:(c + 1) * CH]
                else:
                    v = dst[:, c // QH, W + (c % QH) * CH:W + (c % QH + 1) * CH]
                act.activation(v, ps[:, 4 + (w * NCH + c) % 4, :], ACT.Copy) \
                    .then_inc(sem("qkv1_ready" if w else "q1_ready"), 1)
        for c in range(NCH):
            act.wait_ge(sem("v1_in_psum"), c + 1)
            act.activation(tmp_tok[:, 4 * c:4 * c + 4, :], ps[:, c, :].rearrange("p (n d) -> p n d", d=D),
                           ACT.Copy).then_inc(sem("v1_tok_ready"), 1)
        for c in range(NCH):
            act.wait_ge(sem("red_in_psum"), c + 1)
            act.activation(redT[:, c * CH:(c + 1) * CH], ps[0:16, 4 + c, :], ACT.Copy).then_inc(sem("red_ready"), 1)
        act.wait_ge(sem("gate1_shifted"), 1)
        act.activation(route[:, 3], route[:, 0], ACT.Exp).then_inc(sem("gate1_exp"), 1)

        def window_exp(n, two, three):
            act.wait_ge(sem("win_shifted"), n + 1)
            if not (isinstance(n, int) and n < 2):
                act.wait_ge(sem("win_rv"), n - 1)
            act.activation(wprobs[:, two].rearrange("p g s j -> p (g s j)"),
                           ps[:, 2 * three:2 * three + 2, :].rearrange("p a n -> p (a n)"), ACT.Exp, scale=SCALE) \
                .then_inc(sem("win_exp"), 1)

        for n in range(PEEL):
            window_exp(n, n % 2, n % 3)
        with act.Fori(0, (BLOCKS - PEEL) // BODY) as it:
            for u in range(BODY):
                window_exp(it * BODY + (PEEL + u), u % 2, (PEEL + u) % 3)
        std(5)
        gelus("m1", ACT.Gelu, b1r)

    @block.tensor
    def _(pe):
        def transpose_all(src, after, done):
            for t in range(NT):
                if t % 4 == 0:
                    pe.wait_ge(sem(after), t // 4 + 1)
                m = pe.transpose(ps[:, t // 4, (t % 4) * P:(t % 4 + 1) * P], src[:, t, :], ident[:])
                if t % 4 == 3:
                    m.then_inc(sem(done), 1)

        pe.wait_ge(sem("ident_ready"), 2)
        pe.wait_ge(sem("ones_ready"), 1)
        transpose_all(xn_tok, "xn_ready", "xnT_in_psum")
        pe.wait_ge(sem("splat_scale2"), 1)
        for c in range(NCH):
            cs = slice(c * CH, (c + 1) * CH)
            pe.wait_ge(sem("xnT_ready"), c + 1)
            pe.matmul(ps[0:S, 4 + c, :], splatT[:], xnT[:, cs], start=True, stop=False)
            pe.wait_ge(sem("xsq_ready"), c + 1)
            pe.matmul(ps[0:S, 4 + c, :], ones[:, 0:S], xsqT[:, cs], start=False, stop=True) \
                .then_inc(sem("d2_in_psum"), 1)
        for t in range(NT):
            if t % 4 == 0:
                pe.wait_ge(sem("gaussT_ready"), t // 4 + 1)
            if t % 8 == 0:
                pe.wait_ge(sem("d2_ready"), NCH)
            m = pe.transpose(ps[:, 4 + t // 8, (t % 8) * S:(t % 8 + 1) * S], gaussT[:, t * P:(t + 1) * P],
                             ident[0:S, 0:S])
            if t % 8 == 7:
                m.then_inc(sem("gauss_in_psum"), 1)
        pe.wait_ge(sem("xnT_ready"), NCH)
        for b in range(B):
            pe.wait_ge(sem("gauss_ready"), b + 1)
            for t in range(MT):
                n = b * MT + t
                pe.matmul(ps[:, b, 0:S], xn_tok[:, n, :], gauss[:, n, :], start=t == 0, stop=t == MT - 1)
            for t in range(MT):
                n = b * MT + t
                m = pe.matmul(ps[0:S, 2 + b, 0:1], gauss[:, n, :], ones[:, 0:1], start=t == 0, stop=t == MT - 1)
            m.then_inc(sem("xg_in_psum"), 1)
        pe.wait_ge(sem("w_in"), 64)
        for b in range(B):
            pe.wait_ge(sem("xg_ready"), b + 1)
            pe.matmul(ps[:, 4 + b, 0:S], sqd["L0_attn_Wv"][:], xg[:, b, :], start=True, stop=True) \
                .then_inc(sem("gv_in_psum"), 1)
        for b in range(B):
            pe.wait_ge(sem("gv_ready"), b + 1)
            pe.matmul(ps[0:S, 6 + b, 0:D], gvT[:, b, :], sqd["L0_attn_Wo"][:], start=True, stop=True) \
                .then_inc(sem("gvw_in_psum"), 1)
        pe.wait_ge(sem("gvw_ready"), B)
        for t in range(NT):
            pe.matmul(ps[:, 4, t:t + 1], gaussT[:, t * P:(t + 1) * P], gvw[:, t // MT, D:D + 1], start=True, stop=True)
        for t in range(NT):
            m = pe.matmul(ps[:, t // 4, (t % 4) * D:(t % 4 + 1) * D], gaussT[:, t * P:(t + 1) * P],
                          gvw[:, t // MT, 0:D], start=True, stop=True)
        m.then_inc(sem("splat_in_psum"), 1)

        pe.wait_ge(sem("splat_done"), 1)
        transpose_all(moe_tok, "h_ready", "hT_in_psum")
        pe.wait_ge(sem("hT_ready"), NCH)
        for w in range(2):
            for c in range(NCH):
                if w:
                    pe.wait_ge(sem("parts_ready"), c + 1)
                pe.matmul(ps[:, c, :], wqkv[:, w * D:(w + 1) * D], hT[:, c * CH:(c + 1) * CH],
                          start=True, stop=True).then_inc(sem("qk_in_psum"), 1)
        for t in range(NT):
            m = pe.matmul(ps[:, 4 + t // 4, (t % 4) * D:(t % 4 + 1) * D], hT[:, t * P:(t + 1) * P],
                          wqkv[:, 2 * D:3 * D], start=True, stop=True)
            if t % 4 == 3:
                m.then_inc(sem("v_in_psum"), 1)


        def max_unit(G, slot, u):
            h, q = u // MT, u % MT
            for half in range(2):
                i = 2 * u + half
                n = G * (UNITS * 2) + i
                if i >= MXN:
                    pe.wait_ge(sem("max_taken"), n - MXN + 1)
                elif not (isinstance(G, int) and G == 0):
                    pe.wait_ge(sem("max_taken"), n if i == 0 else n - MXN)
                if i == 2 and not (isinstance(G, int) and G == 0):
                    pe.wait_ge(sem("max_rows_ready"), G)
                pe.matmul(ps[:, MX + i % MXN, :], Qs[0:KQ, slot, h * T + q * P:h * T + (q + 1) * P],
                          Ks[0:KQ, slot, h * T + half * CH:h * T + (half + 1) * CH], start=True, stop=True) \
                    .then_inc(sem("max_scores"), 1)

        def max_rows(G):
            pe.wait_ge(sem("max_split"), G + 1)
            pe.transpose(ps[0:SPLITS * UNITS, MX + 2, 0:P // 2].bitcast(BF16),
                         mxs[:].rearrange("p s u -> p (s u)"), ident_bf[:]).then_inc(sem("max_rows_in_psum"), 1)

        def await_stack(G, slot, turn):
            pe.wait_ge(sem(f"stack_in{slot}"), (turn + 1) * (16 * 2 * HG * SPLITS))

        def group(G, slot, turn, more):
            def after(d):
                return (slot + d) % RING, turn + (slot + d) // RING

            pe.wait_ge(sem(f"maxrow_in{slot}"), (turn + 1) * 16)
            for k in range(STEPS + 1):
                n = G * STEPS + k
                half, m = k // MT, k % MT
                for pair in range(2):
                    if k < STEPS:
                        pe.wait_ge(sem("scores_taken"), n * 2 + pair + 1)
                        for h in (2 * pair, 2 * pair + 1):
                            mm = pe.matmul(ps[:, SC + h, :], Ks[0:KX, slot, h * T + m * P:h * T + (m + 1) * P],
                                           Qs[0:KX, slot, h * T + half * CH:h * T + (half + 1) * CH],
                                           start=True, stop=True)
                        mm.then_inc(sem("scores_done"), 1)
                        u = 2 * (k + AHEAD) + pair
                        if u < UNITS and more >= 1:
                            max_unit(G + 1, after(1)[0], u)
                        if u >= UNITS and more >= 2:
                            if u == UNITS:
                                await_stack(G + 2, *after(2))
                            max_unit(G + 2, after(2)[0], u - UNITS)
                if k == STEPS - AHEAD - 1 and more >= 1:
                    max_rows(G + 1)
                if k:
                    j = k - 1
                    pe.wait_ge(sem("scores_taken"), n * 2 + 2)
                    if j == 0:
                        pe.wait_ge(sem("vg_ready"), G + 1)
                    if j % MT == 0:
                        pe.wait_ge(sem("y_taken"), G * QH + (j // MT + 1))
                    for h in range(HG):
                        mm = pe.matmul(ps[32 * h:32 * h + 32, YB, :], Vg[:, slot, j % MT, h, :],
                                       probs[:, j % 2, h, :], start=j % MT == 0, stop=j % MT == MT - 1)
                    mm.then_inc(sem("pv_done"), 1)

        pe.wait_ge(sem("v_tok_ready"), 1)
        pe.wait_ge(sem("parts_ready"), 2 * NCH)
        await_stack(0, 0, 0)
        for u in range(UNITS):
            max_unit(0, 0, u)
        max_rows(0)
        await_stack(1, 1, 0)
        for u in range(2 * AHEAD):
            max_unit(1, 1, u)
        with pe.Fori(0, GROUPS // RING) as it:
            for slot in range(RING):
                group(it * RING + slot, slot, it, 2)
        for G in range(GROUPS // RING * RING, GROUPS):
            group(G, G % RING, G // RING, GROUPS - 1 - G)

        pe.wait_ge(sem("y_taken"), 1 + GROUPS * QH)
        pe.wait_ge(sem("scores_taken"), 2 + GROUPS * STEPS * 2)
        for t in range(NT):
            if t >= 4:
                pe.wait_ge(sem("quotients"), t - 3)
            for g in range(NG):
                m = pe.transpose(ps[:, t % 4, g * P:(g + 1) * P], Yraw[:, g, t * P:(t + 1) * P], ident[:])
            m.then_inc(sem("y_tok_in_psum"), 1)
        for t in range(NT):
            if t % 4 == 0:
                pe.wait_ge(sem("quotients"), t + 4)
            m = pe.transpose(ps[:, 4 + t // 4, (t % 4) * P:(t % 4 + 1) * P], tmp_tok[:, t, :], ident[:])
            if t % 4 == 3:
                m.then_inc(sem("yT_in_psum"), 1)
        pe.wait_ge(sem("wproj_in"), 16)
        for t in range(NT):
            if t % 4 == 0:
                pe.wait_ge(sem("yT_ready"), t // 4 + 1)
            m = pe.matmul(ps[:, t // 4, (t % 4) * D:(t % 4 + 1) * D], hT[:, t * P:(t + 1) * P], wproj[:],
                          start=True, stop=True)
            if t % 4 == 3:
                m.then_inc(sem("proj_in_psum"), 1)
        pe.wait_ge(sem("msa_done"), 1)

        transpose_all(tmp_tok, "h2_ready", "h2T_in_psum")
        pe.wait_ge(sem("h2T_ready"), NCH)
        for t in range(NT):
            m = pe.matmul(ps[:, 6, t * E:(t + 1) * E], hT[:, t * P:(t + 1) * P], gate_w[:], start=True, stop=True)
        m.then_inc(sem("gate_in_psum"), 1)

        def experts(tag, src, loads):
            def hidden(e, par, c):
                n = e * NCH + c
                for f in range(FT):
                    if not (isinstance(e, int) and e == 0 and c == 0):
                        pe.wait_ge(sem(f"{tag}_h_ready"), (n - 1) * FT + f + 1)
                    pe.matmul(ps[:, f, :], w1r[:, par, f * P:(f + 1) * P], src[:, c * CH:(c + 1) * CH],
                              start=True, stop=True).then_inc(sem(f"{tag}_h_in_psum"), 1)

            def outputs(e, par, c):
                n = e * NCH + c
                pe.wait_ge(sem(f"{tag}_h_ready"), (n + 1) * FT)
                if not (isinstance(e, int) and e == 0 and c < 2):
                    pe.wait_ge(sem(f"{tag}_y_taken"), n - 1)
                for t in range(4):
                    for f in range(FT):
                        m = pe.matmul(ps[:, 4 + c % 2, t * D:(t + 1) * D], hid[:, c % 2, f, t * P:(t + 1) * P],
                                      w2r[:, par, f, :], start=f == 0, stop=f == FT - 1)
                m.then_inc(sem(f"{tag}_y_done"), 1)

            def expert(e, par, turn):
                pe.wait_ge(sem(f"{tag}_w{par}"), (turn + 1) * 16 * loads)
                for c in range(NCH):
                    hidden(e, par, c)
                    if c:
                        outputs(e, par, c - 1)
                outputs(e, par, NCH - 1)

            expert(0, 0, 0)
            expert(1, 1, 0)
            with pe.Fori(1, E // 2) as it:
                for par in range(2):
                    expert(it * 2 + par, par, it)

        experts("m0", hT, 2)

        transpose_all(xn_tok, "xn1_ready", "xn1T_in_psum")
        pe.wait_ge(sem("w_l1"), 8 * 16)
        pe.wait_ge(sem("xn1T_ready"), NCH)
        for w, name in enumerate(("Wq", "Wk", "Wkp", "Wv")):
            for c in range(NCH):
                n = w * NCH + c
                if n >= 4:
                    if n - 4 < NCH:
                        pe.wait_ge(sem("q1_ready"), n - 3)
                    else:
                        pe.wait_ge(sem("qkv1_ready"), n - 3 - NCH)
                pe.matmul(ps[:, 4 + n % 4, :], w1m[name][:], xnT[:, c * CH:(c + 1) * CH],
                          start=True, stop=True).then_inc(sem("qkv1_in_psum"), 1)
        for t in range(NT):
            m = pe.matmul(ps[:, t // 4, (t % 4) * D:(t % 4 + 1) * D], xnT[:, t * P:(t + 1) * P],
                          w1m["Wv"][:], start=True, stop=True)
            if t % 4 == 3:
                m.then_inc(sem("v1_in_psum"), 1)
        pe.wait_ge(sem("qkv1_ready"), 3 * NCH)
        for c in range(NCH):
            pe.matmul(ps[0:16, 4 + c, :], w_red[:], xnT[:, c * CH:(c + 1) * CH], start=True, stop=True) \
                .then_inc(sem("red_in_psum"), 1)
        pe.wait_ge(sem("v1_tok_ready"), NCH)
        pe.wait_ge(sem("wgn_ready"), 1)
        pe.transpose(ps[0:16, 0, 0:E], wgn[:], ident[0:E, 0:E]).then_inc(sem("wgT_in_psum"), 1)
        pe.wait_ge(sem("wgT_ready"), 1)
        pe.wait_ge(sem("red_ready"), NCH)
        for t in range(NT):
            m = pe.matmul(ps[:, 1, t * E:(t + 1) * E], redT[:, t * P:(t + 1) * P], wgT[:], start=True, stop=True)
        m.then_inc(sem("gate1_in_psum"), 1)
        pe.wait_ge(sem("onehot1_ready"), 1)
        for t in range(NT):
            m = pe.transpose(ps[0:E, 2 + t // 4, (t % 4) * P:(t % 4 + 1) * P], oh[:, t, :], ident[:])
            if t % 4 == 3:
                m.then_inc(sem("ohT_in_psum"), 1)
        pe.wait_ge(sem("ohT_ready"), NCH)
        for t in range(NT):
            m = pe.matmul(ps[:, 2 + t // 4, (t % 4) * D:(t % 4 + 1) * D], ohT[:, t * P:(t + 1) * P], b2s[:],
                          start=True, stop=True)
        m.then_inc(sem("b2_in_psum"), 1)
        pe.wait_ge(sem("b2_taken"), 1)

        pe.wait_ge(sem("masks_ready"), 1)
        pe.matmul(ps[:, 0, 0:P], tok_rows[:].rearrange("s q t -> s (q t)"),
                  mask_keys[0:TB].rearrange("p j c -> p (j c)"), start=True, stop=True) \
            .then_inc(sem("mask_in_psum"), 1)
        pe.wait_ge(sem("mask_taken"), 1)
        TB_, RL = 6, 7

        def scores(n, two, three, half, first):
            if half == 0:
                if not (isinstance(n, int) and n < 3):
                    pe.wait_ge(sem("win_exp"), n - 2)
                pe.wait_ge(sem("kdiag_ready"), n + 1)
                pe.wait_ge(sem("qk_ready"), n + 1)
            bank = 2 * three + half
            if first:
                m = mask_toks[:].rearrange("p s j -> p (s j)")
                pe.matmul(ps[:, bank, :], mask_keys[:].rearrange("p j c -> p (j c)"),
                          m.unsqueeze(1).broadcast_to([P, 2, TB * W]), start=True, stop=False,
                          skip_group_check=True)
            for g in (2 * half, 2 * half + 1):
                mm = pe.matmul(ps[:, bank, (g % 2) * TB * W:(g % 2 + 1) * TB * W],
                               kdiag[:, three, HG * g:HG * g + HG, :].rearrange("p j c -> p (j c)"),
                               qk[:, three].rearrange("p s j -> p (s j)"),
                               start=g % 2 == 0 and not first, stop=False, skip_group_check=True)
            if half:
                mm.then_inc(sem("win_scores"), 1)

        def turn_max(n, two):
            pe.wait_ge(sem("win_cmax"), n + 1)
            if not (isinstance(n, int) and n == 0):
                pe.wait_ge(sem("win_mparts"), n)
            pe.matmul(ps[:, TB_, 0:P], ident_bf[:], mask_seen[:], start=True, stop=False, skip_group_check=True)
            for part in range(2):
                mm = pe.matmul(ps[64 * part:64 * part + 64, TB_, 0:P], cmax[:, two], ident[:],
                               start=False, stop=True, skip_group_check=True)
            mm.then_inc(sem("win_max_in_psum"), 1)

        def shift(n, three):
            pe.wait_ge(sem("win_mparts"), n + 1)
            lhs = mparts[:].rearrange("p j c -> p (j c)")
            for g in range(NG):
                mm = pe.matmul(ps[:, 2 * three + g // 2, (g % 2) * TB * W:(g % 2 + 1) * TB * W], lhs,
                               spread[:, g].rearrange("p s j -> p (s j)"),
                               start=False, stop=g % 2 == 1, skip_group_check=True)
            mm.then_inc(sem("win_shifted"), 1)

        def value_products(n, two, three):
            pe.wait_ge(sem("win_exp"), n + 1)
            pe.wait_ge(sem("vdiag_ready"), n + 1)
            if not (isinstance(n, int) and n == 0):
                pe.wait_ge(sem("win_den_taken"), n)
            for part in range(2):
                for g in range(NG):
                    lhs = vdiag[:, three, g] if part == 0 else quad_rows[:]
                    mm = pe.matmul(ps[32 * g:32 * g + 32, RL, part * TB * W:(part + 1) * TB * W],
                                   lhs.rearrange("p j d -> p (j d)"),
                                   wprobs[:, two, g].rearrange("p s j -> p (s j)"), start=True, stop=True,
                                   skip_group_check=True)
            mm.then_inc(sem("win_rv"), 1)

        for n in range(PEEL):
            scores(n, n % 2, n, 0, True)
            if n:
                turn_max(n - 1, (n - 1) % 2)
            scores(n, n % 2, n, 1, True)
            if n:
                shift(n - 1, n - 1)
        with pe.Fori(0, (BLOCKS - PEEL) // BODY) as it:
            for u in range(BODY):
                n = it * BODY + (PEEL + u)
                scores(n, u % 2, (PEEL + u) % 3, 0, False)
                turn_max(it * BODY + (PEEL + u - 1), (u - 1) % 2)
                scores(n, u % 2, (PEEL + u) % 3, 1, False)
                shift(it * BODY + (PEEL + u - 1), (PEEL + u - 1) % 3)
                value_products(it * BODY + (PEEL + u - 2), u % 2, (PEEL + u - 2) % 3)
        turn_max(BLOCKS - 1, (BLOCKS - 1) % 2)
        shift(BLOCKS - 1, (BLOCKS - 1) % 3)
        value_products(BLOCKS - 2, 0, (BLOCKS - 2) % 3)
        value_products(BLOCKS - 1, 1, (BLOCKS - 1) % 3)

        pe.wait_ge(sem("zT_ready"), 1)
        for t in range(NT):
            m = pe.matmul(ps[:, t // 4, (t % 4) * D:(t % 4 + 1) * D], zT[:, t * P:(t + 1) * P], w1m["Wo"][:],
                          start=True, stop=True)
        m.then_inc(sem("wo_in_psum"), 1)
        pe.wait_ge(sem("attn1_done"), NCH)
        experts("m1", xnT, 3)

    @block.vector
    def _(dve):
        st = Steps(dve, sem("dve_chain"))

        def bc(v, n):
            return v.unsqueeze(2).broadcast_to([P, NT, n])

        def row(v):
            return v.unsqueeze(1).broadcast_to([P, NT, D])

        def layernorm(dst, src, n, done, scratch=None):
            for t in range(NT):
                last = dve.bn_stats(stats[:, t, :], src[:, t, :])
            chain(last, st)
            mean0, m2_0, mean1, m2_1 = (stats[:, :, i] for i in (1, 2, 4, 5))
            dve.tensor_tensor(col[:, 0, :], mean0, mean1, ALU.add)
            dve.tensor_tensor(col[:, 1, :], mean0, mean1, ALU.subtract)
            chain(dve.tensor_tensor(col[:, 2, :], m2_0, m2_1, ALU.add), st)
            dve.tensor_scalar(col[:, 0, :], col[:, 0, :], -0.5, None, ALU.mult)
            chain(dve.tensor_tensor(col[:, 1, :], col[:, 1, :], col[:, 1, :], ALU.mult), st)
            dve.scalar_tensor_tensor(col[:, 3, :], col[:, 1, :], D / 4.0, col[:, 2, :], ALU.mult, ALU.add) \
                .then_inc(sem("ln_var"), 1)
            dve.wait_ge(sem("ln_std"), n)
            chain(dve.reciprocal(col[:, 3, :], col[:, 4, :]), st)
            for t in range(NT):
                last = dve.tensor_scalar(dst[:, t, :], src[:, t, :], col[:, 0, t:t + 1], col[:, 3, t:t + 1],
                                         ALU.add, ALU.mult)
                if t % 4 == 3:
                    last.then_inc(sem(done), 1)
            dve.wait_ge(sem(done), NCH)

        dve.wait_ge(sem("x_in"), 16)
        layernorm(xn_tok, x_tok, 1, "xn_ready")

        dve.wait_ge(sem("splat_in"), 64)
        chain(dve.tensor_tensor(tmp_tok[0:S, 0, :], splat[:], splat[:], ALU.mult), st)
        chain(dve.tensor_reduce(scol[:, 4:5], tmp_tok[0:S, 0, :], X, ALU.add), st)
        chain(dve.tensor_scalar(splatT[:], splatT[:], -2.0, None, ALU.mult), st)
        dve.wait_ge(sem("splat_scale"), 1)
        chain(dve.tensor_tensor(scol[:, 1:2], scol[:, 0:1], scol[:, 0:1], ALU.mult), st)
        chain(dve.reciprocal(scol[:, 2:3], scol[:, 1:2]), st)
        dve.tensor_scalar(scol[:, 3:4], scol[:, 2:3], -0.5, None, ALU.mult).then_inc(sem("splat_scale2"), 1)
        dve.wait_ge(sem("splat_scale2"), 1)
        for c in range(NCH):
            dve.wait_ge(sem("d2_in_psum"), c + 1)
            dve.tensor_scalar(gaussT[:, c * CH:(c + 1) * CH], ps[0:S, 4 + c, :], scol[:, 4:5], 0.0,
                              ALU.add, ALU.max).then_inc(sem("d2_ready"), 1)
        for c in range(NCH):
            dve.wait_ge(sem("gauss_exp"), c + 1)
            dve.tensor_scalar(gaussT[:, c * CH:(c + 1) * CH], gaussT[:, c * CH:(c + 1) * CH], splat_amp[:], None,
                              ALU.mult).then_inc(sem("gaussT_ready"), 1)
        for b in range(B):
            dve.wait_ge(sem("xg_in_psum"), b + 1)
            dve.tensor_copy(gvw[:, b, D:D + 1], ps[0:S, 2 + b, 0:1])
            dve.tensor_copy(xg[:, b, :], ps[:, b, 0:S]).then_inc(sem("xg_ready"), 1)
        for b in range(B):
            dve.wait_ge(sem("gv_in_psum"), b + 1)
            dve.tensor_copy(gvT[:, b, :], ps[:, 4 + b, 0:S]).then_inc(sem("gv_ready"), 1)
        for b in range(B):
            dve.wait_ge(sem("gvw_in_psum"), b + 1)
            dve.tensor_copy(gvw[:, b, 0:D], ps[0:S, 6 + b, 0:D]).then_inc(sem("gvw_ready"), 1)
        dve.wait_ge(sem("splat_in_psum"), 1)
        chain(dve.tensor_scalar(col[:, 4, :], ps[:, 4, 0:NT], SPLAT_EPS, None, ALU.add), st)
        chain(dve.reciprocal(col[:, 5, :], col[:, 4, :]), st)
        chain(dve.tensor_tensor(tmp_tok[:], ps[:, 0:4, :].rearrange("p c (t d) -> p (c t) d", d=D),
                                bc(col[:, 5, :], D), ALU.mult), st)
        dve.tensor_tensor(x_tok[:], x_tok[:], tmp_tok[:], ALU.add).then_inc(sem("splat_done"), 1)
        dve.wait_ge(sem("splat_done"), 1)

        dve.wait_ge(sem("rows_in"), 3 * 16)
        layernorm(moe_tok, xn_tok, 2, "h_ready")
        for w in range(2):
            for c in range(NCH):
                n = w * NCH + c
                r1, r2 = split_r[:, n % 2, 0, :], split_r[:, n % 2, 1, :]
                dve.wait_ge(sem("part_hi"), n + 1)
                dve.tensor_tensor(r1, ps[:, n % 4, :], split_hi[:, 0, c * CH:(c + 1) * CH], ALU.subtract) \
                    .then_inc(sem("part_r1"), 1)
                dve.wait_ge(sem("part_mid"), n + 1)
                dve.tensor_tensor(split_hi[:, 2, c * CH:(c + 1) * CH], r1, split_hi[:, 1, c * CH:(c + 1) * CH],
                                  ALU.subtract).then_inc(sem("parts_ready"), 1)

        def max_unit(G, u):
            for i in (2 * u, 2 * u + 1):
                dve.wait_ge(sem("max_scores"), G * (UNITS * 2) + (i + 1))
                dve.tensor_reduce(mxh[:, u, i % 2:i % 2 + 1], ps[:, MX + i % MXN, :], X, ALU.max) \
                    .then_inc(sem("max_taken"), 1)

        def max_rows(G, before=None):
            dve.wait_ge(sem("max_taken"), (G + 1) * (UNITS * 2))
            chain(dve.tensor_reduce(nmx[:], mxh[:], X, ALU.max, negate=True), st)
            chain(dve.tensor_copy(mxs[:, 0, :], nmx[:]), st)
            chain(dve.tensor_tensor(mxr[:], nmx[:], mxs[:, 0, :], ALU.subtract), st)
            chain(dve.tensor_copy(mxs[:, 1, :], mxr[:]), st)
            dve.tensor_tensor(mxs[:, 2, :], mxr[:], mxs[:, 1, :], ALU.subtract).then_inc(sem("max_split"), 1)
            dve.wait_ge(sem("max_rows_in_psum"), G + 1)
            if before is not None:
                slot, turn = before
                dve.wait_ge(sem(f"maxrow_in{slot}"), (turn + 1) * 16)
            dve.tensor_copy(mxrow[:], ps[0:SPLITS * UNITS, MX + 2, 0:P // 2].bitcast(BF16)) \
                .then_inc(sem("max_rows_ready"), 1)

        def group_maxima(G, slot, turn, more):
            for u in range(2 * AHEAD, UNITS):
                max_unit(G + 1, u)
            max_rows(G + 1, (slot, turn))
            if more >= 2:
                for u in range(2 * AHEAD):
                    max_unit(G + 2, u)

        for u in range(UNITS):
            max_unit(0, u)
        max_rows(0)
        for u in range(2 * AHEAD):
            max_unit(1, u)
        with dve.Fori(0, GROUPS // RING) as it:
            st.enter(it, 4 * RING)
            for slot in range(RING):
                group_maxima(it * RING + slot, slot, it, 2)
        st.leave(GROUPS // RING)
        for G in range(GROUPS // RING * RING, GROUPS - 1):
            group_maxima(G, G % RING, G // RING, GROUPS - 1 - G)

        for t in range(NT):
            dve.wait_ge(sem("y_tok_in_psum"), t + 1)
            v = ps[:, t % 4, :].rearrange("p (h r) -> p h r", r=32)
            chain(dve.reciprocal(rden[:, t % 2], v[:, :, DK:DK + 1]), st)
            dve.tensor_tensor(tmp_tok[:, t, :].rearrange("p (h d) -> p h d", d=DK), v[:, :, 0:DK],
                              rden[:, t % 2].broadcast_to([P, H, DK]), ALU.mult).then_inc(sem("quotients"), 1)
        for c in range(NCH):
            dve.wait_ge(sem("proj_in_psum"), c + 1)
            last = dve.tensor_tensor(moe_tok[:, 4 * c:4 * c + 4, :],
                                     ps[:, c, :].rearrange("p (t d) -> p t d", d=D),
                                     xn_tok[:, 4 * c:4 * c + 4, :], ALU.add)
        last.then_inc(sem("msa_done"), 1)
        dve.wait_ge(sem("msa_done"), 1)

        layernorm(tmp_tok, moe_tok, 3, "h2_ready")

        def ebc(v):
            return v.unsqueeze(2).broadcast_to([P, NT, E])

        def first_max(logits, dst):
            chain(dve.tensor_reduce(col[:, 4, :], logits, X, ALU.max), st)
            chain(dve.tensor_tensor(route[:, 1], logits, ebc(col[:, 4, :]), ALU.is_equal), st)
            for e in range(E):
                last = dve.memset(route[:, 2, :, e:e + 1], float(E - e))
            chain(last, st)
            chain(dve.tensor_tensor(route[:, 1], route[:, 1], route[:, 2], ALU.mult), st)
            chain(dve.tensor_reduce(col[:, 5, :], route[:, 1], X, ALU.max), st)
            chain(dve.tensor_tensor(dst, route[:, 1], ebc(col[:, 5, :]), ALU.is_equal), st)

        dve.wait_ge(sem("gate_in_psum"), 1)
        chain(dve.tensor_tensor(route[:, 0], ps[:, 6, 0:NT * E].rearrange("p (t e) -> p t e", e=E),
                                gate_b[:].unsqueeze(1).broadcast_to([P, NT, E]), ALU.add), st)
        first_max(route[:, 0], oh[:])

        def add_experts(tag):
            def expert(e):
                for c in range(NCH):
                    n = e * NCH + c
                    dve.wait_ge(sem(f"{tag}_y_done"), n + 1)
                    if not (isinstance(e, int) and e == 0):
                        dve.wait_ge(sem(f"{tag}_y_taken"), n - NCH + 1)
                    for t in range(4):
                        tt = 4 * c + t
                        last = dve.scalar_tensor_tensor(
                            moe_tok[:, tt, :], ps[:, 4 + c % 2, t * D:(t + 1) * D], oh[:, tt, bass.ds(e, 1)],
                            moe_tok[:, tt, :], ALU.mult, ALU.add)
                    last.then_inc(sem(f"{tag}_y_taken"), 1)
            expert(0)
            with dve.Fori(1, E) as e:
                expert(e)

        add_experts("m0")
        dve.wait_ge(sem("m0_y_taken"), E * NCH)
        chain(dve.tensor_tensor(x_tok[:], x_tok[:], moe_tok[:], ALU.add), st)

        dve.wait_ge(sem("w_l1"), 8 * 16)
        chain(dve.tensor_tensor(wgn[:], wg[:], wg[:], ALU.mult), st)
        dve.tensor_reduce(wgs[:, 0:1], wgn[:], X, ALU.add).then_inc(sem("wg_norm2"), 1)
        layernorm(xn_tok, x_tok, 4, "xn1_ready")
        dve.wait_ge(sem("wg_norm"), 1)
        chain(dve.tensor_scalar(wgs[:, 2:3], wgs[:, 1:2], 1e-4, None, ALU.max), st)
        chain(dve.reciprocal(wgs[:, 3:4], wgs[:, 2:3]), st)
        dve.tensor_scalar(wgn[:], wg[:], wgs[:, 3:4], None, ALU.mult).then_inc(sem("wgn_ready"), 1)
        dve.wait_ge(sem("wgT_in_psum"), 1)
        dve.tensor_copy(wgT[:], ps[0:16, 0, 0:E]).then_inc(sem("wgT_ready"), 1)
        dve.wait_ge(sem("gate1_in_psum"), 1)
        lg = ps[:, 1, 0:NT * E].rearrange("p (t e) -> p t e", e=E)
        chain(dve.tensor_reduce(col[:, 4, :], lg, X, ALU.max), st)
        dve.tensor_tensor(route[:, 0], lg, ebc(col[:, 4, :]), ALU.subtract).then_inc(sem("gate1_shifted"), 1)
        dve.wait_ge(sem("gate1_exp"), 1)
        chain(dve.tensor_reduce(col[:, 6, :], route[:, 3], X, ALU.add), st)
        chain(dve.reciprocal(col[:, 7, :], col[:, 6, :]), st)
        chain(dve.tensor_tensor(route[:, 3], route[:, 3], ebc(col[:, 7, :]), ALU.mult), st)
        first_max(route[:, 3], oh[:])
        dve.tensor_tensor(oh[:], oh[:], route[:, 3], ALU.mult).then_inc(sem("onehot1_ready"), 1)
        for c in range(NCH):
            dve.wait_ge(sem("ohT_in_psum"), c + 1)
            dve.tensor_copy(ohT[:, c * CH:(c + 1) * CH], ps[0:E, 2 + c, :]).then_inc(sem("ohT_ready"), 1)
        dve.wait_ge(sem("b2_in_psum"), 1)
        dve.tensor_copy(moe_tok[:], ps[:, 2:6, :].rearrange("p c (t d) -> p (c t) d", d=D)) \
            .then_inc(sem("b2_taken"), 1)

        dve.wait_ge(sem("mask_in_psum"), 1)
        dve.tensor_copy(mask_seen[:], ps[:, 0, 0:P])
        dve.tensor_copy(mask_once[0:64], ps[0:64, 0, 0:P]).then_inc(sem("mask_taken"), 1)

        def key_max(n, two, three):
            dve.wait_ge(sem("win_scores"), n + 1)
            if not (isinstance(n, int) and n < 2):
                dve.wait_ge(sem("win_max_in_psum"), n - 1)
            dve.tensor_reduce(cmax[:, two].rearrange("p (g s) -> p g s", s=TB),
                              ps[:, 2 * three:2 * three + 2, :].rearrange("p a (g s j) -> p (a g) s j", s=TB, j=W),
                              X, ALU.max).then_inc(sem("win_cmax"), 1)

        def max_parts(n, per=None):
            dve.wait_ge(sem("win_max_in_psum"), n + 1)
            if not (isinstance(n, int) and n == 0):
                dve.wait_ge(sem("win_shifted"), n)
            chain(dve.tensor_reduce(nM[:], ps[:, 6, 0:P].rearrange("p (j c) -> p j c", c=WIN), X, ALU.max,
                                    negate=True), st)
            wide = nM[:].unsqueeze(2).broadcast_to([P, HG, WIN])
            chain(dve.tensor_tensor(mparts[:], mask_once[:].rearrange("p (j c) -> p j c", c=WIN), wide, ALU.add), st)
            dve.tensor_tensor(mparts[64:P], wide[64:P], mparts[64:P], ALU.subtract) \
                .then_inc(sem("win_mparts"), 1)

        def first_key_sum(n, b, blk, two):
            dve.wait_ge(sem("win_rv"), n + 1)
            vw = vT[:, b, bass.ds(blk * TB + 1, TB + W - 1)]
            vw = bass.AP(vw.tensor, vw.offset, [list(vw.ap[0]), [1, TB], [1, W]])
            r = ps[:, 7, 0:TB * W].rearrange("p (s j) -> p s j", j=W)
            den = ps[:, 7, TB * W:2 * TB * W].rearrange("p (s j) -> p s j", j=W)
            chain(dve.tensor_tensor(rv[:, two], r, vw, ALU.mult), st)
            dve.tensor_reduce(denT[:, bass.ds(blk * TB + b * T, TB)], den, X, ALU.add) \
                .then_inc(sem("win_den_taken"), 1)
            dve.tensor_reduce(zT[:, bass.ds(blk * TB + b * T, TB)], rv[:, two], X, ALU.add) \
                .then_inc(sem("win_z"), 1)

        for n in range(PEEL):
            if n:
                max_parts(n - 1)
            key_max(n, n % 2, n % 3)
        with dve.Fori(0, (BLOCKS - PEEL) // BODY) as it:
            st.enter(it, 3 * BODY)
            for u in range(BODY):
                max_parts(it * BODY + (PEEL + u - 1))
                key_max(it * BODY + (PEEL + u), u % 2, (PEEL + u) % 3)
                first_key_sum(it * BODY + (PEEL + u - 2), u % B, it * (BODY // B) + (PEEL + u - 2) // B, u % 2)
        st.leave((BLOCKS - PEEL) // BODY)
        max_parts(BLOCKS - 1)
        first_key_sum(BLOCKS - 2, 0, NB - 1, 0)
        first_key_sum(BLOCKS - 1, 1, NB - 1, 1)
        dve.wait_ge(sem("win_z"), BLOCKS)
        dve.wait_ge(sem("win_den_taken"), BLOCKS)
        chain(dve.reciprocal(denT[:], denT[:]), st)
        dve.tensor_tensor(zT[:], zT[:], denT[:], ALU.mult).then_inc(sem("zT_ready"), 1)
        dve.wait_ge(sem("wo_in_psum"), 1)
        chain(dve.tensor_tensor(tmp_tok[:], ps[:, 0:4, :].rearrange("p c (t d) -> p (c t) d", d=D), xn_tok[:],
                                ALU.add), st)
        layernorm(xn_tok, tmp_tok, 5, "attn1_done")
        chain(dve.tensor_tensor(xn_tok[:], xn_tok[:], row(rows["L1_attn_gamma"][:]), ALU.mult), st)
        chain(dve.tensor_tensor(xn_tok[:], xn_tok[:], row(rows["L1_attn_beta"][:]), ALU.add), st)
        chain(dve.tensor_tensor(x_tok[:], x_tok[:], xn_tok[:], ALU.add), st)
        add_experts("m1")
        dve.wait_ge(sem("m1_y_taken"), E * NCH)
        dve.tensor_tensor(x_tok[:], x_tok[:], moe_tok[:], ALU.add).then_inc(sem("final"), 1)


_INS = ["L0_attn_token_embeddings", "L0_attn_splat_positions", "L0_attn_splat_log_scales",
        "L0_attn_splat_amplitudes", "L0_attn_Wv", "L0_attn_Wo", "L0_ffn_ln1_w", "L0_ffn_ln1_b",
        "L0_ffn_w_qkv", "L0_ffn_w_proj", "L0_ffn_ln2_w", "L0_ffn_ln2_b", "L0_ffn_gate_w", "L0_ffn_gate_b",
        "L0_ffn_w1", "L0_ffn_w2", "L1_attn_gamma", "L1_attn_beta", "L1_ffn_w_red", "L1_ffn_wg",
        "L1_ffn_w1", "L1_ffn_w2", "L1_ffn_b2"]


def laid_out(inputs):
    import numpy as np
    got = {name: np.ascontiguousarray(inputs[name]) for name in _INS}
    got["splat_positions_T"] = np.ascontiguousarray(np.asarray(inputs["L0_attn_splat_positions"]).T)
    for name in ("Wq", "Wk", "Wv", "Wkp", "Wo"):
        got[f"L1_{name}_T"] = np.ascontiguousarray(np.asarray(inputs[f"L1_attn_{name}"]).T)
    b1 = np.asarray(inputs["L1_ffn_b1"]).reshape(E, FT, P)
    got["L1_b1_cols"] = np.ascontiguousarray(b1.transpose(2, 0, 1).reshape(P, E * FT))
    return got


def kernel(**inputs):
    import concourse.bacc as bacc
    from concourse.bass_utils import run_bass_kernel_spmd

    nc = bacc.Bacc("TRN2", target_bir_lowering=False, num_devices=1)
    arrays, aps = {}, {}
    for name, v in laid_out(inputs).items():
        arrays[f"in_{name}"] = v
        aps[name] = nc.dram_tensor(f"in_{name}", v.shape, mybir.dt.from_np(v.dtype), kind="ExternalInput").ap()
    out = nc.dram_tensor("out_x", (B, T, D), F32, kind="ExternalOutput").ap()
    two_layers(nc, aps, out)
    r = run_bass_kernel_spmd(nc, [arrays], core_ids=[0])
    return r.results[0]["out_x"]
```

```python
from contextlib import ExitStack

import concourse.bass as bass
from concourse import mybir

F32 = mybir.dt.float32
BF16 = mybir.dt.bfloat16
I32 = mybir.dt.int32
ALU = mybir.AluOpType
ACT = mybir.ActivationFunctionType
X = mybir.AxisListType.X

P = 128
D = 128
B, T = 2, 1024
N = B * T
NT = N // P
CH = 512
NCH = N // CH
H, DK = 16, 8
S = 64
E = 8
HID = 512
FT = HID // P
LN_EPS = 1e-5
SPLAT_EPS = 1e-8
SCALE = float(DK) ** -0.5

HG = 4
NG = H // HG
GROUPS = B * NG
SPLITS = 3
KQ = SPLITS * SPLITS * DK
KX = KQ + SPLITS
RING = 3
MT = T // P
QH = T // CH
STEPS = QH * MT
UNITS = HG * MT

MTILES = NT + E
ER = 3
FIRST = 4
FIRST_TILE = {"m0": 0, "m1": MTILES}
EW = HID + FT * D
EWB = EW + FT

W = 16
TB = 16
WIN = W + TB
NB = T // TB
PADT = T + W
ARENA = 27648
MOE0 = 8224
SC, MX, MXN, YB = 0, 4, 3, 7
AHEAD = 3
BIG = -1.0e30
PEEL, BODY, VRING = 2, 6, 6
WRING = 3
BLOCKS = B * NB


def chain(ins, steps):
    ins.then_inc(steps.sem, 1)
    steps.n += 1
    steps.eng.wait_ge(steps.sem, steps.base() + steps.n)


class Steps:

    def __init__(self, eng, sem):
        self.eng, self.sem, self.n, self.loop, self.per = eng, sem, 0, None, 0

    def base(self):
        return 0 if self.loop is None else self.loop * self.per

    def enter(self, i, per):
        self.loop, self.per, self.start = i, per, self.n

    def leave(self, times):
        assert self.n - self.start == self.per, (self.n - self.start, self.per)
        self.n += (times - 1) * self.per
        self.loop = None


def two_layers(nc, a, out):
    with ExitStack() as ctx:
        build(nc, ctx, a, out)


def build(nc, ctx, a, out):
    def sb(name, shape, dt=F32):
        return ctx.enter_context(nc.sbuf_tensor(name, shape, dt))

    def dram(name, shape, dt=F32):
        return nc.dram_tensor(name, shape, dt, kind="Internal").ap()

    sems = {}

    def sem(name):
        if name not in sems:
            sems[name] = ctx.enter_context(nc.semaphore(name))
        return sems[name]

    ps = ctx.enter_context(nc.psum_tensor("ps", [P, 8, CH], F32))

    x_tok = sb("x_tok", [P, NT, D])
    xn_tok = sb("xn_tok", [P, NT, D])
    moe_tok = sb("moe_tok", [P, NT, D])
    tmp_tok = sb("tmp_tok", [P, NT, D])
    xnT = sb("xnT", [P, N])
    hT = sb("hT", [P, N])

    ident = sb("ident", [P, P])
    ident_bf = sb("ident_bf", [P, P], BF16)
    ones = sb("ones", [P, 128])
    eps = sb("eps", [P, 1])
    rows = {}
    for name in ("L1_attn_gamma", "L1_attn_beta"):
        rows[name] = sb("row_" + name, [P, D])
    lncol = {}
    for name in ("L0_ffn_ln1_w", "L0_ffn_ln1_b", "L0_ffn_ln2_w", "L0_ffn_ln2_b"):
        lncol[name] = sb("col_" + name, [P, 1])
    gate_b = sb("gate_b_row", [P, E])
    col = sb("columns", [P, 8, NT])
    stats = sb("stats", [P, NT, 6])

    sqd = {"L0_attn_Wv": None, "L0_attn_Wo": None}
    for name in sqd:
        sqd[name] = sb("w_" + name, [D, D])
    wqkv = sb("wqkv", [D, 3 * D])
    gate_w = sb("gate_w_sb", [D, E])
    wproj = sb("wproj", [D, D])
    splatT = sb("splatT", [D, S])
    splat = sb("splat", [S, D])
    splat_ls = sb("splat_ls", [S, 1])
    splat_amp = sb("splat_amp", [S, 1])
    scol = sb("splat_columns", [S, 6])

    arena = sb("arena", [P, ARENA])

    def carve(at, shape, dt=F32):
        n = 1
        for s in shape[1:]:
            n *= s
        words = n * (4 if dt == F32 else 2) // 4
        v = arena[0:shape[0], at:at + words]
        if dt != F32:
            v = v.bitcast(dt)
        if len(shape) > 2:
            names = "abcd"[:len(shape) - 1]
            v = v.rearrange("p (" + " ".join(names) + ") -> p " + " ".join(names),
                            **dict(zip(names[1:], shape[2:])))
        return v, at + words

    xsqT, at = carve(0, [P, N])
    gaussT, at = carve(at, [S, N])
    gauss, at = carve(at, [P, NT, S])
    xg, at = carve(at, [P, B, S])
    gvT, at = carve(at, [P, B, S])
    gvw, at = carve(at, [S, B, D + 1])
    Qs, at = carve(0, [P, RING, HG * T], BF16)
    Ks, at = carve(at, [P, RING, HG * T], BF16)
    probs, at = carve(at, [P, 2, HG, CH])
    Vg, at = carve(at, [P, RING, MT, HG, 32])
    split_hi, _ = carve(at, [P, SPLITS, N], BF16)
    split_r, _ = carve(at + SPLITS * N // 2, [P, 2, 2, CH])
    Yraw, at = carve(at, [P, NG, N])
    Vtok = tmp_tok
    Ytok1 = hT[:].rearrange("p (t d) -> p t d", d=D)
    mxh = sb("mx_halves", [P, UNITS, 2])
    nmx = sb("neg_max", [P, UNITS])
    mxr = sb("max_rest", [P, UNITS])
    mxs = sb("max_parts", [P, SPLITS, UNITS], BF16)
    mxrow = sb("max_rows", [SPLITS * UNITS, P], BF16)
    wall, at = carve(0, [P, E, EWB])
    assert at <= MOE0
    at = MOE0
    wcur, at = carve(at, [P, ER, EWB])
    xs, at = carve(at, [P, ER, D])
    xsT, at = carve(at, [P, ER, P])
    hid, at = carve(at, [P, ER, FT, P])
    ys, at = carve(at, [P, ER, D])
    assert at <= MOE0 + N + 2 * B * PADT
    rden = sb("rden", [P, 2, H, 1])
    route = sb("route", [P, 6, NT, E])
    chosen = sb("chosen", [P, NT, E])
    earlier = sb("earlier", [P, P])
    count = sb("count_from_0", [P, MTILES])
    tile_start = sb("tile_start", [P, NT])
    filled = sb("filled_tiles", [P, E, NT])
    tiles_to = sb("tiles_up_to_expert", [P, 4, E])
    first_slot = sb("first_slot", [P, E])
    ended = sb("experts_ended", [P, MTILES, E])
    te_f = sb("tile_expert_f", [P, MTILES])
    slot_f = sb("slot_f", [P, NT])
    score = sb("score", [P, NT])
    tok_slot = {tag: sb(f"{tag}_slot", [P, NT], I32) for tag in FIRST_TILE}
    tile_expert = sb("tile_expert", [P, 2 * MTILES], I32)
    zero_tok = sb("zero_tok", [P, D])
    oh = sb("onehot", [P, NT, E])
    qT, at = carve(MOE0, [P, N])
    kT, at = carve(at, [P, B, PADT])
    kpT, at = carve(at, [P, B, PADT])
    vT, at = carve(at, [P, B, PADT])
    zT, at = carve(at, [P, N])
    denT, at = carve(at, [P, N])
    qk, at = carve(at, [P, WRING, TB, W])
    kdiag, at = carve(at, [P, WRING, H, WIN])
    vwin, at = carve(at, [P, VRING, D])
    vdiag, at = carve(at, [P, WRING, NG, HG, DK])
    rv, at = carve(at, [P, 2, TB, W])
    wprobs, at = carve(at, [P, 2, NG, TB, W])
    assert at <= ARENA
    cmax = sb("key_max", [P, 2, NG * TB])
    nM = sb("neg_block_max", [P, HG])
    mparts = sb("block_max_parts", [P, HG, WIN], BF16)
    head_rows = sb("head_rows", [P, H])
    quad_rows = sb("quad_rows", [P, HG, DK])
    mask_keys = sb("mask_keys", [P, HG, WIN], BF16)
    mask_toks = sb("mask_toks", [P, TB, W], BF16)
    tok_rows = sb("tok_rows", [TB, P // TB, TB], BF16)
    mask_seen = sb("mask_seen", [P, HG * WIN], BF16)
    mask_once = sb("mask_once", [P, HG * WIN])
    spread = sb("spread_max", [P, NG, TB, W], BF16)
    zero_rows = sb("zero_rows", [P, D])
    w1m = {}
    for name in ("Wq", "Wk", "Wkp", "Wv", "Wo"):
        w1m[name] = sb("w1_" + name, [D, D])
    w_red = sb("w_red_sb", [D, 16])
    wg = sb("wg_sb", [E, 16])
    wgn = sb("wgn", [E, 16])
    wgs = sb("wg_columns", [E, 4])
    wgT = sb("wgT", [16, E])
    redT = sb("redT", [16, N])
    b2s = sb("b2_sb", [E, D])
    ohT = sb("onehotT", [E, N])

    xs_d = {tag: dram(f"{tag}_tokens_sorted", (MTILES * P, D)) for tag in FIRST_TILE}
    ys_d = {tag: dram(f"{tag}_results_sorted", (MTILES * P, D)) for tag in FIRST_TILE}
    v_pad = dram("v_padded", (B, PADT, D))
    qs_d = dram("q_parts", (SPLITS, D, N), BF16)
    ks_d = dram("k_parts", (SPLITS, D, N), BF16)

    class TileCopies:

        def __init__(self, eng, tag, copy, affine=None):
            self.eng, self.tag, self.copy, self.affine = eng, tag, copy, affine

        def weights(self, n, s):
            if isinstance(n, int) and n == FIRST_TILE[self.tag]:
                self.eng.wait_ge(sem(f"{self.tag}_experts_ready"), 1)
                self.eng.wait_ge(sem(f"{self.tag}_weights"), 16 * (1 + E + (self.tag == "m1")))
            width = EWB if self.tag == "m1" else EW
            e = self.eng.value_load(tile_expert[0:1, bass.ds(n, 1)], min_val=0, max_val=E - 1)
            self.copy(wcur[:, s, 0:width], wall[:, bass.ds(e, 1), 0:width].rearrange("p o w -> p (o w)")) \
                .then_inc(sem("tile_w_ready"), 1)

        def transposed(self, n, s):
            self.eng.wait_ge(sem("tile_xsT_in_psum"), n + 1)
            (self.affine or self.copy)(xsT[:, s, :], ps[:, 0, 0:P]).then_inc(sem("tile_xsT_ready"), 1)

        def results(self, n, s, turn):
            self.eng.wait_ge(sem("tile_ys_in_psum"), n + 1)
            if not (isinstance(n, int) and n < ER):
                self.eng.wait_ge(sem(f"tile_ys_stored{s}"), turn * 16)
            self.copy(ys[:, s, :], ps[:, 4 + s, 0:D]).then_inc(sem("tile_ys_ready"), 1)

    block = ctx.enter_context(nc.Block())

    @block.sync
    def _(sp):
        def load(dst, src, s):
            sp.dma_start(dst, src).then_inc(sem(s), 16)

        load(x_tok[:], a["L0_attn_token_embeddings"].rearrange("b (n p) d -> p (b n) d", p=P), "x_in")
        load(splat[:], a["L0_attn_splat_positions"], "splat_in")
        load(splatT[:], a["splat_positions_T"], "splat_in")
        load(splat_ls[:], a["L0_attn_splat_log_scales"].rearrange("(s o) -> s o", o=1), "splat_in")
        load(splat_amp[:], a["L0_attn_splat_amplitudes"].rearrange("(s o) -> s o", o=1), "splat_in")
        for name, t in sqd.items():
            load(t[:], a[name], "w_in")
        load(wqkv[:], a["L0_ffn_w_qkv"], "w_in")
        load(gate_w[:], a["L0_ffn_gate_w"], "w_in")
        for name, t in rows.items():
            load(t[:], a[name].partition_broadcast(P), "rows_in")
        for name, t in lncol.items():
            load(t[:], a[name].rearrange("(d o) -> d o", o=1), "lncol_in")
        load(gate_b[:], a["L0_ffn_gate_b"].partition_broadcast(P), "rows_in")
        load(wproj[:], a["L0_ffn_w_proj"], "w_in")

        sp.wait_ge(sem("zero_tok_ready"), 1)
        for tag in FIRST_TILE:
            load(xs_d[tag].rearrange("(k p) d -> p k d", p=P), zero_tok[:].unsqueeze(1).broadcast_to([P, MTILES, D]),
                 "slots_cleared")

        for n, dst in enumerate((qs_d, ks_d)):
            sp.wait_ge(sem("parts_ready"), NCH * (n + 1))
            load(dst.rearrange("s d t -> d s t"), split_hi, "parts_stored")

        def load_group(G, slot):
            b, g = G // NG, G % NG
            for src_d, dst in ((qs_d, Qs), (ks_d, Ks)):
                q_side = src_d is qs_d
                for h in range(HG):
                    v = src_d[:, bass.ds((g * HG + h) * DK, DK), bass.ds(b * T, T)]
                    for i in range(SPLITS):
                        if q_side:
                            s = v[i].unsqueeze(0).broadcast_to([SPLITS, DK, T])
                        else:
                            s = v
                        load(dst[i * SPLITS * DK:(i + 1) * SPLITS * DK, slot, h * T:(h + 1) * T], s,
                             f"stack_in{slot}")

        def store_max(G, slot):
            sp.wait_ge(sem("max_rows_ready"), G + 1)
            load(Qs[KQ:KX, slot, :], mxrow[:], f"maxrow_in{slot}")

        sp.wait_ge(sem("parts_stored"), 32)
        sp.wait_ge(sem("ksrows_one"), 1)
        for G in range(RING):
            load_group(G, G)
        store_max(0, 0)

        def group(G, slot, prefetch=True):
            store_max(G + 1, (slot + 1) % RING)
            if prefetch:
                sp.wait_ge(sem("scores_done"), (G + 1) * STEPS * 2)
                load_group(G + RING, slot)

        for G in range(GROUPS - 1):
            group(G, G % RING, prefetch=G + RING < GROUPS)

        def expert_weights(tag, w1_d, w2_d, b1_d=None):
            load(wall[:, :, 0:HID], w1_d.rearrange("e d f -> d e f"), f"{tag}_weights")
            for e in range(E):
                load(wall[:, e, HID:EW].rearrange("p (f d) -> p f d", d=D),
                     w2_d[e].rearrange("(f p) d -> p f d", p=P), f"{tag}_weights")
            if b1_d is not None:
                load(wall[:, :, EW:EWB], b1_d.rearrange("p (e f) -> p e f", f=FT), f"{tag}_weights")

        def expert_tiles(tag):
            n0 = FIRST_TILE[tag]

            def load_tile(n, s):
                if not (isinstance(n, int) and n < ER):
                    sp.wait_ge(sem("tile_xsT_in_psum"), n - ER + 1)
                load(xs[:, s, :], xs_d[tag][bass.ds((n - n0) * P, P), :], f"tile_xs_in{s}")

            def store_tile(n, s):
                sp.wait_ge(sem("tile_ys_ready"), n + 1)
                load(ys_d[tag][bass.ds((n - n0) * P, P), :], ys[:, s, :], f"tile_ys_stored{s}")

            sp.wait_ge(sem(f"{tag}_scattered"), 16 * NT)
            for n in range(ER):
                load_tile(n0 + n, n)
            with sp.Fori(n0 // ER, (n0 + MTILES) // ER - 1) as it:
                for s in range(ER):
                    load_tile(it * ER + (ER + s), s)
                    store_tile(it * ER + s, s)
            for n in range(MTILES - ER, MTILES):
                store_tile(n0 + n, n % ER)

        sp.wait_ge(sem("scores_done"), GROUPS * STEPS * 2)
        expert_weights("m0", a["L0_ffn_w1"], a["L0_ffn_w2"])
        expert_tiles("m0")

        for name, t in w1m.items():
            load(t[:], a[f"L1_{name}_T"], "w_l1")
        load(w_red[:], a["L1_ffn_w_red"], "w_l1")
        load(wg[:], a["L1_ffn_wg"], "w_l1")
        load(b2s[:], a["L1_ffn_b2"], "w_l1")
        expert_weights("m1", a["L1_ffn_w1"], a["L1_ffn_w2"], a["L1_b1_cols"])
        sp.wait_ge(sem("masks_ready"), 1)
        sp.wait_ge(sem("v1_tok_ready"), NCH)
        for b in range(B):
            load(v_pad[b, 0:W, :], zero_rows[0:W, :], "v_stored")
            load(v_pad[b, W:PADT, :].rearrange("(n p) d -> p n d", p=P), tmp_tok[:, b * MT:(b + 1) * MT, :],
                 "v_stored")
        sp.wait_ge(sem("v_stored"), 64)

        def window(n, b, blk, slot):
            if not (isinstance(n, int) and n < VRING):
                sp.wait_ge(sem("vdiag_ready"), n - VRING + 1)
            src = v_pad[b, bass.ds(blk * TB, WIN), :]
            load(vwin[:, slot, :], src.unsqueeze(0).broadcast_to([HG, WIN, D]), f"window{slot}")

        for n in range(VRING):
            window(n, n % B, n // B, n)
        with sp.Fori(1, BLOCKS // VRING) as it:
            for u in range(VRING):
                window(it * VRING + u, u % B, it * (VRING // B) + u // B, u)
        for n in range(BLOCKS - BLOCKS % VRING, BLOCKS):
            window(n, n % B, n // B, n % VRING)

        sp.wait_ge(sem("vdiag_ready"), BLOCKS)
        expert_tiles("m1")
        for c in range(NCH):
            sp.wait_ge(sem("final"), c + 1)
            load(out.rearrange("b (n p) d -> p (b n) d", p=P)[:, 4 * c:4 * c + 4], x_tok[:, 4 * c:4 * c + 4], "stored")
        sp.wait_ge(sem("stored"), 16 * NCH)

    @block.gpsimd
    def _(pool):
        st = Steps(pool, sem("pool_chain"))
        pool.memset(ident[:], 0.0)
        pool.memset(ident_bf[:], 0.0)
        pool.memset(eps[:], LN_EPS).then_inc(sem("eps_ready"), 1)
        pool.memset(ones[:], 1.0).then_inc(sem("ones_ready"), 1)
        pool.wait_ge(sem("ones_ready"), 1)
        for m in (ident, ident_bf):
            pool.affine_select(out=m[:], in_=m[:], compare_op=ALU.not_equal, fill=1.0, base=0,
                               pattern=[[-1, P]], channel_multiplier=1).then_inc(sem("ident_ready"), 1)
        chain(pool.memset(earlier[:], 1.0), st)
        pool.affine_select(out=earlier[:], in_=earlier[:], compare_op=ALU.is_ge, fill=0.0, base=-1,
                           pattern=[[1, P]], channel_multiplier=-1).then_inc(sem("earlier_ready"), 1)
        for k in range(MTILES):
            pool.memset(count[:, k:k + 1], float(k))
        for k in range(NT):
            pool.memset(tile_start[:, k:k + 1], float(P * k))
        pool.memset(zero_tok[:], 0.0).then_inc(sem("zero_tok_ready"), 1)

        def scatter(tag, src):
            pool.wait_ge(sem("slots_cleared"), 2 * 16)
            pool.wait_ge(sem(f"{tag}_slots_ready"), 1)
            for t in range(NT):
                pool.indirect_dma_start(
                    out=xs_d[tag][:, :], out_offset=bass.IndirectOffsetOnAxis(ap=tok_slot[tag][:, t:t + 1], axis=0),
                    in_=src[:, t, :], in_offset=None).then_inc(sem(f"{tag}_scattered"), 16)

        def gather(tag, dst):
            for s in range(ER):
                pool.wait_ge(sem(f"tile_ys_stored{s}"), 16 * ((FIRST_TILE[tag] + MTILES) // ER))
            for t in range(NT):
                pool.indirect_dma_start(
                    out=dst[:, t, :], out_offset=None, in_=ys_d[tag][:, :],
                    in_offset=bass.IndirectOffsetOnAxis(ap=tok_slot[tag][:, t:t + 1], axis=0)) \
                    .then_inc(sem(f"{tag}_gathered"), 16)

        pool.wait_ge(sem("xnT_ready"), NCH)
        for c in range(NCH):
            pool.tensor_tensor(xsqT[:, c * CH:(c + 1) * CH], xnT[:, c * CH:(c + 1) * CH],
                               xnT[:, c * CH:(c + 1) * CH], ALU.mult).then_inc(sem("xsq_ready"), 1)
        pool.wait_ge(sem("splat_done"), 1)
        pool.memset(Ks[64:P, :, :], 1.0).then_inc(sem("ksrows_one"), 1)
        pool.wait_ge(sem("ksrows_one"), 1)
        chain(pool.memset(Vg[:, :, :, :, DK:32], 1.0), st)

        def values(G, slot):
            if not (isinstance(G, int) and G < RING):
                pool.wait_ge(sem("pv_done"), (G - RING + 1) * STEPS)
            b, g = G // NG, G % NG
            src = Vtok[:, bass.ds(b * MT, MT), bass.ds(g * HG * DK, HG * DK)]
            pool.tensor_copy(Vg[:, slot, :, :, 0:DK], src.rearrange("p m (h d) -> p m h d", d=DK)) \
                .then_inc(sem("vg_ready"), 1)

        pool.wait_ge(sem("v_tok_ready"), 1)
        for G in range(GROUPS):
            values(G, G % RING)

        def keep(m, pattern, base, mult, op=ALU.is_ge, fill=0.0):
            chain(pool.affine_select(out=m, in_=m, compare_op=op, fill=fill, base=base, pattern=pattern,
                                     channel_multiplier=mult), st)

        chain(pool.memset(zero_rows[:], 0.0), st)
        chain(pool.memset(head_rows[:], 1.0), st)
        keep(head_rows[:], [[-DK, H]], 0, 1)
        keep(head_rows[:], [[DK, H]], DK - 1, -1)
        chain(pool.memset(quad_rows[:], 1.0), st)
        keep(quad_rows[:], [[-32, HG], [0, DK]], 0, 1)
        keep(quad_rows[:], [[32, HG], [0, DK]], 31, -1)
        chain(pool.memset(mask_keys[:], 0.0), st)
        keep(mask_keys[0:TB], [[0, HG], [1, WIN]], -1, -1, fill=BIG)
        keep(mask_keys[0:TB], [[0, HG], [-1, WIN]], W, 1, fill=BIG)
        chain(pool.memset(mask_keys[32:33], BIG), st)
        chain(pool.memset(mask_keys[64:65, :, 0:W], BIG), st)
        chain(pool.memset(mask_toks[:], 0.0), st)
        chain(pool.memset(mask_toks[32:33], 1.0), st)
        keep(mask_toks[32:33], [[-1, TB], [-1, W]], W - 2, 0)
        chain(pool.memset(mask_toks[64:65], 1.0), st)
        chain(pool.memset(tok_rows[:], 0.0), st)
        keep(tok_rows[:], [[0, P // TB], [-1, TB]], 0, 1, op=ALU.not_equal, fill=1.0)
        chain(pool.memset(mask_once[64:P], 0.0), st)
        chain(pool.memset(spread[:], 0.0), st)
        for part in range(2):
            keep(spread[:], [[-TB, NG], [-1, TB], [0, W]], -64 * part, 1, op=ALU.not_equal, fill=1.0)
        scatter("m0", tmp_tok)
        gather("m0", tmp_tok)
        pool.wait_ge(sem("msa_done"), 1)
        for t in (kT, kpT, vT):
            chain(pool.memset(t[:, :, 0:W], 0.0), st)
        pool.memset(zero_rows[:], 0.0).then_inc(sem("masks_ready"), 1)
        scatter("m1", xn_tok)

        def diagonals(n, b, blk, slot, turn):
            three = slot % WRING
            if not (isinstance(n, int) and n < WRING):
                pool.wait_ge(sem("win_scores"), n - 2)
            src = kpT[:, b, bass.ds(blk * TB, WIN)]
            pool.tensor_tensor(kdiag[:, three], src.unsqueeze(1).broadcast_to([P, H, WIN]),
                               head_rows[:].unsqueeze(2).broadcast_to([P, H, WIN]), ALU.mult) \
                .then_inc(sem("kdiag_ready"), 1)
            kw = kT[:, b, bass.ds(blk * TB + 1, TB + W - 1)]
            kw = bass.AP(kw.tensor, kw.offset, [list(kw.ap[0]), [1, TB], [1, W]])
            q = qT[:, bass.ds(blk * TB + b * T, TB)]
            pool.tensor_tensor(qk[:, three], q.unsqueeze(2).broadcast_to([P, TB, W]), kw, ALU.mult) \
                .then_inc(sem("qk_ready"), 1)
            if not (isinstance(n, int) and n < WRING):
                pool.wait_ge(sem("win_rv"), n - 2)
            pool.wait_ge(sem(f"window{slot}"), turn * 16)
            pool.tensor_tensor(vdiag[:, three],
                               vwin[:, slot].rearrange("p (g j d) -> p g j d", g=NG, j=HG),
                               quad_rows[:].unsqueeze(1).broadcast_to([P, NG, HG, DK]), ALU.mult) \
                .then_inc(sem("vdiag_ready"), 1)

        pool.wait_ge(sem("qkv1_ready"), 3 * NCH)
        for n in range(BODY):
            diagonals(n, n % B, n // B, n, 1)
        with pool.Fori(1, BLOCKS // BODY) as it:
            for u in range(BODY):
                diagonals(it * BODY + u, u % B, it * (BODY // B) + u // B, u, it + 1)
        for n in range(BLOCKS - BLOCKS % BODY, BLOCKS):
            diagonals(n, n % B, n // B, n % BODY, n // BODY + 1)
        gather("m1", Ytok1)

    @block.scalar
    def _(act):
        def evacuate(dst, after, ready, affine=None):
            kw = {} if affine is None else {"scale": lncol[affine + "_w"][:], "bias": lncol[affine + "_b"][:]}
            for c in range(NCH):
                act.wait_ge(sem(after), c + 1)
                act.activation(dst[:, c * CH:(c + 1) * CH], ps[:, c, :], ACT.Identity if affine else ACT.Copy,
                               **kw).then_inc(sem(ready), 1)

        def std(n):
            act.wait_ge(sem("ln_var"), n)
            act.activation(col[:, 4, :], col[:, 3, :], ACT.Sqrt, bias=eps[:], scale=1.0 / D) \
                .then_inc(sem("ln_std"), 1)

        act.wait_ge(sem("eps_ready"), 1)
        std(1)
        evacuate(xnT, "xnT_in_psum", "xnT_ready")
        act.wait_ge(sem("splat_in"), 64)
        act.activation(scol[:, 0:1], splat_ls[:], ACT.Exp).then_inc(sem("splat_scale"), 1)
        for c in range(NCH):
            act.wait_ge(sem("d2_ready"), c + 1)
            act.activation(gaussT[:, c * CH:(c + 1) * CH], gaussT[:, c * CH:(c + 1) * CH], ACT.Exp,
                           scale=scol[:, 3:4]).then_inc(sem("gauss_exp"), 1)
        for c in range(2):
            act.wait_ge(sem("gauss_in_psum"), c + 1)
            act.activation(gauss[:, 8 * c:8 * c + 8, :], ps[:, 4 + c, :].rearrange("p (n s) -> p n s", s=S),
                           ACT.Copy).then_inc(sem("gauss_ready"), 1)

        std(2)
        act.wait_ge(sem("lncol_in"), 4 * 16)
        evacuate(hT, "hT_in_psum", "hT_ready", "L0_ffn_ln1")
        for w in range(2):
            for c in range(NCH):
                n = w * NCH + c
                act.wait_ge(sem("qk_in_psum"), n + 1)
                if n == 0:
                    act.wait_ge(sem("splat_done"), 1)
                if w == 1 and c == 0:
                    act.wait_ge(sem("parts_stored"), 16)
                hi = split_hi[:, 0, c * CH:(c + 1) * CH]
                act.activation(hi, ps[:, n % 4, :], ACT.Copy).then_inc(sem("part_hi"), 1)
                act.wait_ge(sem("part_r1"), n + 1)
                act.activation(split_hi[:, 1, c * CH:(c + 1) * CH], split_r[:, n % 2, 0, :], ACT.Copy) \
                    .then_inc(sem("part_mid"), 1)
        def take_y(half):
            G = half // QH
            act.wait_ge(sem("pv_done"), (half + 1) * MT)
            b, g, col0 = G // NG, G % NG, (G // NG) * T + (half % QH) * CH
            act.activation(Yraw[:, g, col0:col0 + CH], ps[:, YB, :], ACT.Copy).then_inc(sem("y_taken"), 1)

        taken = ("scores_taken", "scores_taken", "y_taken", "v_tok_ready")
        for c in range(NCH):
            act.wait_ge(sem("v_in_psum"), c + 1)
            act.activation(Vtok[:, 4 * c:4 * c + 4, :], ps[:, 4 + c, :].rearrange("p (n d) -> p n d", d=D),
                           ACT.Copy).then_inc(sem(taken[c]), 1)

        for G in range(GROUPS):
            b, g = G // NG, G % NG
            for k in range(STEPS):
                n = G * STEPS + k
                for pair in range(2):
                    act.wait_ge(sem("scores_done"), n * 2 + pair + 1)
                    if n >= 2 and pair == 0:
                        act.wait_ge(sem("pv_done"), n - 1)
                    act.activation(probs[:, k % 2, 2 * pair:2 * pair + 2, :],
                                   ps[:, 2 * pair:2 * pair + 2, :], ACT.Exp, scale=SCALE) \
                        .then_inc(sem("scores_taken"), 1)
                if n and k % MT == 0:
                    take_y(n // MT - 1)
        take_y(GROUPS * QH - 1)

        for c in range(NCH):
            act.wait_ge(sem("yT_in_psum"), c + 1)
            act.activation(hT[:, c * CH:(c + 1) * CH], ps[:, 4 + c, :], ACT.Copy).then_inc(sem("yT_ready"), 1)

        std(3)
        evacuate(hT, "h2T_in_psum", "h2T_ready", "L0_ffn_ln2")

        def expert_gelu(tag, n, s, func, bias):
            act.wait_ge(sem("tile_h_in_psum"), n + 1)
            if bias:
                for f in range(FT):
                    last = act.activation(hid[:, s, f, :], ps[:, 1 + s, f * P:(f + 1) * P], func,
                                          bias=wcur[:, s, EW + f:EW + f + 1])
            else:
                last = act.activation(hid[:, s].rearrange("p f m -> p (f m)"), ps[:, 1 + s, :], func)
            last.then_inc(sem("tile_h_ready"), 1)

        def gelus(tag, func, copies=None, before_last=None):
            n0 = FIRST_TILE[tag]

            def step(n, s, turn, first=False, last=False):
                if copies and not last:
                    copies.transposed(n + 1, (s + 1) % ER)
                    copies.weights(n + 1, (s + 1) % ER)
                expert_gelu(tag, n, s, func, copies is not None)
                if copies and not first:
                    copies.results(n - 1, (s - 1) % ER, turn if s else turn - 1)

            if copies:
                copies.transposed(n0, 0)
                copies.weights(n0, 0)
            for n in range(n0, n0 + FIRST):
                step(n, n % ER, n // ER, first=n == n0)
            with act.Fori((n0 + FIRST) // ER, (n0 + MTILES - 2) // ER) as it:
                for u in range(FIRST % ER, FIRST % ER + ER):
                    step(it * ER + u, u % ER, it + u // ER)
            if before_last:
                before_last()
            for n in range(n0 + MTILES - 2, n0 + MTILES):
                step(n, n % ER, n // ER, last=n == n0 + MTILES - 1)
            if copies:
                copies.results(n0 + MTILES - 1, (MTILES - 1) % ER, (n0 + MTILES - 1) // ER)

        gelus("m0", ACT.Gelu_apprx_tanh)

        std(4)
        act.wait_ge(sem("wg_norm2"), 1)
        act.activation(wgs[:, 1:2], wgs[:, 0:1], ACT.Sqrt).then_inc(sem("wg_norm"), 1)
        evacuate(xnT, "xn1T_in_psum", "xn1T_ready")
        for w, dst in enumerate((qT, kT, kpT, vT)):
            for c in range(NCH):
                act.wait_ge(sem("qkv1_in_psum"), w * NCH + c + 1)
                if w == 0:
                    v = dst[:, c * CH:(c + 1) * CH]
                else:
                    v = dst[:, c // QH, W + (c % QH) * CH:W + (c % QH + 1) * CH]
                act.activation(v, ps[:, 4 + (w * NCH + c) % 4, :], ACT.Copy) \
                    .then_inc(sem("qkv1_ready" if w else "q1_ready"), 1)
        for c in range(NCH):
            act.wait_ge(sem("v1_in_psum"), c + 1)
            act.activation(tmp_tok[:, 4 * c:4 * c + 4, :], ps[:, c, :].rearrange("p (n d) -> p n d", d=D),
                           ACT.Copy).then_inc(sem("v1_tok_ready"), 1)
        for c in range(NCH):
            act.wait_ge(sem("red_in_psum"), c + 1)
            act.activation(redT[:, c * CH:(c + 1) * CH], ps[0:16, 4 + c, :], ACT.Copy).then_inc(sem("red_ready"), 1)
        act.wait_ge(sem("gate1_shifted"), 1)
        act.activation(route[:, 3], route[:, 0], ACT.Exp).then_inc(sem("gate1_exp"), 1)

        def window_exp(n, two, three):
            act.wait_ge(sem("win_shifted"), n + 1)
            if not (isinstance(n, int) and n < 2):
                act.wait_ge(sem("win_rv"), n - 1)
            act.activation(wprobs[:, two].rearrange("p g s j -> p (g s j)"),
                           ps[:, 2 * three:2 * three + 2, :].rearrange("p a n -> p (a n)"), ACT.Exp, scale=SCALE) \
                .then_inc(sem("win_exp"), 1)

        for n in range(PEEL):
            window_exp(n, n % 2, n % 3)
        with act.Fori(0, (BLOCKS - PEEL) // BODY) as it:
            for u in range(BODY):
                window_exp(it * BODY + (PEEL + u), u % 2, (PEEL + u) % 3)
        gelus("m1", ACT.Gelu, TileCopies(act, "m1", lambda o, i: act.activation(o, i, ACT.Copy)),
              before_last=lambda: std(5))

    @block.tensor
    def _(pe):
        def transpose_all(src, after, done):
            for t in range(NT):
                if t % 4 == 0:
                    pe.wait_ge(sem(after), t // 4 + 1)
                m = pe.transpose(ps[:, t // 4, (t % 4) * P:(t % 4 + 1) * P], src[:, t, :], ident[:])
                if t % 4 == 3:
                    m.then_inc(sem(done), 1)

        pe.wait_ge(sem("ident_ready"), 2)
        pe.wait_ge(sem("ones_ready"), 1)
        transpose_all(xn_tok, "xn_ready", "xnT_in_psum")
        pe.wait_ge(sem("splat_scale2"), 1)
        for c in range(NCH):
            cs = slice(c * CH, (c + 1) * CH)
            pe.wait_ge(sem("xnT_ready"), c + 1)
            pe.matmul(ps[0:S, 4 + c, :], splatT[:], xnT[:, cs], start=True, stop=False)
            pe.wait_ge(sem("xsq_ready"), c + 1)
            pe.matmul(ps[0:S, 4 + c, :], ones[:, 0:S], xsqT[:, cs], start=False, stop=True) \
                .then_inc(sem("d2_in_psum"), 1)
        for t in range(NT):
            if t % 4 == 0:
                pe.wait_ge(sem("gaussT_ready"), t // 4 + 1)
            if t % 8 == 0:
                pe.wait_ge(sem("d2_ready"), NCH)
            m = pe.transpose(ps[:, 4 + t // 8, (t % 8) * S:(t % 8 + 1) * S], gaussT[:, t * P:(t + 1) * P],
                             ident[0:S, 0:S])
            if t % 8 == 7:
                m.then_inc(sem("gauss_in_psum"), 1)
        pe.wait_ge(sem("xnT_ready"), NCH)
        for b in range(B):
            pe.wait_ge(sem("gauss_ready"), b + 1)
            for t in range(MT):
                n = b * MT + t
                pe.matmul(ps[:, b, 0:S], xn_tok[:, n, :], gauss[:, n, :], start=t == 0, stop=t == MT - 1)
            for t in range(MT):
                n = b * MT + t
                m = pe.matmul(ps[0:S, 2 + b, 0:1], gauss[:, n, :], ones[:, 0:1], start=t == 0, stop=t == MT - 1)
            m.then_inc(sem("xg_in_psum"), 1)
        pe.wait_ge(sem("w_in"), 5 * 16)
        for b in range(B):
            pe.wait_ge(sem("xg_ready"), b + 1)
            pe.matmul(ps[:, 4 + b, 0:S], sqd["L0_attn_Wv"][:], xg[:, b, :], start=True, stop=True) \
                .then_inc(sem("gv_in_psum"), 1)
        for b in range(B):
            pe.wait_ge(sem("gv_ready"), b + 1)
            pe.matmul(ps[0:S, 6 + b, 0:D], gvT[:, b, :], sqd["L0_attn_Wo"][:], start=True, stop=True) \
                .then_inc(sem("gvw_in_psum"), 1)
        pe.wait_ge(sem("gvw_ready"), B)
        for t in range(NT):
            pe.matmul(ps[:, 4, t:t + 1], gaussT[:, t * P:(t + 1) * P], gvw[:, t // MT, D:D + 1], start=True, stop=True)
        for t in range(NT):
            m = pe.matmul(ps[:, t // 4, (t % 4) * D:(t % 4 + 1) * D], gaussT[:, t * P:(t + 1) * P],
                          gvw[:, t // MT, 0:D], start=True, stop=True)
        m.then_inc(sem("splat_in_psum"), 1)

        pe.wait_ge(sem("splat_done"), 1)
        transpose_all(moe_tok, "h_ready", "hT_in_psum")
        pe.wait_ge(sem("hT_ready"), NCH)
        for w in range(2):
            for c in range(NCH):
                if w:
                    pe.wait_ge(sem("parts_ready"), c + 1)
                pe.matmul(ps[:, c, :], wqkv[:, w * D:(w + 1) * D], hT[:, c * CH:(c + 1) * CH],
                          start=True, stop=True).then_inc(sem("qk_in_psum"), 1)
        for t in range(NT):
            m = pe.matmul(ps[:, 4 + t // 4, (t % 4) * D:(t % 4 + 1) * D], hT[:, t * P:(t + 1) * P],
                          wqkv[:, 2 * D:3 * D], start=True, stop=True)
            if t % 4 == 3:
                m.then_inc(sem("v_in_psum"), 1)


        def max_unit(G, slot, u):
            h, q = u // MT, u % MT
            for half in range(2):
                i = 2 * u + half
                n = G * (UNITS * 2) + i
                if i >= MXN:
                    pe.wait_ge(sem("max_taken"), n - MXN + 1)
                elif not (isinstance(G, int) and G == 0):
                    pe.wait_ge(sem("max_taken"), n if i == 0 else n - MXN)
                if i == 2 and not (isinstance(G, int) and G == 0):
                    pe.wait_ge(sem("max_rows_ready"), G)
                pe.matmul(ps[:, MX + i % MXN, :], Qs[0:KQ, slot, h * T + q * P:h * T + (q + 1) * P],
                          Ks[0:KQ, slot, h * T + half * CH:h * T + (half + 1) * CH], start=True, stop=True) \
                    .then_inc(sem("max_scores"), 1)

        def max_rows(G):
            pe.wait_ge(sem("max_split"), G + 1)
            pe.transpose(ps[0:SPLITS * UNITS, MX + 2, 0:P // 2].bitcast(BF16),
                         mxs[:].rearrange("p s u -> p (s u)"), ident_bf[:]).then_inc(sem("max_rows_in_psum"), 1)

        def await_stack(G, slot, turn):
            pe.wait_ge(sem(f"stack_in{slot}"), (turn + 1) * (16 * 2 * HG * SPLITS))

        def group(G, slot, turn, more):
            def after(d):
                return (slot + d) % RING, turn + (slot + d) // RING

            pe.wait_ge(sem(f"maxrow_in{slot}"), (turn + 1) * 16)
            for k in range(STEPS + 1):
                n = G * STEPS + k
                half, m = k // MT, k % MT
                for pair in range(2):
                    if k < STEPS:
                        pe.wait_ge(sem("scores_taken"), n * 2 + pair + 1)
                        for h in (2 * pair, 2 * pair + 1):
                            mm = pe.matmul(ps[:, SC + h, :], Ks[0:KX, slot, h * T + m * P:h * T + (m + 1) * P],
                                           Qs[0:KX, slot, h * T + half * CH:h * T + (half + 1) * CH],
                                           start=True, stop=True)
                        mm.then_inc(sem("scores_done"), 1)
                        u = 2 * (k + AHEAD) + pair
                        if u < UNITS and more >= 1:
                            max_unit(G + 1, after(1)[0], u)
                        if u >= UNITS and more >= 2:
                            if u == UNITS:
                                await_stack(G + 2, *after(2))
                            max_unit(G + 2, after(2)[0], u - UNITS)
                if k == STEPS - AHEAD - 1 and more >= 1:
                    max_rows(G + 1)
                if k:
                    j = k - 1
                    pe.wait_ge(sem("scores_taken"), n * 2 + 2)
                    if j == 0:
                        pe.wait_ge(sem("vg_ready"), G + 1)
                    if j % MT == 0:
                        pe.wait_ge(sem("y_taken"), G * QH + (j // MT + 1))
                    for h in range(HG):
                        mm = pe.matmul(ps[32 * h:32 * h + 32, YB, :], Vg[:, slot, j % MT, h, :],
                                       probs[:, j % 2, h, :], start=j % MT == 0, stop=j % MT == MT - 1)
                    mm.then_inc(sem("pv_done"), 1)

        pe.wait_ge(sem("v_tok_ready"), 1)
        pe.wait_ge(sem("parts_ready"), 2 * NCH)
        await_stack(0, 0, 0)
        for u in range(UNITS):
            max_unit(0, 0, u)
        max_rows(0)
        await_stack(1, 1, 0)
        for u in range(2 * AHEAD):
            max_unit(1, 1, u)
        with pe.Fori(0, GROUPS // RING) as it:
            for slot in range(RING):
                group(it * RING + slot, slot, it, 2)
        for G in range(GROUPS // RING * RING, GROUPS):
            group(G, G % RING, G // RING, GROUPS - 1 - G)

        pe.wait_ge(sem("y_taken"), 1 + GROUPS * QH)
        pe.wait_ge(sem("scores_taken"), 2 + GROUPS * STEPS * 2)
        for t in range(NT):
            if t >= 4:
                pe.wait_ge(sem("quotients"), t - 3)
            for g in range(NG):
                m = pe.transpose(ps[:, t % 4, g * P:(g + 1) * P], Yraw[:, g, t * P:(t + 1) * P], ident[:])
            m.then_inc(sem("y_tok_in_psum"), 1)
        for t in range(NT):
            if t % 4 == 0:
                pe.wait_ge(sem("quotients"), t + 4)
            m = pe.transpose(ps[:, 4 + t // 4, (t % 4) * P:(t % 4 + 1) * P], tmp_tok[:, t, :], ident[:])
            if t % 4 == 3:
                m.then_inc(sem("yT_in_psum"), 1)
        for t in range(NT):
            if t % 4 == 0:
                pe.wait_ge(sem("yT_ready"), t // 4 + 1)
            m = pe.matmul(ps[:, t // 4, (t % 4) * D:(t % 4 + 1) * D], hT[:, t * P:(t + 1) * P], wproj[:],
                          start=True, stop=True)
            if t % 4 == 3:
                m.then_inc(sem("proj_in_psum"), 1)
        pe.wait_ge(sem("msa_done"), 1)

        transpose_all(tmp_tok, "h2_ready", "h2T_in_psum")
        pe.wait_ge(sem("h2T_ready"), NCH)
        for t in range(NT):
            m = pe.matmul(ps[:, 6, t * E:(t + 1) * E], hT[:, t * P:(t + 1) * P], gate_w[:], start=True, stop=True)
        m.then_inc(sem("gate_in_psum"), 1)

        def route_counts(tag, bank):
            pe.wait_ge(sem("earlier_ready"), 1)
            pe.wait_ge(sem(f"{tag}_chosen"), 1)
            pe.matmul(ps[:, bank, 0:NT * E], earlier[:], chosen[:].rearrange("p t e -> p (t e)"),
                      start=True, stop=False, skip_group_check=True)
            for t in range(NT):
                m = pe.matmul(ps[:, bank, (t + 1) * E:(NT + 1) * E], ones[:],
                              chosen[:, t, :].unsqueeze(1).broadcast_to([P, NT - t, E]),
                              start=False, stop=t == NT - 1, skip_group_check=True)
            m.then_inc(sem(f"{tag}_counts_in_psum"), 1)

        route_counts("m0", 7)

        def expert_tiles(tag, midway=None):
            n0 = FIRST_TILE[tag]

            def turned(n, s, turn):
                pe.wait_ge(sem(f"tile_xs_in{s}"), (turn + 1) * 16)
                if not (isinstance(n, int) and n == 0):
                    pe.wait_ge(sem("tile_xsT_ready"), n)
                pe.transpose(ps[:, 0, 0:P], xs[:, s, :], ident[:]).then_inc(sem("tile_xsT_in_psum"), 1)

            def hidden(n, s):
                pe.wait_ge(sem("tile_xsT_ready"), n + 1)
                pe.wait_ge(sem("tile_w_ready"), n + 1)
                for f in range(FT):
                    m = pe.matmul(ps[:, 1 + s, f * P:(f + 1) * P], wcur[:, s, f * P:(f + 1) * P], xsT[:, s, :],
                                  start=True, stop=True)
                m.then_inc(sem("tile_h_in_psum"), 1)

            def results(n, s):
                pe.wait_ge(sem("tile_h_ready"), n + 1)
                if not (isinstance(n, int) and n < ER):
                    pe.wait_ge(sem("tile_ys_ready"), n - ER + 1)
                for f in range(FT):
                    m = pe.matmul(ps[:, 4 + s, 0:D], hid[:, s, f, :], wcur[:, s, HID + f * D:HID + (f + 1) * D],
                                  start=f == 0, stop=f == FT - 1)
                m.then_inc(sem("tile_ys_in_psum"), 1)

            def step(n, s, turn, first=False, last=False):
                if not last:
                    turned(n + 1, (s + 1) % ER, turn + (s + 1) // ER)
                hidden(n, s)
                if not first:
                    results(n - 1, (s - 1) % ER)

            def loop(first, last):
                with pe.Fori((n0 + first) // ER, (n0 + last) // ER) as it:
                    for u in range(ER):
                        step(it * ER + (u + FIRST % ER), (u + FIRST) % ER, it + (u + FIRST % ER) // ER)

            turned(n0, 0, n0 // ER)
            for n in range(n0, n0 + FIRST):
                step(n, n % ER, n // ER, first=n == n0)
            if midway is None:
                loop(FIRST, MTILES - 2)
            else:
                loop(FIRST, FIRST + 3 * ER)
                midway()
                loop(FIRST + 3 * ER, MTILES - 2)
            for n in range(n0 + MTILES - 2, n0 + MTILES):
                step(n, n % ER, n // ER, last=n == n0 + MTILES - 1)
            results(n0 + MTILES - 1, (MTILES - 1) % ER)

        expert_tiles("m0")

        transpose_all(xn_tok, "xn1_ready", "xn1T_in_psum")
        pe.wait_ge(sem("w_l1"), 8 * 16)
        pe.wait_ge(sem("xn1T_ready"), NCH)
        for w, name in enumerate(("Wq", "Wk", "Wkp", "Wv")):
            for c in range(NCH):
                n = w * NCH + c
                if n >= 4:
                    if n - 4 < NCH:
                        pe.wait_ge(sem("q1_ready"), n - 3)
                    else:
                        pe.wait_ge(sem("qkv1_ready"), n - 3 - NCH)
                pe.matmul(ps[:, 4 + n % 4, :], w1m[name][:], xnT[:, c * CH:(c + 1) * CH],
                          start=True, stop=True).then_inc(sem("qkv1_in_psum"), 1)
        for t in range(NT):
            m = pe.matmul(ps[:, t // 4, (t % 4) * D:(t % 4 + 1) * D], xnT[:, t * P:(t + 1) * P],
                          w1m["Wv"][:], start=True, stop=True)
            if t % 4 == 3:
                m.then_inc(sem("v1_in_psum"), 1)
        pe.wait_ge(sem("qkv1_ready"), 3 * NCH)
        for c in range(NCH):
            pe.matmul(ps[0:16, 4 + c, :], w_red[:], xnT[:, c * CH:(c + 1) * CH], start=True, stop=True) \
                .then_inc(sem("red_in_psum"), 1)
        pe.wait_ge(sem("v1_tok_ready"), NCH)
        pe.wait_ge(sem("wgn_ready"), 1)
        pe.transpose(ps[0:16, 0, 0:E], wgn[:], ident[0:E, 0:E]).then_inc(sem("wgT_in_psum"), 1)
        pe.wait_ge(sem("wgT_ready"), 1)
        pe.wait_ge(sem("red_ready"), NCH)
        for t in range(NT):
            m = pe.matmul(ps[:, 1, t * E:(t + 1) * E], redT[:, t * P:(t + 1) * P], wgT[:], start=True, stop=True)
        m.then_inc(sem("gate1_in_psum"), 1)
        route_counts("m1", 7)
        pe.wait_ge(sem("onehot1_ready"), 1)
        for t in range(NT):
            m = pe.transpose(ps[0:E, 2 + t // 4, (t % 4) * P:(t % 4 + 1) * P], oh[:, t, :], ident[:])
            if t % 4 == 3:
                m.then_inc(sem("ohT_in_psum"), 1)
        pe.wait_ge(sem("ohT_ready"), NCH)
        for t in range(NT):
            m = pe.matmul(ps[:, 2 + t // 4, (t % 4) * D:(t % 4 + 1) * D], ohT[:, t * P:(t + 1) * P], b2s[:],
                          start=True, stop=True)
        m.then_inc(sem("b2_in_psum"), 1)
        pe.wait_ge(sem("b2_taken"), 1)

        pe.wait_ge(sem("masks_ready"), 1)
        pe.matmul(ps[:, 0, 0:P], tok_rows[:].rearrange("s q t -> s (q t)"),
                  mask_keys[0:TB].rearrange("p j c -> p (j c)"), start=True, stop=True) \
            .then_inc(sem("mask_in_psum"), 1)
        pe.wait_ge(sem("mask_taken"), 1)
        TB_, RL = 6, 7

        def scores(n, two, three, half, first):
            if half == 0:
                if not (isinstance(n, int) and n < 3):
                    pe.wait_ge(sem("win_exp"), n - 2)
                pe.wait_ge(sem("kdiag_ready"), n + 1)
                pe.wait_ge(sem("qk_ready"), n + 1)
            bank = 2 * three + half
            if first:
                m = mask_toks[:].rearrange("p s j -> p (s j)")
                pe.matmul(ps[:, bank, :], mask_keys[:].rearrange("p j c -> p (j c)"),
                          m.unsqueeze(1).broadcast_to([P, 2, TB * W]), start=True, stop=False,
                          skip_group_check=True)
            for g in (2 * half, 2 * half + 1):
                mm = pe.matmul(ps[:, bank, (g % 2) * TB * W:(g % 2 + 1) * TB * W],
                               kdiag[:, three, HG * g:HG * g + HG, :].rearrange("p j c -> p (j c)"),
                               qk[:, three].rearrange("p s j -> p (s j)"),
                               start=g % 2 == 0 and not first, stop=False, skip_group_check=True)
            if half:
                mm.then_inc(sem("win_scores"), 1)

        def turn_max(n, two):
            pe.wait_ge(sem("win_cmax"), n + 1)
            if not (isinstance(n, int) and n == 0):
                pe.wait_ge(sem("win_mparts"), n)
            pe.matmul(ps[:, TB_, 0:P], ident_bf[:], mask_seen[:], start=True, stop=False, skip_group_check=True)
            for part in range(2):
                mm = pe.matmul(ps[64 * part:64 * part + 64, TB_, 0:P], cmax[:, two], ident[:],
                               start=False, stop=True, skip_group_check=True)
            mm.then_inc(sem("win_max_in_psum"), 1)

        def shift(n, three):
            pe.wait_ge(sem("win_mparts"), n + 1)
            lhs = mparts[:].rearrange("p j c -> p (j c)")
            for g in range(NG):
                mm = pe.matmul(ps[:, 2 * three + g // 2, (g % 2) * TB * W:(g % 2 + 1) * TB * W], lhs,
                               spread[:, g].rearrange("p s j -> p (s j)"),
                               start=False, stop=g % 2 == 1, skip_group_check=True)
            mm.then_inc(sem("win_shifted"), 1)

        def value_products(n, two, three):
            pe.wait_ge(sem("win_exp"), n + 1)
            pe.wait_ge(sem("vdiag_ready"), n + 1)
            if not (isinstance(n, int) and n == 0):
                pe.wait_ge(sem("win_den_taken"), n)
            for part in range(2):
                for g in range(NG):
                    lhs = vdiag[:, three, g] if part == 0 else quad_rows[:]
                    mm = pe.matmul(ps[32 * g:32 * g + 32, RL, part * TB * W:(part + 1) * TB * W],
                                   lhs.rearrange("p j d -> p (j d)"),
                                   wprobs[:, two, g].rearrange("p s j -> p (s j)"), start=True, stop=True,
                                   skip_group_check=True)
            mm.then_inc(sem("win_rv"), 1)

        for n in range(PEEL):
            scores(n, n % 2, n, 0, True)
            if n:
                turn_max(n - 1, (n - 1) % 2)
            scores(n, n % 2, n, 1, True)
            if n:
                shift(n - 1, n - 1)
        with pe.Fori(0, (BLOCKS - PEEL) // BODY) as it:
            for u in range(BODY):
                n = it * BODY + (PEEL + u)
                scores(n, u % 2, (PEEL + u) % 3, 0, False)
                turn_max(it * BODY + (PEEL + u - 1), (u - 1) % 2)
                scores(n, u % 2, (PEEL + u) % 3, 1, False)
                shift(it * BODY + (PEEL + u - 1), (PEEL + u - 1) % 3)
                value_products(it * BODY + (PEEL + u - 2), u % 2, (PEEL + u - 2) % 3)
        turn_max(BLOCKS - 1, (BLOCKS - 1) % 2)
        shift(BLOCKS - 1, (BLOCKS - 1) % 3)
        value_products(BLOCKS - 2, 0, (BLOCKS - 2) % 3)
        value_products(BLOCKS - 1, 1, (BLOCKS - 1) % 3)

        def project():
            pe.wait_ge(sem("zT_ready"), 1)
            for c in range(NCH):
                if c:
                    pe.wait_ge(sem("wo_taken"), c)
                for t in range(4 * c, 4 * c + 4):
                    m = pe.matmul(ps[:, 7, (t % 4) * D:(t % 4 + 1) * D], zT[:, t * P:(t + 1) * P], w1m["Wo"][:],
                                  start=True, stop=True)
                m.then_inc(sem("wo_in_psum"), 1)

        expert_tiles("m1", midway=project)

    @block.vector
    def _(dve):
        st = Steps(dve, sem("dve_chain"))

        def bc(v, n):
            return v.unsqueeze(2).broadcast_to([P, NT, n])

        def row(v):
            return v.unsqueeze(1).broadcast_to([P, NT, D])

        def layernorm(dst, src, n, done, chunk=None):
            for t in range(NT):
                if chunk and t % 4 == 0:
                    chunk(t // 4)
                last = dve.bn_stats(stats[:, t, :], src[:, t, :])
            chain(last, st)
            mean0, m2_0, mean1, m2_1 = (stats[:, :, i] for i in (1, 2, 4, 5))
            dve.tensor_tensor(col[:, 0, :], mean0, mean1, ALU.add)
            dve.tensor_tensor(col[:, 1, :], mean0, mean1, ALU.subtract)
            chain(dve.tensor_tensor(col[:, 2, :], m2_0, m2_1, ALU.add), st)
            dve.tensor_scalar(col[:, 0, :], col[:, 0, :], -0.5, None, ALU.mult)
            chain(dve.tensor_tensor(col[:, 1, :], col[:, 1, :], col[:, 1, :], ALU.mult), st)
            dve.scalar_tensor_tensor(col[:, 3, :], col[:, 1, :], D / 4.0, col[:, 2, :], ALU.mult, ALU.add) \
                .then_inc(sem("ln_var"), 1)
            dve.wait_ge(sem("ln_std"), n)
            chain(dve.reciprocal(col[:, 3, :], col[:, 4, :]), st)
            for t in range(NT):
                last = dve.tensor_scalar(dst[:, t, :], src[:, t, :], col[:, 0, t:t + 1], col[:, 3, t:t + 1],
                                         ALU.add, ALU.mult)
                if t % 4 == 3:
                    last.then_inc(sem(done), 1)
            dve.wait_ge(sem(done), NCH)

        dve.wait_ge(sem("x_in"), 16)
        layernorm(xn_tok, x_tok, 1, "xn_ready")

        dve.wait_ge(sem("splat_in"), 64)
        chain(dve.tensor_tensor(tmp_tok[0:S, 0, :], splat[:], splat[:], ALU.mult), st)
        chain(dve.tensor_reduce(scol[:, 4:5], tmp_tok[0:S, 0, :], X, ALU.add), st)
        chain(dve.tensor_scalar(splatT[:], splatT[:], -2.0, None, ALU.mult), st)
        dve.wait_ge(sem("splat_scale"), 1)
        chain(dve.tensor_tensor(scol[:, 1:2], scol[:, 0:1], scol[:, 0:1], ALU.mult), st)
        chain(dve.reciprocal(scol[:, 2:3], scol[:, 1:2]), st)
        dve.tensor_scalar(scol[:, 3:4], scol[:, 2:3], -0.5, None, ALU.mult).then_inc(sem("splat_scale2"), 1)
        dve.wait_ge(sem("splat_scale2"), 1)
        for c in range(NCH):
            dve.wait_ge(sem("d2_in_psum"), c + 1)
            dve.tensor_scalar(gaussT[:, c * CH:(c + 1) * CH], ps[0:S, 4 + c, :], scol[:, 4:5], 0.0,
                              ALU.add, ALU.max).then_inc(sem("d2_ready"), 1)
        for c in range(NCH):
            dve.wait_ge(sem("gauss_exp"), c + 1)
            dve.tensor_scalar(gaussT[:, c * CH:(c + 1) * CH], gaussT[:, c * CH:(c + 1) * CH], splat_amp[:], None,
                              ALU.mult).then_inc(sem("gaussT_ready"), 1)
        for b in range(B):
            dve.wait_ge(sem("xg_in_psum"), b + 1)
            dve.tensor_copy(gvw[:, b, D:D + 1], ps[0:S, 2 + b, 0:1])
            dve.tensor_copy(xg[:, b, :], ps[:, b, 0:S]).then_inc(sem("xg_ready"), 1)
        for b in range(B):
            dve.wait_ge(sem("gv_in_psum"), b + 1)
            dve.tensor_copy(gvT[:, b, :], ps[:, 4 + b, 0:S]).then_inc(sem("gv_ready"), 1)
        for b in range(B):
            dve.wait_ge(sem("gvw_in_psum"), b + 1)
            dve.tensor_copy(gvw[:, b, 0:D], ps[0:S, 6 + b, 0:D]).then_inc(sem("gvw_ready"), 1)
        dve.wait_ge(sem("splat_in_psum"), 1)
        chain(dve.tensor_scalar(col[:, 4, :], ps[:, 4, 0:NT], SPLAT_EPS, None, ALU.add), st)
        chain(dve.reciprocal(col[:, 5, :], col[:, 4, :]), st)
        chain(dve.tensor_tensor(tmp_tok[:], ps[:, 0:4, :].rearrange("p c (t d) -> p (c t) d", d=D),
                                bc(col[:, 5, :], D), ALU.mult), st)
        dve.tensor_tensor(x_tok[:], x_tok[:], tmp_tok[:], ALU.add).then_inc(sem("splat_done"), 1)
        dve.wait_ge(sem("splat_done"), 1)

        dve.wait_ge(sem("rows_in"), 3 * 16)
        layernorm(moe_tok, xn_tok, 2, "h_ready")
        for w in range(2):
            for c in range(NCH):
                n = w * NCH + c
                r1, r2 = split_r[:, n % 2, 0, :], split_r[:, n % 2, 1, :]
                dve.wait_ge(sem("part_hi"), n + 1)
                dve.tensor_tensor(r1, ps[:, n % 4, :], split_hi[:, 0, c * CH:(c + 1) * CH], ALU.subtract) \
                    .then_inc(sem("part_r1"), 1)
                dve.wait_ge(sem("part_mid"), n + 1)
                dve.tensor_tensor(split_hi[:, 2, c * CH:(c + 1) * CH], r1, split_hi[:, 1, c * CH:(c + 1) * CH],
                                  ALU.subtract).then_inc(sem("parts_ready"), 1)

        def max_unit(G, u):
            for i in (2 * u, 2 * u + 1):
                dve.wait_ge(sem("max_scores"), G * (UNITS * 2) + (i + 1))
                dve.tensor_reduce(mxh[:, u, i % 2:i % 2 + 1], ps[:, MX + i % MXN, :], X, ALU.max) \
                    .then_inc(sem("max_taken"), 1)

        def max_rows(G, before=None):
            dve.wait_ge(sem("max_taken"), (G + 1) * (UNITS * 2))
            chain(dve.tensor_reduce(nmx[:], mxh[:], X, ALU.max, negate=True), st)
            chain(dve.tensor_copy(mxs[:, 0, :], nmx[:]), st)
            chain(dve.tensor_tensor(mxr[:], nmx[:], mxs[:, 0, :], ALU.subtract), st)
            chain(dve.tensor_copy(mxs[:, 1, :], mxr[:]), st)
            dve.tensor_tensor(mxs[:, 2, :], mxr[:], mxs[:, 1, :], ALU.subtract).then_inc(sem("max_split"), 1)
            dve.wait_ge(sem("max_rows_in_psum"), G + 1)
            if before is not None:
                slot, turn = before
                dve.wait_ge(sem(f"maxrow_in{slot}"), (turn + 1) * 16)
            dve.tensor_copy(mxrow[:], ps[0:SPLITS * UNITS, MX + 2, 0:P // 2].bitcast(BF16)) \
                .then_inc(sem("max_rows_ready"), 1)

        def group_maxima(G, slot, turn, more):
            for u in range(2 * AHEAD, UNITS):
                max_unit(G + 1, u)
            max_rows(G + 1, (slot, turn))
            if more >= 2:
                for u in range(2 * AHEAD):
                    max_unit(G + 2, u)

        for u in range(UNITS):
            max_unit(0, u)
        max_rows(0)
        for u in range(2 * AHEAD):
            max_unit(1, u)
        with dve.Fori(0, GROUPS // RING) as it:
            st.enter(it, 4 * RING)
            for slot in range(RING):
                group_maxima(it * RING + slot, slot, it, 2)
        st.leave(GROUPS // RING)
        for G in range(GROUPS // RING * RING, GROUPS - 1):
            group_maxima(G, G % RING, G // RING, GROUPS - 1 - G)

        for t in range(NT):
            dve.wait_ge(sem("y_tok_in_psum"), t + 1)
            v = ps[:, t % 4, :].rearrange("p (h r) -> p h r", r=32)
            chain(dve.reciprocal(rden[:, t % 2], v[:, :, DK:DK + 1]), st)
            dve.tensor_tensor(tmp_tok[:, t, :].rearrange("p (h d) -> p h d", d=DK), v[:, :, 0:DK],
                              rden[:, t % 2].broadcast_to([P, H, DK]), ALU.mult).then_inc(sem("quotients"), 1)
        for c in range(NCH):
            dve.wait_ge(sem("proj_in_psum"), c + 1)
            last = dve.tensor_tensor(moe_tok[:, 4 * c:4 * c + 4, :],
                                     ps[:, c, :].rearrange("p (t d) -> p t d", d=D),
                                     xn_tok[:, 4 * c:4 * c + 4, :], ALU.add)
        last.then_inc(sem("msa_done"), 1)
        dve.wait_ge(sem("msa_done"), 1)

        layernorm(tmp_tok, moe_tok, 3, "h2_ready")

        def ebc(v):
            return v.unsqueeze(2).broadcast_to([P, NT, E])

        def first_max(logits, dst, done):
            chain(dve.tensor_reduce(col[:, 4, :], logits, X, ALU.max), st)
            chain(dve.tensor_tensor(route[:, 1], logits, ebc(col[:, 4, :]), ALU.is_equal), st)
            for e in range(E):
                last = dve.memset(route[:, 2, :, e:e + 1], float(E - e))
            chain(last, st)
            chain(dve.tensor_tensor(route[:, 1], route[:, 1], route[:, 2], ALU.mult), st)
            chain(dve.tensor_reduce(col[:, 5, :], route[:, 1], X, ALU.max), st)
            dve.tensor_tensor(dst, route[:, 1], ebc(col[:, 5, :]), ALU.is_equal).then_inc(sem(done), 1)
            dve.wait_ge(sem(done), 1)

        def route_slots(tag):
            dve.wait_ge(sem(f"{tag}_counts_in_psum"), 1)
            rank = ps[:, 7, 0:NT * E].rearrange("p (t e) -> p t e", e=E)
            total = ps[:, 7, NT * E:(NT + 1) * E]
            chain(dve.tensor_tensor(filled[:], total.unsqueeze(2).broadcast_to([P, E, NT]),
                                    tile_start[:].unsqueeze(1).broadcast_to([P, E, NT]), ALU.is_gt), st)
            chain(dve.tensor_reduce(tiles_to[:, 0], filled[:], X, ALU.add), st)
            for i in range(3):
                by = 1 << i
                dve.tensor_copy(tiles_to[:, i + 1, 0:by], tiles_to[:, i, 0:by])
                chain(dve.tensor_tensor(tiles_to[:, i + 1, by:E], tiles_to[:, i, by:E], tiles_to[:, i, 0:E - by],
                                        ALU.add), st)
            chain(dve.tensor_tensor(first_slot[:], tiles_to[:, 3], tiles_to[:, 0], ALU.subtract), st)
            chain(dve.tensor_scalar(first_slot[:], first_slot[:], float(P), None, ALU.mult), st)
            chain(dve.tensor_tensor(route[:, 1], rank, first_slot[:].unsqueeze(1).broadcast_to([P, NT, E]),
                                    ALU.add), st)
            chain(dve.tensor_tensor(route[:, 1], route[:, 1], chosen[:], ALU.mult), st)
            chain(dve.tensor_reduce(slot_f[:], route[:, 1], X, ALU.add), st)
            dve.tensor_copy(tok_slot[tag][:], slot_f[:]).then_inc(sem(f"{tag}_slots_ready"), 1)
            n0 = FIRST_TILE[tag]
            chain(dve.tensor_tensor(ended[:], tiles_to[:, 3].unsqueeze(1).broadcast_to([P, MTILES, E]),
                                    count[:].unsqueeze(2).broadcast_to([P, MTILES, E]), ALU.is_le), st)
            chain(dve.tensor_reduce(te_f[:], ended[:], X, ALU.add), st)
            dve.tensor_scalar(tile_expert[:, n0:n0 + MTILES], te_f[:], float(E - 1), None, ALU.min) \
                .then_inc(sem(f"{tag}_experts_ready"), 1)

        dve.wait_ge(sem("gate_in_psum"), 1)
        chain(dve.tensor_tensor(route[:, 0], ps[:, 6, 0:NT * E].rearrange("p (t e) -> p t e", e=E),
                                gate_b[:].unsqueeze(1).broadcast_to([P, NT, E]), ALU.add), st)
        first_max(route[:, 0], chosen[:], "m0_chosen")
        dve.wait_ge(sem("zero_tok_ready"), 1)
        route_slots("m0")
        chain(dve.tensor_tensor(x_tok[:], x_tok[:], moe_tok[:], ALU.add), st)
        def m0_copies():
            n0 = FIRST_TILE["m0"]
            w, b = lncol["L0_ffn_ln2_w"], lncol["L0_ffn_ln2_b"]
            copies = TileCopies(dve, "m0", lambda o, i: dve.tensor_scalar(o, i, 1.0, None, ALU.mult),
                                affine=lambda o, i: dve.tensor_scalar(o, i, w[:], b[:], ALU.mult, ALU.add))

            def step(n, s, turn, first=False, last=False):
                if not last:
                    copies.transposed(n + 1, (s + 1) % ER)
                    copies.weights(n + 1, (s + 1) % ER)
                if not first:
                    copies.results(n - 1, (s - 1) % ER, turn if s else turn - 1)

            copies.transposed(n0, 0)
            copies.weights(n0, 0)
            for n in range(n0, n0 + FIRST):
                step(n, n % ER, n // ER, first=n == n0)
            with dve.Fori((n0 + FIRST) // ER, (n0 + MTILES - 2) // ER) as it:
                for u in range(FIRST % ER, FIRST % ER + ER):
                    step(it * ER + u, u % ER, it + u // ER)
            for n in range(n0 + MTILES - 2, n0 + MTILES):
                step(n, n % ER, n // ER, last=n == n0 + MTILES - 1)
            copies.results(n0 + MTILES - 1, (MTILES - 1) % ER, (n0 + MTILES - 1) // ER)

        m0_copies()

        def gathered0(c):
            v = slice(4 * c, 4 * c + 4)
            dve.wait_ge(sem("m0_gathered"), NT * 16)
            chain(dve.tensor_tensor(x_tok[:, v, :], x_tok[:, v, :], tmp_tok[:, v, :], ALU.add), st)

        dve.wait_ge(sem("w_l1"), 8 * 16)
        chain(dve.tensor_tensor(wgn[:], wg[:], wg[:], ALU.mult), st)
        dve.tensor_reduce(wgs[:, 0:1], wgn[:], X, ALU.add).then_inc(sem("wg_norm2"), 1)
        layernorm(xn_tok, x_tok, 4, "xn1_ready", chunk=gathered0)
        dve.wait_ge(sem("wg_norm"), 1)
        chain(dve.tensor_scalar(wgs[:, 2:3], wgs[:, 1:2], 1e-4, None, ALU.max), st)
        chain(dve.reciprocal(wgs[:, 3:4], wgs[:, 2:3]), st)
        dve.tensor_scalar(wgn[:], wg[:], wgs[:, 3:4], None, ALU.mult).then_inc(sem("wgn_ready"), 1)
        dve.wait_ge(sem("wgT_in_psum"), 1)
        dve.tensor_copy(wgT[:], ps[0:16, 0, 0:E]).then_inc(sem("wgT_ready"), 1)
        dve.wait_ge(sem("gate1_in_psum"), 1)
        lg = ps[:, 1, 0:NT * E].rearrange("p (t e) -> p t e", e=E)
        chain(dve.tensor_reduce(col[:, 4, :], lg, X, ALU.max), st)
        dve.tensor_tensor(route[:, 0], lg, ebc(col[:, 4, :]), ALU.subtract).then_inc(sem("gate1_shifted"), 1)
        dve.wait_ge(sem("gate1_exp"), 1)
        chain(dve.tensor_reduce(col[:, 6, :], route[:, 3], X, ALU.add), st)
        chain(dve.reciprocal(col[:, 7, :], col[:, 6, :]), st)
        chain(dve.tensor_tensor(route[:, 3], route[:, 3], ebc(col[:, 7, :]), ALU.mult), st)
        first_max(route[:, 3], chosen[:], "m1_chosen")
        dve.tensor_reduce(score[:], route[:, 3], X, ALU.max)
        dve.tensor_tensor(oh[:], chosen[:], route[:, 3], ALU.mult).then_inc(sem("onehot1_ready"), 1)
        route_slots("m1")
        for c in range(NCH):
            dve.wait_ge(sem("ohT_in_psum"), c + 1)
            dve.tensor_copy(ohT[:, c * CH:(c + 1) * CH], ps[0:E, 2 + c, :]).then_inc(sem("ohT_ready"), 1)
        dve.wait_ge(sem("b2_in_psum"), 1)
        dve.tensor_copy(moe_tok[:], ps[:, 2:6, :].rearrange("p c (t d) -> p (c t) d", d=D)) \
            .then_inc(sem("b2_taken"), 1)

        dve.wait_ge(sem("mask_in_psum"), 1)
        dve.tensor_copy(mask_seen[:], ps[:, 0, 0:P])
        dve.tensor_copy(mask_once[0:64], ps[0:64, 0, 0:P]).then_inc(sem("mask_taken"), 1)

        def key_max(n, two, three):
            dve.wait_ge(sem("win_scores"), n + 1)
            if not (isinstance(n, int) and n < 2):
                dve.wait_ge(sem("win_max_in_psum"), n - 1)
            dve.tensor_reduce(cmax[:, two].rearrange("p (g s) -> p g s", s=TB),
                              ps[:, 2 * three:2 * three + 2, :].rearrange("p a (g s j) -> p (a g) s j", s=TB, j=W),
                              X, ALU.max).then_inc(sem("win_cmax"), 1)

        def max_parts(n, per=None):
            dve.wait_ge(sem("win_max_in_psum"), n + 1)
            if not (isinstance(n, int) and n == 0):
                dve.wait_ge(sem("win_shifted"), n)
            chain(dve.tensor_reduce(nM[:], ps[:, 6, 0:P].rearrange("p (j c) -> p j c", c=WIN), X, ALU.max,
                                    negate=True), st)
            wide = nM[:].unsqueeze(2).broadcast_to([P, HG, WIN])
            chain(dve.tensor_tensor(mparts[:], mask_once[:].rearrange("p (j c) -> p j c", c=WIN), wide, ALU.add), st)
            dve.tensor_tensor(mparts[64:P], wide[64:P], mparts[64:P], ALU.subtract) \
                .then_inc(sem("win_mparts"), 1)

        def first_key_sum(n, b, blk, two):
            dve.wait_ge(sem("win_rv"), n + 1)
            vw = vT[:, b, bass.ds(blk * TB + 1, TB + W - 1)]
            vw = bass.AP(vw.tensor, vw.offset, [list(vw.ap[0]), [1, TB], [1, W]])
            r = ps[:, 7, 0:TB * W].rearrange("p (s j) -> p s j", j=W)
            den = ps[:, 7, TB * W:2 * TB * W].rearrange("p (s j) -> p s j", j=W)
            chain(dve.tensor_tensor(rv[:, two], r, vw, ALU.mult), st)
            dve.tensor_reduce(denT[:, bass.ds(blk * TB + b * T, TB)], den, X, ALU.add) \
                .then_inc(sem("win_den_taken"), 1)
            dve.tensor_reduce(zT[:, bass.ds(blk * TB + b * T, TB)], rv[:, two], X, ALU.add) \
                .then_inc(sem("win_z"), 1)

        for n in range(PEEL):
            if n:
                max_parts(n - 1)
            key_max(n, n % 2, n % 3)
        with dve.Fori(0, (BLOCKS - PEEL) // BODY) as it:
            st.enter(it, 3 * BODY)
            for u in range(BODY):
                max_parts(it * BODY + (PEEL + u - 1))
                key_max(it * BODY + (PEEL + u), u % 2, (PEEL + u) % 3)
                first_key_sum(it * BODY + (PEEL + u - 2), u % B, it * (BODY // B) + (PEEL + u - 2) // B, u % 2)
        st.leave((BLOCKS - PEEL) // BODY)
        max_parts(BLOCKS - 1)
        first_key_sum(BLOCKS - 2, 0, NB - 1, 0)
        first_key_sum(BLOCKS - 1, 1, NB - 1, 1)
        dve.wait_ge(sem("win_z"), BLOCKS)
        dve.wait_ge(sem("win_den_taken"), BLOCKS)
        chain(dve.reciprocal(denT[:], denT[:]), st)
        dve.tensor_tensor(zT[:], zT[:], denT[:], ALU.mult).then_inc(sem("zT_ready"), 1)
        for c in range(NCH):
            v = slice(4 * c, 4 * c + 4)
            dve.wait_ge(sem("wo_in_psum"), c + 1)
            dve.tensor_tensor(tmp_tok[:, v, :], ps[:, 7, :].rearrange("p (t d) -> p t d", d=D), xn_tok[:, v, :],
                              ALU.add).then_inc(sem("wo_taken"), 1)
        dve.wait_ge(sem("wo_taken"), NCH)
        dve.wait_ge(sem("m1_scattered"), 16 * NT)
        layernorm(xn_tok, tmp_tok, 5, "attn1_done")
        chain(dve.tensor_tensor(xn_tok[:], xn_tok[:], row(rows["L1_attn_gamma"][:]), ALU.mult), st)
        chain(dve.tensor_tensor(xn_tok[:], xn_tok[:], row(rows["L1_attn_beta"][:]), ALU.add), st)
        chain(dve.tensor_tensor(x_tok[:], x_tok[:], xn_tok[:], ALU.add), st)
        chain(dve.tensor_tensor(x_tok[:], x_tok[:], moe_tok[:], ALU.add), st)
        dve.wait_ge(sem("m1_gathered"), NT * 16)
        for c in range(NCH):
            for t in range(4 * c, 4 * c + 4):
                last = dve.scalar_tensor_tensor(x_tok[:, t, :], Ytok1[:, t, :], score[:, t:t + 1], x_tok[:, t, :],
                                                ALU.mult, ALU.add)
            last.then_inc(sem("final"), 1)


_INS = ["L0_attn_token_embeddings", "L0_attn_splat_positions", "L0_attn_splat_log_scales",
        "L0_attn_splat_amplitudes", "L0_attn_Wv", "L0_attn_Wo", "L0_ffn_ln1_w", "L0_ffn_ln1_b",
        "L0_ffn_w_qkv", "L0_ffn_w_proj", "L0_ffn_ln2_w", "L0_ffn_ln2_b", "L0_ffn_gate_w", "L0_ffn_gate_b",
        "L0_ffn_w1", "L0_ffn_w2", "L1_attn_gamma", "L1_attn_beta", "L1_ffn_w_red", "L1_ffn_wg",
        "L1_ffn_w1", "L1_ffn_w2", "L1_ffn_b2"]


def laid_out(inputs):
    import numpy as np
    got = {name: np.ascontiguousarray(inputs[name]) for name in _INS}
    got["splat_positions_T"] = np.ascontiguousarray(np.asarray(inputs["L0_attn_splat_positions"]).T)
    for name in ("Wq", "Wk", "Wv", "Wkp", "Wo"):
        got[f"L1_{name}_T"] = np.ascontiguousarray(np.asarray(inputs[f"L1_attn_{name}"]).T)
    b1 = np.asarray(inputs["L1_ffn_b1"]).reshape(E, FT, P)
    got["L1_b1_cols"] = np.ascontiguousarray(b1.transpose(2, 0, 1).reshape(P, E * FT))
    return got


def kernel(**inputs):
    import concourse.bacc as bacc
    from concourse.bass_utils import run_bass_kernel_spmd

    nc = bacc.Bacc("TRN2", target_bir_lowering=False, num_devices=1)
    arrays, aps = {}, {}
    for name, v in laid_out(inputs).items():
        arrays[f"in_{name}"] = v
        aps[name] = nc.dram_tensor(f"in_{name}", v.shape, mybir.dt.from_np(v.dtype), kind="ExternalInput").ap()
    out = nc.dram_tensor("out_x", (B, T, D), F32, kind="ExternalOutput").ap()
    two_layers(nc, aps, out)
    r = run_bass_kernel_spmd(nc, [arrays], core_ids=[0])
    return r.results[0]["out_x"]
```

```python
from contextlib import ExitStack

import concourse.bass as bass
from concourse import mybir

F32 = mybir.dt.float32
BF16 = mybir.dt.bfloat16
I32 = mybir.dt.int32
ALU = mybir.AluOpType
ACT = mybir.ActivationFunctionType
X = mybir.AxisListType.X

P = 128
D = 128
B, T = 2, 1024
N = B * T
NT = N // P
CH = 512
NCH = N // CH
H, DK = 16, 8
S = 64
E = 8
HID = 512
FT = HID // P
LN_EPS = 1e-5
SPLAT_EPS = 1e-8
SCALE = float(DK) ** -0.5

HG = 4
NG = H // HG
GROUPS = B * NG
SPLITS = 3
KQ = SPLITS * SPLITS * DK
KX = KQ + SPLITS
RING = 3
MT = T // P
QH = T // CH
STEPS = QH * MT
UNITS = HG * MT

MTILES = NT + E
ER = 3
DI = D + 1
XR = 2 * ER
FIRST_TILE = {"m0": 0, "m1": MTILES}
LOOP_FROM = {"m0": 4, "m1": 10}
EW = HID + FT * D
EWB = EW + FT

W = 16
TB = 16
WIN = W + TB
NB = T // TB
PADT = T + W
ARENA = 27648
MOE0 = E * EWB
SC, MX, MXN, YB = 0, 4, 3, 7
AHEAD = 3
BIG = -1.0e30
PEEL, BODY, VRING = 2, 6, 6
WRING = 3
BLOCKS = B * NB


def chain(ins, steps):
    ins.then_inc(steps.sem, 1)
    steps.n += 1
    steps.eng.wait_ge(steps.sem, steps.base() + steps.n)


class Steps:

    def __init__(self, eng, sem):
        self.eng, self.sem, self.n, self.loop, self.per = eng, sem, 0, None, 0

    def base(self):
        return 0 if self.loop is None else self.loop * self.per

    def enter(self, i, per):
        self.loop, self.per, self.start = i, per, self.n

    def leave(self, times):
        assert self.n - self.start == self.per, (self.n - self.start, self.per)
        self.n += (times - 1) * self.per
        self.loop = None


def tile_loop(eng, step, tag):
    lo, hi = FIRST_TILE[tag] + LOOP_FROM[tag], FIRST_TILE[tag] + MTILES - 2
    assert (hi - lo) % XR == 0
    with eng.Fori(lo // XR, lo // XR + (hi - lo) // XR) as turn:
        for u in range(lo % XR, lo % XR + XR):
            step(turn, u)


def two_layers(nc, a, out):
    with ExitStack() as ctx:
        build(nc, ctx, a, out)


def build(nc, ctx, a, out):
    def sb(name, shape, dt=F32):
        return ctx.enter_context(nc.sbuf_tensor(name, shape, dt))

    def dram(name, shape, dt=F32):
        return nc.dram_tensor(name, shape, dt, kind="Internal").ap()

    sems = {}

    def sem(name):
        if name not in sems:
            sems[name] = ctx.enter_context(nc.semaphore(name))
        return sems[name]

    ps = ctx.enter_context(nc.psum_tensor("ps", [P, 8, CH], F32))

    x_tok = sb("x_tok", [P, NT, D])
    xn_tok = sb("xn_tok", [P, NT, D])
    moe_tok = sb("moe_tok", [P, NT, D])
    tmp_rows = sb("tmp_tok", [P, NT, DI])
    tmp_tok = tmp_rows[:, :, 0:D]
    xnT = sb("xnT", [P, N])
    hT = sb("hT", [P, N])

    ident = sb("ident", [P, P])
    ident_bf = sb("ident_bf", [P, P], BF16)
    ones = sb("ones", [P, 128])
    eps = sb("eps", [P, 1])
    rows = {}
    for name in ("L1_attn_gamma", "L1_attn_beta"):
        rows[name] = sb("row_" + name, [P, D])
    lncol = {}
    for name in ("L0_ffn_ln1_w", "L0_ffn_ln1_b", "L0_ffn_ln2_w", "L0_ffn_ln2_b"):
        lncol[name] = sb("col_" + name, [P, 1])
    gate_b = sb("gate_b_row", [P, E])
    col = sb("columns", [P, 8, NT])
    stats = sb("stats", [P, NT, 6])

    sqd = {"L0_attn_Wv": None, "L0_attn_Wo": None}
    for name in sqd:
        sqd[name] = sb("w_" + name, [D, D])
    wqkv = sb("wqkv", [D, 3 * D])
    gate_w = sb("gate_w_sb", [D, E])
    wproj = sb("wproj", [D, D])
    splatT = sb("splatT", [D, S])
    splat = sb("splat", [S, D])
    splat_ls = sb("splat_ls", [S, 1])
    splat_amp = sb("splat_amp", [S, 1])
    scol = sb("splat_columns", [S, 6])
    splat_sq = sb("splat_squares", [S, D])

    arena = sb("arena", [P, ARENA])

    def carve(at, shape, dt=F32):
        n = 1
        for s in shape[1:]:
            n *= s
        words = n * (4 if dt == F32 else 2) // 4
        v = arena[0:shape[0], at:at + words]
        if dt != F32:
            v = v.bitcast(dt)
        if len(shape) > 2:
            names = "abcd"[:len(shape) - 1]
            v = v.rearrange("p (" + " ".join(names) + ") -> p " + " ".join(names),
                            **dict(zip(names[1:], shape[2:])))
        return v, at + words

    Qs, at = carve(0, [P, RING, HG * T], BF16)
    Ks, at = carve(at, [P, RING, HG * T], BF16)
    empty_rows, _ = carve(at, [P, MTILES, DI])
    probs, at = carve(at, [P, 2, HG, CH])
    Vg, at = carve(at, [P, RING, MT, HG, 32])
    parts, _ = carve(at, [P, 2, SPLITS, N], BF16)
    part_rest, _ = carve(at + SPLITS * N, [P, 2, CH])
    Yraw, at = carve(at, [P, NG, N])
    Vtok = tmp_tok
    Ytok1 = hT[:].rearrange("p (t d) -> p t d", d=D)
    mxh = sb("mx_halves", [P, UNITS, 2])
    nmx = sb("neg_max", [P, UNITS])
    mxr = sb("max_rest", [P, UNITS])
    mxs = sb("max_parts", [P, SPLITS, UNITS], BF16)
    mxrow = sb("max_rows", [SPLITS * UNITS, P], BF16)
    wall, at = carve(0, [P, E, EWB])
    assert at == MOE0
    at = MOE0
    wcur, at = carve(at, [P, ER, EWB])
    xs, at = carve(at, [P, XR, DI])
    xsT, at = carve(at, [P, ER, P])
    hid, at = carve(at, [P, ER, FT, P])
    ys, at = carve(at, [P, ER, D])
    assert at <= MOE0 + N + 2 * B * PADT
    xsqT, at = carve(MOE0 + N + 2 * B * PADT, [P, N])
    splat_out = xsqT.rearrange("p (t d) -> p t d", d=D)
    gaussT, at = carve(at, [S, N])
    gauss, at = carve(at, [P, NT, S])
    xg, at = carve(at, [P, B, S])
    gvT, at = carve(at, [P, B, S])
    gvw, at = carve(at, [S, B, D + 1])
    assert at <= ARENA
    rden = sb("rden", [P, 2, H, 1])
    route = sb("route", [P, 4, NT, E])
    chosen = sb("chosen", [P, NT, E], BF16)
    ones_bf = sb("ones_bf", [P, P], BF16)
    earlier = sb("earlier", [P, P], BF16)
    count = sb("count_from_0", [P, MTILES])
    tile_start = sb("tile_start", [P, NT])
    filled = sb("filled_tiles", [P, E, NT])
    tiles_to = sb("tiles_up_to_expert", [P, 4, E])
    first_slot = sb("first_slot", [P, E])
    ended = sb("experts_ended", [P, MTILES, E])
    te_f = sb("tile_expert_f", [P, MTILES])
    slot_f = sb("slot_f", [P, NT])
    score = sb("score", [P, NT])
    tok_slot = {tag: sb(f"{tag}_slot", [P, NT], I32) for tag in FIRST_TILE}
    tile_expert = sb("tile_expert", [P, 2 * MTILES], I32)
    qT, at = carve(MOE0, [P, N])
    kT, at = carve(at, [P, B, PADT])
    kpT, at = carve(at, [P, B, PADT])
    vT, at = carve(at, [P, B, PADT])
    zT, at = carve(at, [P, N])
    denT, at = carve(at, [P, N])
    qk, at = carve(at, [P, WRING, TB, W])
    kdiag, at = carve(at, [P, WRING, H, WIN])
    vwin, at = carve(at, [P, VRING, D])
    vdiag, at = carve(at, [P, WRING, NG, HG, DK])
    rv, at = carve(at, [P, 2, TB, W])
    wprobs, at = carve(at, [P, 2, NG, TB, W])
    assert at <= ARENA
    cmax = sb("key_max", [P, 2, NG * TB])
    nM = sb("neg_block_max", [P, HG])
    mparts = sb("block_max_parts", [P, HG, WIN], BF16)
    head_rows = sb("head_rows", [P, H])
    quad_rows = sb("quad_rows", [P, HG, DK])
    mask_keys = sb("mask_keys", [P, HG, WIN], BF16)
    mask_toks = sb("mask_toks", [P, TB, W], BF16)
    tok_rows = sb("tok_rows", [TB, P // TB, TB], BF16)
    mask_seen = sb("mask_seen", [P, HG * WIN], BF16)
    mask_once = sb("mask_once", [P, HG * WIN])
    spread = sb("spread_max", [P, NG, TB, W], BF16)
    zero_rows = sb("zero_rows", [P, D])
    w1m = {}
    for name in ("Wq", "Wk", "Wkp", "Wv", "Wo"):
        w1m[name] = sb("w1_" + name, [D, D])
    w_red = sb("w_red_sb", [D, 16])
    wg = sb("wg_sb", [E, 16])
    wgn = sb("wgn", [E, 16])
    wgs = sb("wg_columns", [E, 4])
    wgT = sb("wgT", [16, E])
    redT = sb("redT", [16, N])
    b2_row = sb("b2_row", [1, E * D])

    xs_d = {tag: dram(f"{tag}_tokens_sorted", (MTILES * P, DI)) for tag in FIRST_TILE}
    ys_d = {tag: dram(f"{tag}_results", (N + MTILES * P, D)) for tag in FIRST_TILE}
    v_pad = dram("v_padded", (B, PADT, D))
    qs_d = dram("q_parts", (SPLITS, D, N), BF16)
    ks_d = dram("k_parts", (H, SPLITS * DK, N), BF16)

    class TileCopies:

        def __init__(self, eng, tag, copy, affine=None):
            self.eng, self.tag, self.copy, self.affine = eng, tag, copy, affine

        def weights(self, turn, u):
            n = turn * XR + u
            if isinstance(n, int) and n == FIRST_TILE[self.tag]:
                self.eng.wait_ge(sem(f"{self.tag}_experts_ready"), 1)
                self.eng.wait_ge(sem(f"{self.tag}_weights"), 16 * (1 + E + (self.tag == "m1")))
            width = EWB if self.tag == "m1" else EW
            e = self.eng.value_load(tile_expert[0:1, bass.ds(n, 1)], min_val=0, max_val=E - 1)
            self.copy(wcur[:, u % ER, 0:width], wall[:, bass.ds(e, 1), 0:width].rearrange("p o w -> p (o w)")) \
                .then_inc(sem("tile_w_ready"), 1)

        def transposed(self, turn, u):
            self.eng.wait_ge(sem("tile_xsT_in_psum"), turn * XR + (u + 1))
            (self.affine or self.copy)(xsT[:, u % ER, :], ps[:, 0, 0:P]).then_inc(sem("tile_xsT_ready"), 1)

        def results(self, turn, u):
            n, s = turn * XR + u, u % ER
            self.eng.wait_ge(sem("tile_ys_in_psum"), turn * XR + (u + 1))
            if not (isinstance(n, int) and n < ER):
                self.eng.wait_ge(sem(f"tile_ys_stored{s}"), (turn * 2 + u // ER) * 16)
            self.copy(ys[:, s, :], ps[:, 4 + s, 0:D]).then_inc(sem("tile_ys_ready"), 1)

    block = ctx.enter_context(nc.Block())

    @block.sync
    def _(sp):
        def load(dst, src, s):
            sp.dma_start(dst, src).then_inc(sem(s), 16)

        load(x_tok[:], a["L0_attn_token_embeddings"].rearrange("b (n p) d -> p (b n) d", p=P), "x_in")
        for name, t in sqd.items():
            load(t[:], a[name], "w_in")
        load(wqkv[:], a["L0_ffn_w_qkv"], "w_in")
        load(gate_w[:], a["L0_ffn_gate_w"], "w_in")
        for name, t in lncol.items():
            load(t[:], a[name].rearrange("(d o) -> d o", o=1), "lncol_in")
        load(splat[:], a["L0_attn_splat_positions"], "splat_in")
        load(splatT[:], a["splat_positions_T"], "splat_in")
        load(splat_ls[:], a["L0_attn_splat_log_scales"].rearrange("(s o) -> s o", o=1), "splat_in")
        load(splat_amp[:], a["L0_attn_splat_amplitudes"].rearrange("(s o) -> s o", o=1), "splat_in")
        for name, t in rows.items():
            load(t[:], a[name].partition_broadcast(P), "rows_in")
        load(gate_b[:], a["L0_ffn_gate_b"].partition_broadcast(P), "rows_in")
        load(wproj[:], a["L0_ffn_w_proj"], "w_in")

        sp.wait_ge(sem("numbers_ready"), 1)
        for tag in FIRST_TILE:
            load(xs_d[tag].rearrange("(k p) d -> p k d", p=P), empty_rows, "slots_cleared")

        sp.wait_ge(sem("parts_ready"), NCH)
        load(qs_d.rearrange("s d t -> d s t"), parts[:, 0], "q_parts_stored")

        def load_q(G, slot):
            b, g = G // NG, G % NG
            for h in range(HG):
                for i in range(SPLITS):
                    v = qs_d[i, bass.ds((g * HG + h) * DK, DK), bass.ds(b * T, T)]
                    load(Qs[i * SPLITS * DK:(i + 1) * SPLITS * DK, slot, h * T:(h + 1) * T],
                         v.unsqueeze(0).broadcast_to([SPLITS, DK, T]), f"stack_in{slot}")

        def load_k(G, slot):
            b, g = G // NG, G % NG
            for h in range(HG):
                v = ks_d[bass.ds(g * HG + h, 1), :, bass.ds(b * T, T)]
                load(Ks[0:KQ, slot, h * T:(h + 1) * T], v.broadcast_to([SPLITS, SPLITS * DK, T]), f"stack_in{slot}")

        def store_max(G, slot):
            sp.wait_ge(sem("max_rows_ready"), G + 1)
            load(Qs[KQ:KX, slot, :], mxrow[:], f"maxrow_in{slot}")

        sp.wait_ge(sem("q_parts_stored"), 16)
        load_q(0, 0)
        sp.wait_ge(sem("parts_ready"), 2 * NCH)
        for j in range(SPLITS):
            load(ks_d.rearrange("h (j d) t -> j h d t", d=DK)[j], parts[:, 1, j, :], "k_parts_stored")
        sp.wait_ge(sem("k_parts_stored"), SPLITS * 16)
        sp.wait_ge(sem("ksrows_one"), 1)
        load_k(0, 0)
        for G in range(1, RING):
            load_q(G, G)
            load_k(G, G)
        store_max(0, 0)

        def group(G, slot, prefetch=True):
            store_max(G + 1, (slot + 1) % RING)
            if prefetch:
                sp.wait_ge(sem("scores_done"), (G + 1) * STEPS * 2)
                load_q(G + RING, slot)
                load_k(G + RING, slot)

        for G in range(GROUPS - 1):
            group(G, G % RING, prefetch=G + RING < GROUPS)

        def expert_weights(tag, w1_d, w2_d, b1_d=None):
            load(wall[:, :, 0:HID], w1_d.rearrange("e d f -> d e f"), f"{tag}_weights")
            for e in range(E):
                load(wall[:, e, HID:EW].rearrange("p (f d) -> p f d", d=D),
                     w2_d[e].rearrange("(f p) d -> p f d", p=P), f"{tag}_weights")
            if b1_d is not None:
                load(wall[:, :, EW:EWB], b1_d.rearrange("p (e f) -> p e f", f=FT), f"{tag}_weights")

        def expert_tiles(tag, dst):
            n0 = FIRST_TILE[tag]

            def load_tile(turn, u):
                if not (isinstance(turn, int) and turn * XR + u < XR):
                    sp.wait_ge(sem(f"tile_ys_stored{u % ER}"), (turn * 2 + (u - XR) // ER + 1) * 16)
                load(xs[:, u % XR, :], xs_d[tag][bass.ds((turn * XR + u - n0) * P, P), :], f"tile_xs_in{u % XR}")

            sp.wait_ge(sem(f"{tag}_scattered"), 16 * NT)
            for u in range(XR):
                load_tile(n0 // XR, u)
            with sp.Fori(n0 // XR, (n0 + MTILES) // XR - 1) as turn:
                for u in range(XR):
                    load_tile(turn, XR + u)
            for s in range(ER):
                sp.wait_ge(sem(f"tile_ys_stored{s}"), (n0 + MTILES) // ER * 16)
            for c in range(NCH):
                v = slice(4 * c, 4 * c + 4)
                load(dst[:, v, :], ys_d[tag][0:N, :].rearrange("(n p) d -> p n d", p=P)[:, v, :], f"results_in{c}")

        sp.wait_ge(sem("scores_done"), GROUPS * STEPS * 2)
        expert_weights("m0", a["L0_ffn_w1"], a["L0_ffn_w2"])
        expert_tiles("m0", tmp_tok)

        for name, t in w1m.items():
            load(t[:], a[f"L1_{name}_T"], "w_l1")
        load(w_red[:], a["L1_ffn_w_red"], "w_l1")
        load(wg[:], a["L1_ffn_wg"], "w_l1")
        load(b2_row[:], a["L1_ffn_b2"].rearrange("(o e) d -> o (e d)", o=1), "w_l1")
        expert_weights("m1", a["L1_ffn_w1"], a["L1_ffn_w2"], a["L1_b1_cols"])
        sp.wait_ge(sem("masks_ready"), 1)
        sp.wait_ge(sem("v1_tok_ready"), NCH)
        for b in range(B):
            load(v_pad[b, 0:W, :], zero_rows[0:W, :], "v_stored")
            load(v_pad[b, W:PADT, :].rearrange("(n p) d -> p n d", p=P), tmp_tok[:, b * MT:(b + 1) * MT, :],
                 "v_stored")
        sp.wait_ge(sem("v_stored"), 64)

        def window(n, b, blk, slot):
            if not (isinstance(n, int) and n < VRING):
                sp.wait_ge(sem("vdiag_ready"), n - VRING + 1)
            src = v_pad[b, bass.ds(blk * TB, WIN), :]
            load(vwin[:, slot, :], src.unsqueeze(0).broadcast_to([HG, WIN, D]), f"window{slot}")

        for n in range(VRING):
            window(n, n % B, n // B, n)
        with sp.Fori(1, BLOCKS // VRING) as it:
            for u in range(VRING):
                window(it * VRING + u, u % B, it * (VRING // B) + u // B, u)
        for n in range(BLOCKS - BLOCKS % VRING, BLOCKS):
            window(n, n % B, n // B, n % VRING)

        sp.wait_ge(sem("vdiag_ready"), BLOCKS)
        expert_tiles("m1", Ytok1)
        for c in range(NCH):
            sp.wait_ge(sem("final"), c + 1)
            load(out.rearrange("b (n p) d -> p (b n) d", p=P)[:, 4 * c:4 * c + 4], x_tok[:, 4 * c:4 * c + 4], "stored")
        sp.wait_ge(sem("stored"), 16 * NCH)

    @block.gpsimd
    def _(pool):
        st = Steps(pool, sem("pool_chain"))
        pool.memset(ident[:], 0.0)
        pool.memset(ident_bf[:], 0.0)
        pool.memset(eps[:], LN_EPS).then_inc(sem("eps_ready"), 1)
        pool.memset(ones[:], 1.0).then_inc(sem("ones_ready"), 1)
        pool.wait_ge(sem("ones_ready"), 1)
        for m in (ident, ident_bf):
            pool.affine_select(out=m[:], in_=m[:], compare_op=ALU.not_equal, fill=1.0, base=0,
                               pattern=[[-1, P]], channel_multiplier=1).then_inc(sem("ident_ready"), 1)
        chain(pool.memset(ones_bf[:], 1.0), st)
        chain(pool.memset(earlier[:], 1.0), st)
        pool.affine_select(out=earlier[:], in_=earlier[:], compare_op=ALU.is_ge, fill=0.0, base=-1,
                           pattern=[[1, P]], channel_multiplier=-1)
        for k in range(MTILES):
            pool.memset(count[:, k:k + 1], float(k))
        for k in range(NT):
            pool.memset(tile_start[:, k:k + 1], float(P * k))
        pool.memset(empty_rows, 0.0).then_inc(sem("consts_ready"), 1)
        pool.wait_ge(sem("consts_ready"), 1)

        pool.memset(Ks[64:P, :, :], 1.0).then_inc(sem("ksrows_one"), 1)
        pool.wait_ge(sem("ksrows_one"), 1)
        chain(pool.memset(Vg[:, :, :, :, DK:32], 1.0), st)

        def scatter_ready(tag):
            pool.wait_ge(sem("slots_cleared"), 2 * 16)
            pool.wait_ge(sem(f"{tag}_slots_ready"), 1)

        def scatter(tag, src, t):
            pool.indirect_dma_start(
                out=xs_d[tag][:, :], out_offset=bass.IndirectOffsetOnAxis(ap=tok_slot[tag][:, t:t + 1], axis=0),
                in_=src[:, t, :], in_offset=None).then_inc(sem(f"{tag}_scattered"), 16)

        def send_results(tag):
            def send(turn, u):
                pool.wait_ge(sem("tile_ys_ready"), turn * XR + (u + 1))
                pool.indirect_dma_start(
                    out=ys_d[tag][:, :],
                    out_offset=bass.IndirectOffsetOnAxis(ap=xs[:, u % XR, D:DI].bitcast(I32), axis=0),
                    in_=ys[:, u % ER, :], in_offset=None).then_inc(sem(f"tile_ys_stored{u % ER}"), 16)

            for n in range(FIRST_TILE[tag], FIRST_TILE[tag] + MTILES):
                send(n // XR, n % XR)

        def values(G, slot):
            if not (isinstance(G, int) and G < RING):
                pool.wait_ge(sem("pv_done"), (G - RING + 1) * STEPS)
            b, g = G // NG, G % NG
            src = Vtok[:, bass.ds(b * MT, MT), bass.ds(g * HG * DK, HG * DK)]
            pool.tensor_copy(Vg[:, slot, :, :, 0:DK], src.rearrange("p m (h d) -> p m h d", d=DK)) \
                .then_inc(sem("vg_ready"), 1)

        pool.wait_ge(sem("v_tok_ready"), 1)
        for G in range(GROUPS):
            values(G, G % RING)

        def keep(m, pattern, base, mult, op=ALU.is_ge, fill=0.0):
            chain(pool.affine_select(out=m, in_=m, compare_op=op, fill=fill, base=base, pattern=pattern,
                                     channel_multiplier=mult), st)

        chain(pool.memset(head_rows[:], 1.0), st)
        keep(head_rows[:], [[-DK, H]], 0, 1)
        keep(head_rows[:], [[DK, H]], DK - 1, -1)
        chain(pool.memset(quad_rows[:], 1.0), st)
        keep(quad_rows[:], [[-32, HG], [0, DK]], 0, 1)
        keep(quad_rows[:], [[32, HG], [0, DK]], 31, -1)
        chain(pool.memset(mask_keys[:], 0.0), st)
        keep(mask_keys[0:TB], [[0, HG], [1, WIN]], -1, -1, fill=BIG)
        keep(mask_keys[0:TB], [[0, HG], [-1, WIN]], W, 1, fill=BIG)
        chain(pool.memset(mask_keys[32:33], BIG), st)
        chain(pool.memset(mask_keys[64:65, :, 0:W], BIG), st)
        chain(pool.memset(mask_toks[:], 0.0), st)
        chain(pool.memset(mask_toks[32:33], 1.0), st)
        keep(mask_toks[32:33], [[-1, TB], [-1, W]], W - 2, 0)
        chain(pool.memset(mask_toks[64:65], 1.0), st)
        chain(pool.memset(tok_rows[:], 0.0), st)
        keep(tok_rows[:], [[0, P // TB], [-1, TB]], 0, 1, op=ALU.not_equal, fill=1.0)
        chain(pool.memset(mask_once[64:P], 0.0), st)
        chain(pool.memset(spread[:], 0.0), st)
        for part in range(2):
            keep(spread[:], [[-TB, NG], [-1, TB], [0, W]], -64 * part, 1, op=ALU.not_equal, fill=1.0)
        scatter_ready("m0")
        for t in range(NT):
            scatter("m0", tmp_rows, t)
        send_results("m0")
        pool.wait_ge(sem("xn1_ready"), 1)
        for t in (kT, kpT, vT):
            chain(pool.memset(t[:, :, 0:W], 0.0), st)
        pool.memset(zero_rows[:], 0.0).then_inc(sem("masks_ready"), 1)

        def diagonals(n, b, blk, slot, turn):
            three = slot % WRING
            if not (isinstance(n, int) and n < WRING):
                pool.wait_ge(sem("win_scores"), n - 2)
            src = kpT[:, b, bass.ds(blk * TB, WIN)]
            pool.tensor_tensor(kdiag[:, three], src.unsqueeze(1).broadcast_to([P, H, WIN]),
                               head_rows[:].unsqueeze(2).broadcast_to([P, H, WIN]), ALU.mult) \
                .then_inc(sem("kdiag_ready"), 1)
            kw = kT[:, b, bass.ds(blk * TB + 1, TB + W - 1)]
            kw = bass.AP(kw.tensor, kw.offset, [list(kw.ap[0]), [1, TB], [1, W]])
            q = qT[:, bass.ds(blk * TB + b * T, TB)]
            pool.tensor_tensor(qk[:, three], q.unsqueeze(2).broadcast_to([P, TB, W]), kw, ALU.mult) \
                .then_inc(sem("qk_ready"), 1)
            if not (isinstance(n, int) and n < WRING):
                pool.wait_ge(sem("win_rv"), n - 2)
            pool.wait_ge(sem(f"window{slot}"), turn * 16)
            pool.tensor_tensor(vdiag[:, three],
                               vwin[:, slot].rearrange("p (g j d) -> p g j d", g=NG, j=HG),
                               quad_rows[:].unsqueeze(1).broadcast_to([P, NG, HG, DK]), ALU.mult) \
                .then_inc(sem("vdiag_ready"), 1)

        pool.wait_ge(sem("q1_ready"), NCH)
        pool.wait_ge(sem("qkv1_ready"), 2 * NCH)
        SOLO = (PEEL + NT + BODY - 1) // BODY
        for n in range(SOLO * BODY):
            diagonals(n, n % B, n // B, n % BODY, n // BODY + 1)
            if n == PEEL:
                pool.wait_ge(sem("xn1_rows_ready"), 1)
                scatter_ready("m1")
            if PEEL <= n < PEEL + NT:
                scatter("m1", tmp_rows, n - PEEL)
        with pool.Fori(SOLO, BLOCKS // BODY) as it:
            for u in range(BODY):
                diagonals(it * BODY + u, u % B, it * (BODY // B) + u // B, u, it + 1)
        for n in range(BLOCKS - BLOCKS % BODY, BLOCKS):
            diagonals(n, n % B, n // B, n % BODY, n // BODY + 1)
        send_results("m1")

    @block.scalar
    def _(act):
        def evacuate(dst, after, ready, affine=None):
            kw = {} if affine is None else {"scale": lncol[affine + "_w"][:], "bias": lncol[affine + "_b"][:]}
            for c in range(NCH):
                act.wait_ge(sem(after), c + 1)
                act.activation(dst[:, c * CH:(c + 1) * CH], ps[:, c, :], ACT.Identity if affine else ACT.Copy,
                               **kw).then_inc(sem(ready), 1)

        def norm(n, dst, src):
            act.wait_ge(sem("ln_var"), n)
            act.activation(col[:, 4, :], col[:, 3, :], ACT.Sqrt, bias=eps[:], scale=1.0 / D) \
                .then_inc(sem("ln_std"), 1)
            act.wait_ge(sem("ln_scale"), n)
            for t in range(NT // 2, NT):
                last = act.activation(dst[:, t, :], src[:, t, :], ACT.Identity, scale=col[:, 3, t:t + 1],
                                      bias=col[:, 1, t:t + 1])
                if t % 4 == 3:
                    last.then_inc(sem("ln_by_act"), 1)

        act.wait_ge(sem("eps_ready"), 1)
        norm(1, xn_tok, x_tok)

        norm(2, moe_tok, xn_tok)
        act.wait_ge(sem("lncol_in"), 4 * 16)
        evacuate(hT, "hT_in_psum", "hT_ready", "L0_ffn_ln1")
        for w in range(2):
            for c in range(NCH):
                n = w * NCH + c
                act.wait_ge(sem("qk_in_psum"), n + 1)
                hi = parts[:, w, 0, c * CH:(c + 1) * CH]
                act.activation(hi, ps[:, n % 4, :], ACT.Copy).then_inc(sem("part_hi"), 1)
                act.wait_ge(sem("part_r1"), n + 1)
                act.activation(parts[:, w, 1, c * CH:(c + 1) * CH], part_rest[:, n % 2, :], ACT.Copy) \
                    .then_inc(sem("part_mid"), 1)

        def take_y(half):
            G = half // QH
            act.wait_ge(sem("pv_done"), (half + 1) * MT)
            b, g, col0 = G // NG, G % NG, (G // NG) * T + (half % QH) * CH
            act.activation(Yraw[:, g, col0:col0 + CH], ps[:, YB, :], ACT.Copy).then_inc(sem("y_taken"), 1)

        taken = ("scores_taken", "scores_taken", "y_taken", "v_tok_ready")
        for c in range(NCH):
            act.wait_ge(sem("v_in_psum"), c + 1)
            act.activation(Vtok[:, 4 * c:4 * c + 4, :], ps[:, 4 + c, :].rearrange("p (n d) -> p n d", d=D),
                           ACT.Copy).then_inc(sem(taken[c]), 1)

        act.wait_ge(sem("splat_in"), 64)
        act.activation(scol[:, 0:1], splat_ls[:], ACT.Exp).then_inc(sem("splat_scale"), 1)

        act.wait_ge(sem("slots_cleared"), 2 * 16)
        for G in range(GROUPS):
            b, g = G // NG, G % NG
            for k in range(STEPS):
                n = G * STEPS + k
                for pair in range(2):
                    act.wait_ge(sem("scores_done"), n * 2 + pair + 1)
                    if n >= 2 and pair == 0:
                        act.wait_ge(sem("pv_done"), n - 1)
                    act.activation(probs[:, k % 2, 2 * pair:2 * pair + 2, :],
                                   ps[:, 2 * pair:2 * pair + 2, :], ACT.Exp, scale=SCALE) \
                        .then_inc(sem("scores_taken"), 1)
                if n and k % MT == 0:
                    take_y(n // MT - 1)
        take_y(GROUPS * QH - 1)

        for c in range(NCH):
            act.wait_ge(sem("yT_in_psum"), c + 1)
            act.activation(hT[:, c * CH:(c + 1) * CH], ps[:, 4 + c, :], ACT.Copy).then_inc(sem("yT_ready"), 1)

        norm(3, tmp_tok, moe_tok)
        evacuate(hT, "h2T_in_psum", "h2T_ready", "L0_ffn_ln2")

        for c in range(NCH):
            act.wait_ge(sem("xnT_in_psum"), c + 1)
            cs = slice(c * CH, (c + 1) * CH)
            act.activation(xnT[:, cs], ps[:, c, :], ACT.Copy)
            act.activation(xsqT[:, cs], ps[:, c, :], ACT.Square).then_inc(sem("xnT_ready"), 1)
        act.wait_ge(sem("splat_scale2"), 1)
        for c in range(NCH):
            cs = slice(c * CH, (c + 1) * CH)
            act.wait_ge(sem("d2_in_psum"), c + 1)
            act.activation(gaussT[:, cs], ps[0:S, c, :], ACT.Relu, bias=scol[:, 4:5]).then_inc(sem("d2_ready"), 1)
            act.wait_ge(sem("d2_ready"), c + 1)
            act.activation(gaussT[:, cs], gaussT[:, cs], ACT.Exp, scale=scol[:, 3:4]).then_inc(sem("gauss_exp"), 1)
            act.wait_ge(sem("gauss_exp"), c + 1)
            act.activation(gaussT[:, cs], gaussT[:, cs], ACT.Copy, scale=splat_amp[:]).then_inc(sem("gaussT_ready"), 1)
        for c in range(2):
            act.wait_ge(sem("gauss_in_psum"), c + 1)
            act.activation(gauss[:, 8 * c:8 * c + 8, :], ps[:, 4 + c, :].rearrange("p (n s) -> p n s", s=S),
                           ACT.Copy).then_inc(sem("gauss_ready"), 1)

        def expert_gelu(tag, n, s, func, bias):
            act.wait_ge(sem("tile_h_in_psum"), n + 1)
            if bias:
                for f in range(FT):
                    last = act.activation(hid[:, s, f, :], ps[:, 1 + s, f * P:(f + 1) * P], func,
                                          bias=wcur[:, s, EW + f:EW + f + 1])
            else:
                last = act.activation(hid[:, s].rearrange("p f m -> p (f m)"), ps[:, 1 + s, :], func)
            last.then_inc(sem("tile_h_ready"), 1)

        def gelus(tag, func, copies=None):
            n0 = FIRST_TILE[tag]
            loop_from = n0 + LOOP_FROM[tag]

            def step(turn, u, copying=False):
                if copying:
                    copies.transposed(turn, u + 1)
                    copies.weights(turn, u + 1)
                expert_gelu(tag, turn * XR + u, u % ER, func, copies is not None)
                if copying and turn * XR + u > n0:
                    copies.results(turn, u - 1)

            if copies:
                copies.transposed(n0 // XR, 0)
                copies.weights(n0 // XR, 0)
            for n in range(n0, loop_from):
                step(n // XR, n % XR, copying=copies is not None)
            tile_loop(act, step, tag)
            for n in range(n0 + MTILES - 2, n0 + MTILES):
                step(n // XR, n % XR)

        gelus("m0", ACT.Gelu_apprx_tanh)

        norm(4, xn_tok, x_tok)
        act.wait_ge(sem("wg_norm2"), 1)
        act.activation(wgs[:, 1:2], wgs[:, 0:1], ACT.Sqrt).then_inc(sem("wg_norm"), 1)
        evacuate(xnT, "xn1T_in_psum", "xn1T_ready")
        for c in range(NCH):
            act.wait_ge(sem("red_in_psum"), c + 1)
            act.activation(redT[:, c * CH:(c + 1) * CH], ps[0:16, 4 + c, :], ACT.Copy).then_inc(sem("red_ready"), 1)
        for c in range(NCH):
            act.wait_ge(sem("v1_in_psum"), c + 1)
            act.activation(tmp_tok[:, 4 * c:4 * c + 4, :], ps[:, c, :].rearrange("p (n d) -> p n d", d=D),
                           ACT.Copy).then_inc(sem("v1_tok_ready"), 1)
        act.wait_ge(sem("gate1_shifted"), 1)
        act.activation(route[:, 3], route[:, 0], ACT.Exp).then_inc(sem("gate1_exp"), 1)
        for w, dst in enumerate((qT, kT, kpT, vT)):
            for c in range(NCH):
                act.wait_ge(sem("qkv1_in_psum"), w * NCH + c + 1)
                if w == 0:
                    v = dst[:, c * CH:(c + 1) * CH]
                else:
                    v = dst[:, c // QH, W + (c % QH) * CH:W + (c % QH + 1) * CH]
                act.activation(v, ps[:, 4 + (w * NCH + c) % 4, :], ACT.Copy) \
                    .then_inc(sem("qkv1_ready" if w else "q1_ready"), 1)

        act.wait_ge(sem("v_stored"), 64)
        act.wait_ge(sem("ln_by_act"), 4 * (NCH // 2))
        act.activation(tmp_tok, xn_tok[:], ACT.Copy).then_inc(sem("xn1_rows_ready"), 1)

        def window_exp(n, two, three):
            act.wait_ge(sem("win_shifted"), n + 1)
            if not (isinstance(n, int) and n < 2):
                act.wait_ge(sem("win_rv"), n - 1)
            act.activation(wprobs[:, two].rearrange("p g s j -> p (g s j)"),
                           ps[:, 2 * three:2 * three + 2, :].rearrange("p a n -> p (a n)"), ACT.Exp, scale=SCALE) \
                .then_inc(sem("win_exp"), 1)

        for n in range(PEEL):
            window_exp(n, n % 2, n % 3)
        with act.Fori(0, (BLOCKS - PEEL) // BODY) as it:
            for u in range(BODY):
                window_exp(it * BODY + (PEEL + u), u % 2, (PEEL + u) % 3)
        gelus("m1", ACT.Gelu, TileCopies(act, "m1", lambda o, i: act.activation(o, i, ACT.Copy)))
        norm(5, xn_tok, tmp_tok)

    @block.tensor
    def _(pe):
        def transpose_all(src, n, after, done):
            for t in range(NT):
                if t % 4 == 0 and t < NT // 2:
                    pe.wait_ge(sem(after), t // 4 + 1)
                elif t % 4 == 0:
                    pe.wait_ge(sem("ln_by_act"), (n - 1) * (NCH // 2) + (t - NT // 2) // 4 + 1)
                m = pe.transpose(ps[:, t // 4, (t % 4) * P:(t % 4 + 1) * P], src[:, t, :], ident[:])
                if t % 4 == 3:
                    m.then_inc(sem(done), 1)

        pe.wait_ge(sem("ident_ready"), 2)
        pe.wait_ge(sem("ones_ready"), 1)
        pe.wait_ge(sem("consts_ready"), 1)
        pe.matmul(ps[:, 7, 0:1], earlier[:], ones_bf[:, 0:1], start=True, stop=True) \
            .then_inc(sem("number_in_psum"), 1)
        transpose_all(moe_tok, 2, "h_ready", "hT_in_psum")
        pe.wait_ge(sem("w_in"), 5 * 16)
        def qk_products(w):
            for c in range(NCH):
                if w:
                    pe.wait_ge(sem("parts_ready"), c + 1)
                else:
                    pe.wait_ge(sem("hT_ready"), c + 1)
                pe.matmul(ps[:, c, :], wqkv[:, w * D:(w + 1) * D], hT[:, c * CH:(c + 1) * CH],
                          start=True, stop=True).then_inc(sem("qk_in_psum"), 1)

        qk_products(0)
        pe.wait_ge(sem("numbers_ready"), 1)
        for t in range(NT):
            m = pe.matmul(ps[:, 4 + t // 4, (t % 4) * D:(t % 4 + 1) * D], hT[:, t * P:(t + 1) * P],
                          wqkv[:, 2 * D:3 * D], start=True, stop=True)
            if t % 4 == 3:
                m.then_inc(sem("v_in_psum"), 1)
        qk_products(1)

        def max_unit(G, slot, u):
            h, q = u // MT, u % MT
            for half in range(2):
                i = 2 * u + half
                n = G * (UNITS * 2) + i
                if i >= MXN:
                    pe.wait_ge(sem("max_taken"), n - MXN + 1)
                elif not (isinstance(G, int) and G == 0):
                    pe.wait_ge(sem("max_taken"), n if i == 0 else n - MXN)
                if i == 2 and not (isinstance(G, int) and G == 0):
                    pe.wait_ge(sem("max_rows_ready"), G)
                pe.matmul(ps[:, MX + i % MXN, :], Qs[0:KQ, slot, h * T + q * P:h * T + (q + 1) * P],
                          Ks[0:KQ, slot, h * T + half * CH:h * T + (half + 1) * CH], start=True, stop=True) \
                    .then_inc(sem("max_scores"), 1)

        def max_rows(G):
            pe.wait_ge(sem("max_split"), G + 1)
            pe.transpose(ps[0:SPLITS * UNITS, MX + 2, 0:P // 2].bitcast(BF16),
                         mxs[:].rearrange("p s u -> p (s u)"), ident_bf[:]).then_inc(sem("max_rows_in_psum"), 1)

        def await_stack(G, slot, turn):
            pe.wait_ge(sem(f"stack_in{slot}"), (turn + 1) * (16 * HG * (SPLITS + 1)))

        def group(G, slot, turn, more):
            def after(d):
                return (slot + d) % RING, turn + (slot + d) // RING

            pe.wait_ge(sem(f"maxrow_in{slot}"), (turn + 1) * 16)
            for k in range(STEPS + 1):
                n = G * STEPS + k
                half, m = k // MT, k % MT
                for pair in range(2):
                    if k < STEPS:
                        pe.wait_ge(sem("scores_taken"), n * 2 + pair + 1)
                        for h in (2 * pair, 2 * pair + 1):
                            mm = pe.matmul(ps[:, SC + h, :], Ks[0:KX, slot, h * T + m * P:h * T + (m + 1) * P],
                                           Qs[0:KX, slot, h * T + half * CH:h * T + (half + 1) * CH],
                                           start=True, stop=True)
                        mm.then_inc(sem("scores_done"), 1)
                        u = 2 * (k + AHEAD) + pair
                        if u < UNITS and more >= 1:
                            max_unit(G + 1, after(1)[0], u)
                        if u >= UNITS and more >= 2:
                            if u == UNITS:
                                await_stack(G + 2, *after(2))
                            max_unit(G + 2, after(2)[0], u - UNITS)
                if k == STEPS - AHEAD - 1 and more >= 1:
                    max_rows(G + 1)
                if k:
                    j = k - 1
                    pe.wait_ge(sem("scores_taken"), n * 2 + 2)
                    if j == 0:
                        pe.wait_ge(sem("vg_ready"), G + 1)
                    if j % MT == 0:
                        pe.wait_ge(sem("y_taken"), G * QH + (j // MT + 1))
                    for h in range(HG):
                        mm = pe.matmul(ps[32 * h:32 * h + 32, YB, :], Vg[:, slot, j % MT, h, :],
                                       probs[:, j % 2, h, :], start=j % MT == 0, stop=j % MT == MT - 1)
                    mm.then_inc(sem("pv_done"), 1)

        pe.wait_ge(sem("v_tok_ready"), 1)
        pe.wait_ge(sem("parts_ready"), 2 * NCH)
        await_stack(0, 0, 0)
        for u in range(UNITS):
            max_unit(0, 0, u)
        max_rows(0)
        await_stack(1, 1, 0)
        for u in range(2 * AHEAD):
            max_unit(1, 1, u)
        with pe.Fori(0, GROUPS // RING) as it:
            for slot in range(RING):
                group(it * RING + slot, slot, it, 2)
        for G in range(GROUPS // RING * RING, GROUPS):
            group(G, G % RING, G // RING, GROUPS - 1 - G)

        pe.wait_ge(sem("y_taken"), 1 + GROUPS * QH)
        pe.wait_ge(sem("scores_taken"), 2 + GROUPS * STEPS * 2)
        for t in range(NT):
            if t >= 4:
                pe.wait_ge(sem("quotients"), t - 3)
            for g in range(NG):
                m = pe.transpose(ps[:, t % 4, g * P:(g + 1) * P], Yraw[:, g, t * P:(t + 1) * P], ident[:])
            m.then_inc(sem("y_tok_in_psum"), 1)
        for t in range(NT):
            if t % 4 == 0:
                pe.wait_ge(sem("quotients"), t + 4)
            m = pe.transpose(ps[:, 4 + t // 4, (t % 4) * P:(t % 4 + 1) * P], tmp_tok[:, t, :], ident[:])
            if t % 4 == 3:
                m.then_inc(sem("yT_in_psum"), 1)
        for t in range(NT):
            if t % 4 == 0:
                pe.wait_ge(sem("yT_ready"), t // 4 + 1)
            m = pe.matmul(ps[:, t // 4, (t % 4) * D:(t % 4 + 1) * D], hT[:, t * P:(t + 1) * P], wproj[:],
                          start=True, stop=True)
            if t % 4 == 3:
                m.then_inc(sem("proj_in_psum"), 1)
        pe.wait_ge(sem("msa_done"), 1)

        transpose_all(tmp_tok, 3, "h2_ready", "h2T_in_psum")
        pe.wait_ge(sem("h2T_ready"), NCH)
        for t in range(NT):
            m = pe.matmul(ps[:, 6, t * E:(t + 1) * E], hT[:, t * P:(t + 1) * P], gate_w[:], start=True, stop=True)
        m.then_inc(sem("gate_in_psum"), 1)

        def route_counts(tag, bank):
            pe.wait_ge(sem(f"{tag}_chosen"), 1)
            pe.matmul(ps[:, bank, 0:NT * E], earlier[:], chosen[:].rearrange("p t e -> p (t e)"),
                      start=True, stop=False, skip_group_check=True)
            for t in range(NT):
                m = pe.matmul(ps[:, bank, (t + 1) * E:(NT + 1) * E], ones_bf[:],
                              chosen[:, t, :].unsqueeze(1).broadcast_to([P, NT - t, E]),
                              start=False, stop=t == NT - 1, skip_group_check=True)
            m.then_inc(sem(f"{tag}_counts_in_psum"), 1)

        transpose_all(xn_tok, 1, "xn_ready", "xnT_in_psum")
        pe.wait_ge(sem("splat_scale2"), 1)
        for c in range(NCH):
            cs = slice(c * CH, (c + 1) * CH)
            pe.wait_ge(sem("xnT_ready"), c + 1)
            pe.matmul(ps[0:S, c, :], splatT[:], xnT[:, cs], start=True, stop=False)
            pe.matmul(ps[0:S, c, :], ones[:, 0:S], xsqT[:, cs], start=False, stop=True) \
                .then_inc(sem("d2_in_psum"), 1)
        route_counts("m0", 7)
        for t in range(NT):
            if t % 4 == 0:
                pe.wait_ge(sem("gaussT_ready"), t // 4 + 1)
            m = pe.transpose(ps[:, 4 + t // 8, (t % 8) * S:(t % 8 + 1) * S], gaussT[:, t * P:(t + 1) * P],
                             ident[0:S, 0:S])
            if t % 8 == 7:
                m.then_inc(sem("gauss_in_psum"), 1)

        for b in range(B):
            pe.wait_ge(sem("gauss_ready"), b + 1)
            for t in range(MT):
                n = b * MT + t
                m = pe.matmul(ps[:, b, 0:S], xn_tok[:, n, :], gauss[:, n, :], start=t == 0, stop=t == MT - 1)
            m.then_inc(sem("xg_in_psum"), 1)
        for b in range(B):
            pe.wait_ge(sem("xg_ready"), b + 1)
            pe.matmul(ps[:, 2 + b, 0:S], sqd["L0_attn_Wv"][:], xg[:, b, :], start=True, stop=True) \
                .then_inc(sem("gv_in_psum"), 1)
        for b in range(B):
            pe.wait_ge(sem("gv_ready"), b + 1)
            pe.matmul(ps[0:S, 4 + b, 0:D], gvT[:, b, :], sqd["L0_attn_Wo"][:], start=True, stop=True) \
                .then_inc(sem("gvw_in_psum"), 1)
        pe.wait_ge(sem("gvw_ready"), B)
        for t in range(NT):
            m = pe.matmul(ps[:, t // 3, (t % 3) * (D + 1):(t % 3 + 1) * (D + 1)], gaussT[:, t * P:(t + 1) * P],
                          gvw[:, t // MT, :], start=True, stop=True)
        m.then_inc(sem("splat_in_psum"), 1)

        pe.wait_ge(sem("splat_taken"), 1)

        def expert_tiles(tag, between=None):
            n0 = FIRST_TILE[tag]

            def turned(turn, u):
                n = turn * XR + u
                pe.wait_ge(sem(f"tile_xs_in{u % XR}"), (turn + (u // XR + 1)) * 16)
                if not (isinstance(n, int) and n == 0):
                    pe.wait_ge(sem("tile_xsT_ready"), n)
                pe.transpose(ps[:, 0, 0:P], xs[:, u % XR, 0:D], ident[:]).then_inc(sem("tile_xsT_in_psum"), 1)

            def hidden(turn, u):
                pe.wait_ge(sem("tile_xsT_ready"), turn * XR + (u + 1))
                pe.wait_ge(sem("tile_w_ready"), turn * XR + (u + 1))
                for f in range(FT):
                    m = pe.matmul(ps[:, 1 + u % ER, f * P:(f + 1) * P], wcur[:, u % ER, f * P:(f + 1) * P],
                                  xsT[:, u % ER, :], start=True, stop=True)
                m.then_inc(sem("tile_h_in_psum"), 1)

            def results(turn, u):
                s = u % ER
                pe.wait_ge(sem("tile_h_ready"), turn * XR + (u + 1))
                if not (isinstance(turn, int) and turn * XR + u < ER):
                    pe.wait_ge(sem("tile_ys_ready"), turn * XR + (u - ER + 1))
                for f in range(FT):
                    m = pe.matmul(ps[:, 4 + s, 0:D], hid[:, s, f, :], wcur[:, s, HID + f * D:HID + (f + 1) * D],
                                  start=f == 0, stop=f == FT - 1 and tag == "m0")
                if tag == "m1":
                    e = pe.value_load(tile_expert[0:1, bass.ds(turn * XR + u, 1)], min_val=0, max_val=E - 1)
                    m = pe.matmul(ps[:, 4 + s, 0:D], ones[0:1, :], b2_row[:, bass.ds(e * D, D)],
                                  start=False, stop=True)
                m.then_inc(sem("tile_ys_in_psum"), 1)

            def step(turn, u, first=False, last=False):
                if not last:
                    turned(turn, u + 1)
                hidden(turn, u)
                if not first:
                    results(turn, u - 1)

            pe.wait_ge(sem(f"{tag}_experts_ready"), 1)
            turned(n0 // XR, 0)
            for n in range(n0, n0 + LOOP_FROM[tag]):
                step(n // XR, n % XR, first=n == n0)
                if between is not None:
                    between(n - n0)
            tile_loop(pe, step, tag)
            for n in range(n0 + MTILES - 2, n0 + MTILES):
                step(n // XR, n % XR, last=n == n0 + MTILES - 1)
            results((n0 + MTILES - 1) // XR, XR - 1)

        expert_tiles("m0")

        transpose_all(xn_tok, 4, "xn1_ready", "xn1T_in_psum")
        pe.wait_ge(sem("w_l1"), 8 * 16)
        for c in range(NCH):
            pe.wait_ge(sem("xn1T_ready"), c + 1)
            pe.matmul(ps[0:16, 4 + c, :], w_red[:], xnT[:, c * CH:(c + 1) * CH], start=True, stop=True) \
                .then_inc(sem("red_in_psum"), 1)
        for t in range(NT):
            m = pe.matmul(ps[:, t // 4, (t % 4) * D:(t % 4 + 1) * D], xnT[:, t * P:(t + 1) * P],
                          w1m["Wv"][:], start=True, stop=True)
            if t % 4 == 3:
                m.then_inc(sem("v1_in_psum"), 1)
        pe.wait_ge(sem("red_ready"), NCH)
        pe.wait_ge(sem("wgn_ready"), 1)
        pe.transpose(ps[0:16, 5, 0:E], wgn[:], ident[0:E, 0:E]).then_inc(sem("wgT_in_psum"), 1)
        pe.wait_ge(sem("wgT_ready"), 1)
        for t in range(NT):
            m = pe.matmul(ps[:, 4, t * E:(t + 1) * E], redT[:, t * P:(t + 1) * P], wgT[:], start=True, stop=True)
        m.then_inc(sem("gate1_in_psum"), 1)
        pe.wait_ge(sem("gate1_shifted"), 1)
        for w, name in enumerate(("Wq", "Wk", "Wkp", "Wv")):
            if w == 2:
                pe.wait_ge(sem("v1_tok_ready"), NCH)
                route_counts("m1", 3)
                pe.wait_ge(sem("masks_ready"), 1)
                pe.matmul(ps[:, 0, 0:P], tok_rows[:].rearrange("s q t -> s (q t)"),
                          mask_keys[0:TB].rearrange("p j c -> p (j c)"), start=True, stop=True) \
                    .then_inc(sem("mask_in_psum"), 1)
            for c in range(NCH):
                n = w * NCH + c
                if n >= 4:
                    if n - 4 < NCH:
                        pe.wait_ge(sem("q1_ready"), n - 3)
                    else:
                        pe.wait_ge(sem("qkv1_ready"), n - 3 - NCH)
                pe.matmul(ps[:, 4 + n % 4, :], w1m[name][:], xnT[:, c * CH:(c + 1) * CH],
                          start=True, stop=True).then_inc(sem("qkv1_in_psum"), 1)
        pe.wait_ge(sem("qkv1_ready"), 3 * NCH)

        pe.wait_ge(sem("mask_taken"), 1)
        TURNED, SUMS = 6, 7

        def scores(n, two, three, half, first):
            if half == 0:
                if not (isinstance(n, int) and n < 3):
                    pe.wait_ge(sem("win_exp"), n - 2)
                pe.wait_ge(sem("kdiag_ready"), n + 1)
                pe.wait_ge(sem("qk_ready"), n + 1)
            bank = 2 * three + half
            if first:
                m = mask_toks[:].rearrange("p s j -> p (s j)")
                pe.matmul(ps[:, bank, :], mask_keys[:].rearrange("p j c -> p (j c)"),
                          m.unsqueeze(1).broadcast_to([P, 2, TB * W]), start=True, stop=False,
                          skip_group_check=True)
            for g in (2 * half, 2 * half + 1):
                mm = pe.matmul(ps[:, bank, (g % 2) * TB * W:(g % 2 + 1) * TB * W],
                               kdiag[:, three, HG * g:HG * g + HG, :].rearrange("p j c -> p (j c)"),
                               qk[:, three].rearrange("p s j -> p (s j)"),
                               start=g % 2 == 0 and not first, stop=False, skip_group_check=True)
            if half:
                mm.then_inc(sem("win_scores"), 1)

        def turn_max(n, two):
            pe.wait_ge(sem("win_cmax"), n + 1)
            if not (isinstance(n, int) and n == 0):
                pe.wait_ge(sem("win_mparts"), n)
            pe.matmul(ps[:, TURNED, 0:P], ident_bf[:], mask_seen[:], start=True, stop=False, skip_group_check=True)
            for part in range(2):
                mm = pe.matmul(ps[64 * part:64 * part + 64, TURNED, 0:P], cmax[:, two], ident[:],
                               start=False, stop=True, skip_group_check=True)
            mm.then_inc(sem("win_max_in_psum"), 1)

        def shift(n, three):
            pe.wait_ge(sem("win_mparts"), n + 1)
            lhs = mparts[:].rearrange("p j c -> p (j c)")
            for g in range(NG):
                mm = pe.matmul(ps[:, 2 * three + g // 2, (g % 2) * TB * W:(g % 2 + 1) * TB * W], lhs,
                               spread[:, g].rearrange("p s j -> p (s j)"),
                               start=False, stop=g % 2 == 1, skip_group_check=True)
            mm.then_inc(sem("win_shifted"), 1)

        def value_products(n, two, three):
            pe.wait_ge(sem("win_exp"), n + 1)
            pe.wait_ge(sem("vdiag_ready"), n + 1)
            if not (isinstance(n, int) and n == 0):
                pe.wait_ge(sem("win_den_taken"), n)
            for part in range(2):
                for g in range(NG):
                    lhs = vdiag[:, three, g] if part == 0 else quad_rows[:]
                    mm = pe.matmul(ps[32 * g:32 * g + 32, SUMS, part * TB * W:(part + 1) * TB * W],
                                   lhs.rearrange("p j d -> p (j d)"),
                                   wprobs[:, two, g].rearrange("p s j -> p (s j)"), start=True, stop=True,
                                   skip_group_check=True)
            mm.then_inc(sem("win_rv"), 1)

        for n in range(PEEL):
            scores(n, n % 2, n, 0, True)
            if n:
                turn_max(n - 1, (n - 1) % 2)
            scores(n, n % 2, n, 1, True)
            if n:
                shift(n - 1, n - 1)
        with pe.Fori(0, (BLOCKS - PEEL) // BODY) as it:
            for u in range(BODY):
                n = it * BODY + (PEEL + u)
                scores(n, u % 2, (PEEL + u) % 3, 0, False)
                turn_max(it * BODY + (PEEL + u - 1), (u - 1) % 2)
                scores(n, u % 2, (PEEL + u) % 3, 1, False)
                value_products(it * BODY + (PEEL + u - 2), u % 2, (PEEL + u - 2) % 3)
                shift(it * BODY + (PEEL + u - 1), (PEEL + u - 1) % 3)
        turn_max(BLOCKS - 1, (BLOCKS - 1) % 2)
        shift(BLOCKS - 1, (BLOCKS - 1) % 3)
        value_products(BLOCKS - 2, 0, (BLOCKS - 2) % 3)
        value_products(BLOCKS - 1, 1, (BLOCKS - 1) % 3)

        def project(n):
            c = n - (LOOP_FROM["m1"] - NCH)
            if c == 0:
                pe.wait_ge(sem("zT_ready"), 1)
            if c > 0:
                pe.wait_ge(sem("wo_taken"), c)
            if c >= 0:
                for t in range(4 * c, 4 * c + 4):
                    m = pe.matmul(ps[:, 7, (t % 4) * D:(t % 4 + 1) * D], zT[:, t * P:(t + 1) * P], w1m["Wo"][:],
                                  start=True, stop=True)
                m.then_inc(sem("wo_in_psum"), 1)

        expert_tiles("m1", between=project)

    @block.vector
    def _(dve):
        st = Steps(dve, sem("dve_chain"))

        def bc(v, n):
            return v.unsqueeze(2).broadcast_to([P, NT, n])

        def row(v):
            return v.unsqueeze(1).broadcast_to([P, NT, D])

        def ln_stats(src, chunk=None):
            for t in range(NT):
                if chunk and t % 4 == 0:
                    chunk(t // 4)
                last = dve.bn_stats(stats[:, t, :], src[:, t, :])
            chain(last, st)
            mean0, m2_0, mean1, m2_1 = (stats[:, :, i] for i in (1, 2, 4, 5))
            dve.tensor_tensor(col[:, 0, :], mean0, mean1, ALU.add)
            dve.tensor_tensor(col[:, 1, :], mean0, mean1, ALU.subtract)
            chain(dve.tensor_tensor(col[:, 2, :], m2_0, m2_1, ALU.add), st)
            dve.tensor_scalar(col[:, 0, :], col[:, 0, :], -0.5, None, ALU.mult)
            chain(dve.tensor_tensor(col[:, 1, :], col[:, 1, :], col[:, 1, :], ALU.mult), st)
            dve.scalar_tensor_tensor(col[:, 3, :], col[:, 1, :], D / 4.0, col[:, 2, :], ALU.mult, ALU.add) \
                .then_inc(sem("ln_var"), 1)

        def ln_apply(dst, src, n, done):
            dve.wait_ge(sem("ln_std"), n)
            chain(dve.reciprocal(col[:, 3, :], col[:, 4, :]), st)
            dve.tensor_tensor(col[:, 1, :], col[:, 0, :], col[:, 3, :], ALU.mult).then_inc(sem("ln_scale"), 1)
            for t in range(NT // 2):
                last = dve.tensor_scalar(dst[:, t, :], src[:, t, :], col[:, 0, t:t + 1], col[:, 3, t:t + 1],
                                         ALU.add, ALU.mult)
                if t % 4 == 3:
                    last.then_inc(sem(done), 1)
            dve.wait_ge(sem(done), NCH // 2)
            dve.wait_ge(sem("ln_by_act"), n * (NCH // 2))

        def layernorm(dst, src, n, done, chunk=None):
            ln_stats(src, chunk)
            ln_apply(dst, src, n, done)

        dve.wait_ge(sem("x_in"), 16)
        layernorm(xn_tok, x_tok, 1, "xn_ready")

        layernorm(moe_tok, xn_tok, 2, "h_ready")
        dve.wait_ge(sem("consts_ready"), 1)
        dve.wait_ge(sem("number_in_psum"), 1)
        chain(dve.tensor_scalar(te_f[:], count[:], float(P), ps[:, 7, 0:1], ALU.mult, ALU.add), st)
        chain(dve.tensor_scalar(empty_rows[:, :, D:DI].rearrange("p k o -> p (k o)").bitcast(I32), te_f[:],
                                float(N), None, ALU.add), st)
        dve.tensor_scalar(tmp_rows[:, :, D:DI].rearrange("p t o -> p (t o)").bitcast(I32), tile_start[:],
                          ps[:, 7, 0:1], None, ALU.add).then_inc(sem("numbers_ready"), 1)
        for w in range(2):
            for c in range(NCH):
                n = w * NCH + c
                r1 = part_rest[:, n % 2, :]
                dve.wait_ge(sem("part_hi"), n + 1)
                dve.tensor_tensor(r1, ps[:, n % 4, :], parts[:, w, 0, c * CH:(c + 1) * CH], ALU.subtract) \
                    .then_inc(sem("part_r1"), 1)
                dve.wait_ge(sem("part_mid"), n + 1)
                dve.tensor_tensor(parts[:, w, 2, c * CH:(c + 1) * CH], r1, parts[:, w, 1, c * CH:(c + 1) * CH],
                                  ALU.subtract).then_inc(sem("parts_ready"), 1)

        dve.wait_ge(sem("splat_in"), 64)
        chain(dve.tensor_tensor(splat_sq[:], splat[:], splat[:], ALU.mult), st)
        chain(dve.tensor_reduce(scol[:, 4:5], splat_sq[:], X, ALU.add), st)
        chain(dve.tensor_scalar(splatT[:], splatT[:], -2.0, None, ALU.mult), st)
        dve.wait_ge(sem("splat_scale"), 1)
        chain(dve.tensor_tensor(scol[:, 1:2], scol[:, 0:1], scol[:, 0:1], ALU.mult), st)
        chain(dve.reciprocal(scol[:, 2:3], scol[:, 1:2]), st)
        dve.tensor_scalar(scol[:, 3:4], scol[:, 2:3], -0.5, None, ALU.mult).then_inc(sem("splat_scale2"), 1)
        dve.wait_ge(sem("splat_scale2"), 1)

        def max_unit(G, u):
            for i in (2 * u, 2 * u + 1):
                dve.wait_ge(sem("max_scores"), G * (UNITS * 2) + (i + 1))
                dve.tensor_reduce(mxh[:, u, i % 2:i % 2 + 1], ps[:, MX + i % MXN, :], X, ALU.max) \
                    .then_inc(sem("max_taken"), 1)

        def max_rows(G, before=None):
            dve.wait_ge(sem("max_taken"), (G + 1) * (UNITS * 2))
            chain(dve.tensor_reduce(nmx[:], mxh[:], X, ALU.max, negate=True), st)
            chain(dve.tensor_copy(mxs[:, 0, :], nmx[:]), st)
            chain(dve.tensor_tensor(mxr[:], nmx[:], mxs[:, 0, :], ALU.subtract), st)
            chain(dve.tensor_copy(mxs[:, 1, :], mxr[:]), st)
            dve.tensor_tensor(mxs[:, 2, :], mxr[:], mxs[:, 1, :], ALU.subtract).then_inc(sem("max_split"), 1)
            dve.wait_ge(sem("max_rows_in_psum"), G + 1)
            if before is not None:
                slot, turn = before
                dve.wait_ge(sem(f"maxrow_in{slot}"), (turn + 1) * 16)
            dve.tensor_copy(mxrow[:], ps[0:SPLITS * UNITS, MX + 2, 0:P // 2].bitcast(BF16)) \
                .then_inc(sem("max_rows_ready"), 1)

        def group_maxima(G, slot, turn, more):
            for u in range(2 * AHEAD, UNITS):
                max_unit(G + 1, u)
            max_rows(G + 1, (slot, turn))
            if more >= 2:
                for u in range(2 * AHEAD):
                    max_unit(G + 2, u)

        for u in range(UNITS):
            max_unit(0, u)
        max_rows(0)
        for u in range(2 * AHEAD):
            max_unit(1, u)
        with dve.Fori(0, GROUPS // RING) as it:
            st.enter(it, 4 * RING)
            for slot in range(RING):
                group_maxima(it * RING + slot, slot, it, 2)
        st.leave(GROUPS // RING)
        for G in range(GROUPS // RING * RING, GROUPS - 1):
            group_maxima(G, G % RING, G // RING, GROUPS - 1 - G)

        for t in range(NT):
            dve.wait_ge(sem("y_tok_in_psum"), t + 1)
            v = ps[:, t % 4, :].rearrange("p (h r) -> p h r", r=32)
            chain(dve.reciprocal(rden[:, t % 2], v[:, :, DK:DK + 1]), st)
            dve.tensor_tensor(tmp_tok[:, t, :].rearrange("p (h d) -> p h d", d=DK), v[:, :, 0:DK],
                              rden[:, t % 2].broadcast_to([P, H, DK]), ALU.mult).then_inc(sem("quotients"), 1)
        for c in range(NCH):
            dve.wait_ge(sem("proj_in_psum"), c + 1)
            last = dve.tensor_tensor(moe_tok[:, 4 * c:4 * c + 4, :],
                                     ps[:, c, :].rearrange("p (t d) -> p t d", d=D),
                                     xn_tok[:, 4 * c:4 * c + 4, :], ALU.add)
        last.then_inc(sem("msa_done"), 1)
        dve.wait_ge(sem("msa_done"), 1)

        layernorm(tmp_tok, moe_tok, 3, "h2_ready")

        def ebc(v):
            return v.unsqueeze(2).broadcast_to([P, NT, E])

        def first_max(logits, dst, done):
            chain(dve.tensor_reduce(col[:, 4, :], logits, X, ALU.max), st)
            chain(dve.tensor_tensor(route[:, 1], logits, ebc(col[:, 4, :]), ALU.is_equal), st)
            for e in range(E):
                last = dve.memset(route[:, 2, :, e:e + 1], float(E - e))
            chain(last, st)
            chain(dve.tensor_tensor(route[:, 1], route[:, 1], route[:, 2], ALU.mult), st)
            chain(dve.tensor_reduce(col[:, 5, :], route[:, 1], X, ALU.max), st)
            dve.tensor_tensor(dst, route[:, 1], ebc(col[:, 5, :]), ALU.is_equal).then_inc(sem(done), 1)
            dve.wait_ge(sem(done), 1)

        def route_slots(tag, bank):
            dve.wait_ge(sem(f"{tag}_counts_in_psum"), 1)
            rank = ps[:, bank, 0:NT * E].rearrange("p (t e) -> p t e", e=E)
            total = ps[:, bank, NT * E:(NT + 1) * E]
            chain(dve.tensor_tensor(filled[:], total.unsqueeze(2).broadcast_to([P, E, NT]),
                                    tile_start[:].unsqueeze(1).broadcast_to([P, E, NT]), ALU.is_gt), st)
            chain(dve.tensor_reduce(tiles_to[:, 0], filled[:], X, ALU.add), st)
            for i in range(3):
                by = 1 << i
                dve.tensor_copy(tiles_to[:, i + 1, 0:by], tiles_to[:, i, 0:by])
                chain(dve.tensor_tensor(tiles_to[:, i + 1, by:E], tiles_to[:, i, by:E], tiles_to[:, i, 0:E - by],
                                        ALU.add), st)
            chain(dve.tensor_tensor(first_slot[:], tiles_to[:, 3], tiles_to[:, 0], ALU.subtract), st)
            chain(dve.tensor_scalar(first_slot[:], first_slot[:], float(P), None, ALU.mult), st)
            chain(dve.tensor_tensor(route[:, 1], rank, first_slot[:].unsqueeze(1).broadcast_to([P, NT, E]),
                                    ALU.add), st)
            chain(dve.tensor_tensor(route[:, 1], route[:, 1], chosen[:], ALU.mult), st)
            chain(dve.tensor_reduce(slot_f[:], route[:, 1], X, ALU.add), st)
            dve.tensor_copy(tok_slot[tag][:], slot_f[:]).then_inc(sem(f"{tag}_slots_ready"), 1)
            n0 = FIRST_TILE[tag]
            chain(dve.tensor_tensor(ended[:], tiles_to[:, 3].unsqueeze(1).broadcast_to([P, MTILES, E]),
                                    count[:].unsqueeze(2).broadcast_to([P, MTILES, E]), ALU.is_le), st)
            chain(dve.tensor_reduce(te_f[:], ended[:], X, ALU.add), st)
            dve.tensor_scalar(tile_expert[:, n0:n0 + MTILES], te_f[:], float(E - 1), None, ALU.min) \
                .then_inc(sem(f"{tag}_experts_ready"), 1)

        dve.wait_ge(sem("rows_in"), 3 * 16)
        dve.wait_ge(sem("gate_in_psum"), 1)
        chain(dve.tensor_tensor(route[:, 0], ps[:, 6, 0:NT * E].rearrange("p (t e) -> p t e", e=E),
                                gate_b[:].unsqueeze(1).broadcast_to([P, NT, E]), ALU.add), st)
        first_max(route[:, 0], chosen[:], "m0_chosen")
        route_slots("m0", 7)
        dve.wait_ge(sem("gaussT_ready"), NCH)
        for b in range(B):
            dve.tensor_reduce(gvw[:, b, D:D + 1], gaussT[:, b * T:(b + 1) * T], X, ALU.add)
        for b in range(B):
            dve.wait_ge(sem("xg_in_psum"), b + 1)
            dve.tensor_copy(xg[:, b, :], ps[:, b, 0:S]).then_inc(sem("xg_ready"), 1)
        for b in range(B):
            dve.wait_ge(sem("gv_in_psum"), b + 1)
            dve.tensor_copy(gvT[:, b, :], ps[:, 2 + b, 0:S]).then_inc(sem("gv_ready"), 1)
        for b in range(B):
            dve.wait_ge(sem("gvw_in_psum"), b + 1)
            dve.tensor_copy(gvw[:, b, 0:D], ps[0:S, 4 + b, 0:D]).then_inc(sem("gvw_ready"), 1)
        dve.wait_ge(sem("splat_in_psum"), 1)
        banks = ps[:, 0:NT // 3, 0:3 * (D + 1)].rearrange("p c (t d) -> p c t d", d=D + 1)
        NL = NT // 3 * 3
        dve.tensor_scalar(col[:, 4, 0:NL].rearrange("p (c t o) -> p c t o", t=3, o=1), banks[:, :, :, D:D + 1],
                          SPLAT_EPS, None, ALU.add)
        chain(dve.tensor_scalar(col[:, 4, NL:NT], ps[:, NT // 3, D:D + 1], SPLAT_EPS, None, ALU.add), st)
        chain(dve.reciprocal(col[:, 5, :], col[:, 4, :]), st)
        dve.tensor_tensor(splat_out[:, 0:NL, :].rearrange("p (c t) d -> p c t d", t=3), banks[:, :, :, 0:D],
                          col[:, 5, 0:NL].rearrange("p (c t o) -> p c t o", t=3, o=1)
                          .broadcast_to([P, NL // 3, 3, D]), ALU.mult)
        dve.tensor_scalar(splat_out[:, NL, :], ps[:, NT // 3, 0:D], col[:, 5, NL:NT], None, ALU.mult) \
            .then_inc(sem("splat_taken"), 1)
        dve.wait_ge(sem("splat_taken"), 1)

        def tile_copies(copies, n0, start, tag):
            def step(turn, u, first=False, last=False):
                if not last:
                    copies.transposed(turn, u + 1)
                    copies.weights(turn, u + 1)
                if not first:
                    copies.results(turn, u - 1)

            if start == 0:
                copies.transposed(n0 // XR, 0)
                copies.weights(n0 // XR, 0)
            for n in range(n0 + start, n0 + LOOP_FROM[tag]):
                step(n // XR, n % XR, first=n == n0)
            tile_loop(dve, step, tag)
            for n in range(n0 + MTILES - 2, n0 + MTILES):
                step(n // XR, n % XR, last=n == n0 + MTILES - 1)
            copies.results((n0 + MTILES - 1) // XR, XR - 1)

        def times_one(o, i):
            return dve.tensor_scalar(o, i, 1.0, None, ALU.mult)

        def ln2_affine(o, i):
            return dve.tensor_scalar(o, i, lncol["L0_ffn_ln2_w"][:], lncol["L0_ffn_ln2_b"][:], ALU.mult, ALU.add)

        tile_copies(TileCopies(dve, "m0", times_one, ln2_affine), FIRST_TILE["m0"], 0, "m0")

        chain(dve.tensor_tensor(x_tok[:], x_tok[:], moe_tok[:], ALU.add), st)
        chain(dve.tensor_tensor(x_tok[:], x_tok[:], splat_out[:], ALU.add), st)

        def gathered0(c):
            v = slice(4 * c, 4 * c + 4)
            dve.wait_ge(sem(f"results_in{c}"), 16)
            chain(dve.tensor_tensor(x_tok[:, v, :], x_tok[:, v, :], tmp_tok[:, v, :], ALU.add), st)

        dve.wait_ge(sem("w_l1"), 8 * 16)
        chain(dve.tensor_tensor(wgn[:], wg[:], wg[:], ALU.mult), st)
        dve.tensor_reduce(wgs[:, 0:1], wgn[:], X, ALU.add).then_inc(sem("wg_norm2"), 1)
        layernorm(xn_tok, x_tok, 4, "xn1_ready", chunk=gathered0)
        dve.wait_ge(sem("wg_norm"), 1)
        chain(dve.tensor_scalar(wgs[:, 2:3], wgs[:, 1:2], 1e-4, None, ALU.max), st)
        chain(dve.reciprocal(wgs[:, 3:4], wgs[:, 2:3]), st)
        dve.tensor_scalar(wgn[:], wg[:], wgs[:, 3:4], None, ALU.mult).then_inc(sem("wgn_ready"), 1)
        dve.wait_ge(sem("wgT_in_psum"), 1)
        dve.tensor_copy(wgT[:], ps[0:16, 5, 0:E]).then_inc(sem("wgT_ready"), 1)
        dve.wait_ge(sem("gate1_in_psum"), 1)
        lg = ps[:, 4, 0:NT * E].rearrange("p (t e) -> p t e", e=E)
        chain(dve.tensor_reduce(col[:, 4, :], lg, X, ALU.max), st)
        dve.tensor_tensor(route[:, 0], lg, ebc(col[:, 4, :]), ALU.subtract).then_inc(sem("gate1_shifted"), 1)
        dve.wait_ge(sem("gate1_exp"), 1)
        chain(dve.tensor_reduce(col[:, 6, :], route[:, 3], X, ALU.add), st)
        chain(dve.reciprocal(col[:, 7, :], col[:, 6, :]), st)
        chain(dve.tensor_tensor(route[:, 3], route[:, 3], ebc(col[:, 7, :]), ALU.mult), st)
        first_max(route[:, 3], chosen[:], "m1_chosen")
        chain(dve.tensor_reduce(score[:], route[:, 3], X, ALU.max), st)
        route_slots("m1", 3)
        dve.wait_ge(sem("mask_in_psum"), 1)
        dve.tensor_copy(mask_seen[:], ps[:, 0, 0:P])
        dve.tensor_copy(mask_once[0:64], ps[0:64, 0, 0:P]).then_inc(sem("mask_taken"), 1)

        def key_max(n, two, three):
            dve.wait_ge(sem("win_scores"), n + 1)
            if not (isinstance(n, int) and n < 2):
                dve.wait_ge(sem("win_max_in_psum"), n - 1)
            dve.tensor_reduce(cmax[:, two].rearrange("p (g s) -> p g s", s=TB),
                              ps[:, 2 * three:2 * three + 2, :].rearrange("p a (g s j) -> p (a g) s j", s=TB, j=W),
                              X, ALU.max).then_inc(sem("win_cmax"), 1)

        def max_parts(n):
            dve.wait_ge(sem("win_max_in_psum"), n + 1)
            if not (isinstance(n, int) and n == 0):
                dve.wait_ge(sem("win_shifted"), n)
            chain(dve.tensor_reduce(nM[:], ps[:, 6, 0:P].rearrange("p (j c) -> p j c", c=WIN), X, ALU.max,
                                    negate=True), st)
            wide = nM[:].unsqueeze(2).broadcast_to([P, HG, WIN])
            chain(dve.tensor_tensor(mparts[:], mask_once[:].rearrange("p (j c) -> p j c", c=WIN), wide, ALU.add), st)
            dve.tensor_tensor(mparts[64:P], wide[64:P], mparts[64:P], ALU.subtract) \
                .then_inc(sem("win_mparts"), 1)

        dve.wait_ge(sem("qkv1_ready"), 3 * NCH)

        def first_key_sum(n, b, blk, two):
            dve.wait_ge(sem("win_rv"), n + 1)
            vw = vT[:, b, bass.ds(blk * TB + 1, TB + W - 1)]
            vw = bass.AP(vw.tensor, vw.offset, [list(vw.ap[0]), [1, TB], [1, W]])
            r = ps[:, 7, 0:TB * W].rearrange("p (s j) -> p s j", j=W)
            den = ps[:, 7, TB * W:2 * TB * W].rearrange("p (s j) -> p s j", j=W)
            chain(dve.tensor_tensor(rv[:, two], r, vw, ALU.mult), st)
            dve.tensor_reduce(denT[:, bass.ds(blk * TB + b * T, TB)], den, X, ALU.add) \
                .then_inc(sem("win_den_taken"), 1)
            dve.tensor_reduce(zT[:, bass.ds(blk * TB + b * T, TB)], rv[:, two], X, ALU.add) \
                .then_inc(sem("win_z"), 1)

        for n in range(PEEL):
            if n:
                max_parts(n - 1)
            key_max(n, n % 2, n % 3)
        with dve.Fori(0, (BLOCKS - PEEL) // BODY) as it:
            st.enter(it, 3 * BODY)
            for u in range(BODY):
                max_parts(it * BODY + (PEEL + u - 1))
                key_max(it * BODY + (PEEL + u), u % 2, (PEEL + u) % 3)
                first_key_sum(it * BODY + (PEEL + u - 2), u % B, it * (BODY // B) + (PEEL + u - 2) // B, u % 2)
        st.leave((BLOCKS - PEEL) // BODY)
        max_parts(BLOCKS - 1)
        first_key_sum(BLOCKS - 2, 0, NB - 1, 0)
        first_key_sum(BLOCKS - 1, 1, NB - 1, 1)
        dve.wait_ge(sem("win_z"), BLOCKS)
        dve.wait_ge(sem("win_den_taken"), BLOCKS)
        chain(dve.reciprocal(denT[:], denT[:]), st)
        dve.tensor_tensor(zT[:], zT[:], denT[:], ALU.mult).then_inc(sem("zT_ready"), 1)
        chain(dve.tensor_tensor(x_tok[:], x_tok[:], row(rows["L1_attn_beta"][:]), ALU.add), st)
        dve.wait_ge(sem("m1_scattered"), 16 * NT)

        def projected(c):
            v = slice(4 * c, 4 * c + 4)
            dve.wait_ge(sem("wo_in_psum"), c + 1)
            dve.tensor_tensor(tmp_tok[:, v, :], ps[:, 7, :].rearrange("p (t d) -> p t d", d=D), xn_tok[:, v, :],
                              ALU.add).then_inc(sem("wo_taken"), 1)
            dve.wait_ge(sem("wo_taken"), c + 1)

        ln_stats(tmp_tok, chunk=projected)
        n = FIRST_TILE["m1"] + LOOP_FROM["m1"]
        dve.wait_ge(sem("tile_xsT_ready"), n + 1)
        dve.wait_ge(sem("tile_w_ready"), n + 1)
        dve.wait_ge(sem("tile_ys_ready"), n - 1)
        tile_copies(TileCopies(dve, "m1", times_one), FIRST_TILE["m1"], LOOP_FROM["m1"], "m1")
        ln_apply(xn_tok, tmp_tok, 5, "attn1_done")
        chain(dve.tensor_tensor(xn_tok[:], xn_tok[:], row(rows["L1_attn_gamma"][:]), ALU.mult), st)
        chain(dve.tensor_tensor(x_tok[:], x_tok[:], xn_tok[:], ALU.add), st)
        for c in range(NCH):
            dve.wait_ge(sem(f"results_in{c}"), 2 * 16)
            for t in range(4 * c, 4 * c + 4):
                last = dve.scalar_tensor_tensor(x_tok[:, t, :], Ytok1[:, t, :], score[:, t:t + 1], x_tok[:, t, :],
                                                ALU.mult, ALU.add)
            last.then_inc(sem("final"), 1)


_INS = ["L0_attn_token_embeddings", "L0_attn_splat_positions", "L0_attn_splat_log_scales",
        "L0_attn_splat_amplitudes", "L0_attn_Wv", "L0_attn_Wo", "L0_ffn_ln1_w", "L0_ffn_ln1_b",
        "L0_ffn_w_qkv", "L0_ffn_w_proj", "L0_ffn_ln2_w", "L0_ffn_ln2_b", "L0_ffn_gate_w", "L0_ffn_gate_b",
        "L0_ffn_w1", "L0_ffn_w2", "L1_attn_gamma", "L1_attn_beta", "L1_ffn_w_red", "L1_ffn_wg",
        "L1_ffn_w1", "L1_ffn_w2", "L1_ffn_b2"]


def laid_out(inputs):
    import numpy as np
    got = {name: np.ascontiguousarray(inputs[name]) for name in _INS}
    got["splat_positions_T"] = np.ascontiguousarray(np.asarray(inputs["L0_attn_splat_positions"]).T)
    for name in ("Wq", "Wk", "Wv", "Wkp", "Wo"):
        got[f"L1_{name}_T"] = np.ascontiguousarray(np.asarray(inputs[f"L1_attn_{name}"]).T)
    b1 = np.asarray(inputs["L1_ffn_b1"]).reshape(E, FT, P)
    got["L1_b1_cols"] = np.ascontiguousarray(b1.transpose(2, 0, 1).reshape(P, E * FT))
    return got


def kernel(**inputs):
    import concourse.bacc as bacc
    from concourse.bass_utils import run_bass_kernel_spmd

    nc = bacc.Bacc("TRN2", target_bir_lowering=False, num_devices=1)
    arrays, aps = {}, {}
    for name, v in laid_out(inputs).items():
        arrays[f"in_{name}"] = v
        aps[name] = nc.dram_tensor(f"in_{name}", v.shape, mybir.dt.from_np(v.dtype), kind="ExternalInput").ap()
    out = nc.dram_tensor("out_x", (B, T, D), F32, kind="ExternalOutput").ap()
    two_layers(nc, aps, out)
    r = run_bass_kernel_spmd(nc, [arrays], core_ids=[0])
    return r.results[0]["out_x"]
```
